# Optimizing a Trainium2 kernel written in Bass

```python
import numpy as np
import jax
import jax.numpy as jnp

def _softmax(x, axis=-1):
    return jax.nn.softmax(x, axis=axis)

def _gelu(x):
    return jax.nn.gelu(x, approximate=True)

def _silu(x):
    return jax.nn.silu(x)

def _sigmoid(x):
    return jax.nn.sigmoid(x)

def _layernorm(x, axis=-1, eps=1e-05):
    m = jnp.mean(x, axis=axis, keepdims=True)
    v = jnp.var(x, axis=axis, keepdims=True)
    return (x - m) / jnp.sqrt(v + eps)

def _scatter_add(tgt, idx, src, axis=0):
    return tgt.at[idx].add(src)

def _segment_sum(src, seg, n):
    return jax.ops.segment_sum(src, seg, n)
kernel_name = 'mk_macaron_d2_jaxref_r8_b06567'

def setup_inputs(seed: int=0):
    np.random.seed(seed)
    _w = jnp.asarray

    def _L0_attn_setup():
        import jax, jax.numpy as jnp
        import numpy as np
        MAX_W, MIN_W = (120, 24)
        key = jax.random.key(seed)
        ks = jax.random.split(key, 11)
        B, S, D, H = (2, 256, 128, 16)
        hd = D // H
        s = 1.0 / float(np.sqrt(D))
        return {'x': jax.random.normal(ks[0], (B, S, D), jnp.float32), 'alpha': jnp.float32(0.1), 'Wq': jax.random.normal(ks[1], (D, D), jnp.float32) * s, 'bq': jnp.zeros((D,), jnp.float32), 'Wk': jax.random.normal(ks[2], (D, D), jnp.float32) * s, 'bk': jnp.zeros((D,), jnp.float32), 'Wv': jax.random.normal(ks[3], (D, D), jnp.float32) * s, 'bv': jnp.zeros((D,), jnp.float32), 'W_o': jax.random.normal(ks[4], (H, hd, hd), jnp.float32), 'Wfc': jax.random.normal(ks[5], (D, D), jnp.float32) * s, 'bfc': jnp.zeros((D,), jnp.float32)}
    _L0_attn_in = _L0_attn_setup()

    def _L0_ffn_setup():
        import jax, jax.numpy as jnp
        import numpy as np
        B, S, DIM = (2, 256, 128)
        HID = 256
        E, NSH, TOPK = (8, 2, 2)

        def _ffn(x, w1, w2, w3):
            return jax.nn.silu(x @ w1.T) * (x @ w3.T) @ w2.T
        key = jax.random.key(seed)
        ks = jax.random.split(key, 8)
        sc = 0.02
        return {'x': jax.random.normal(ks[0], (B, S, DIM), jnp.float32), 'router_w': jax.random.normal(ks[1], (E, DIM), jnp.float32) * sc, 'expert_bias': jnp.zeros((E,), jnp.float32), 'w1': jax.random.normal(ks[2], (E, HID, DIM), jnp.float32) * sc, 'w3': jax.random.normal(ks[3], (E, HID, DIM), jnp.float32) * sc, 'w2': jax.random.normal(ks[4], (E, DIM, HID), jnp.float32) * sc, 'sw1': jax.random.normal(ks[5], (NSH, HID, DIM), jnp.float32) * sc, 'sw3': jax.random.normal(ks[6], (NSH, HID, DIM), jnp.float32) * sc, 'sw2': jax.random.normal(ks[7], (NSH, DIM, HID), jnp.float32) * sc}
    _L0_ffn_in = _L0_ffn_setup()

    def _L1_attn_setup():
        import jax, jax.numpy as jnp
        import numpy as np
        B, N, DM, H = (1, 256, 128, 16)
        CURV = 1.0
        key = jax.random.key(seed)
        ks = jax.random.split(key, 5)
        s = 1.0 / np.sqrt(DM)
        x = jax.random.normal(ks[0], (B, N, DM), dtype=jnp.float32)
        Wq = jax.random.uniform(ks[1], (DM, DM), jnp.float32, -s, s)
        Wk = jax.random.uniform(ks[2], (DM, DM), jnp.float32, -s, s)
        Wv = jax.random.uniform(ks[3], (DM, DM), jnp.float32, -s, s)
        Wo = jax.random.uniform(ks[4], (DM, DM), jnp.float32, -s, s)
        return {'x': x, 'Wq': Wq, 'Wk': Wk, 'Wv': Wv, 'Wo': Wo}
    _L1_attn_in = _L1_attn_setup()

    def _L1_ffn_setup():
        import jax, jax.numpy as jnp
        import numpy as np
        TOP_K = 2
        CAP_FACTOR = 1.25
        MIN_CAPACITY = 4
        key = jax.random.key(seed)
        k1, k2, k3, k4 = jax.random.split(key, 4)
        B, T, C, E = (8, 256, 128, 8)
        x = jax.random.normal(k1, (B, T, C), dtype=jnp.float32)
        w_g = jax.random.normal(k2, (E, C), dtype=jnp.float32) * 0.02
        c_fc = jax.random.normal(k3, (E, C, 4 * C), dtype=jnp.float32) * 0.02
        c_proj = jax.random.normal(k4, (E, 4 * C, C), dtype=jnp.float32) * 0.02
        return {'x': x, 'w_g': w_g, 'c_fc': c_fc, 'c_proj': c_proj}
    _L1_ffn_in = _L1_ffn_setup()
    _d = {'L0_attn_x': _L0_attn_in['x'], 'L0_attn_alpha': _L0_attn_in['alpha'], 'L0_attn_Wq': _L0_attn_in['Wq'], 'L0_attn_bq': _L0_attn_in['bq'], 'L0_attn_Wk': _L0_attn_in['Wk'], 'L0_attn_bk': _L0_attn_in['bk'], 'L0_attn_Wv': _L0_attn_in['Wv'], 'L0_attn_bv': _L0_attn_in['bv'], 'L0_attn_W_o': _L0_attn_in['W_o'], 'L0_attn_Wfc': _L0_attn_in['Wfc'], 'L0_attn_bfc': _L0_attn_in['bfc'], 'L0_ffn_router_w': _L0_ffn_in['router_w'], 'L0_ffn_expert_bias': _L0_ffn_in['expert_bias'], 'L0_ffn_w1': _L0_ffn_in['w1'], 'L0_ffn_w3': _L0_ffn_in['w3'], 'L0_ffn_w2': _L0_ffn_in['w2'], 'L0_ffn_sw1': _L0_ffn_in['sw1'], 'L0_ffn_sw3': _L0_ffn_in['sw3'], 'L0_ffn_sw2': _L0_ffn_in['sw2'], 'L1_attn_Wq': _L1_attn_in['Wq'], 'L1_attn_Wk': _L1_attn_in['Wk'], 'L1_attn_Wv': _L1_attn_in['Wv'], 'L1_attn_Wo': _L1_attn_in['Wo'], 'L1_ffn_w_g': _L1_ffn_in['w_g'], 'L1_ffn_c_fc': _L1_ffn_in['c_fc'], 'L1_ffn_c_proj': _L1_ffn_in['c_proj']}
    _x0 = _d['L0_attn_x']
    _d['L0_attn_x'] = jax.random.normal(jax.random.fold_in(jax.random.key(seed), 1), (8, 512, 128), dtype=_x0.dtype)
    del _x0
    return _d

def reference(L0_attn_x, L0_attn_alpha, L0_attn_Wq, L0_attn_bq, L0_attn_Wk, L0_attn_bk, L0_attn_Wv, L0_attn_bv, L0_attn_W_o, L0_attn_Wfc, L0_attn_bfc, L0_ffn_router_w, L0_ffn_expert_bias, L0_ffn_w1, L0_ffn_w3, L0_ffn_w2, L0_ffn_sw1, L0_ffn_sw3, L0_ffn_sw2, L1_attn_Wq, L1_attn_Wk, L1_attn_Wv, L1_attn_Wo, L1_ffn_w_g, L1_ffn_c_fc, L1_ffn_c_proj):

    def _L0_attn_ref(x, alpha, Wq, bq, Wk, bk, Wv, bv, W_o, Wfc, bfc):
        import jax, jax.numpy as jnp
        import numpy as np
        MAX_W, MIN_W = (120, 24)
        B, S, D = x.shape
        H, hd, _ = W_o.shape
        fluct = jnp.abs(x[:, -1] - x[:, -2])
        a = jax.nn.sigmoid(alpha)
        ewma_prev = fluct[0, 0]
        signal = a * fluct.mean() + (1.0 - a) * ewma_prev
        scale = jax.nn.sigmoid(signal)
        w = jnp.floor(MIN_W + (MAX_W - MIN_W) * scale).astype(jnp.int32)
        half = w // 2
        q = (x @ Wq + bq).reshape(B, S, H, hd).transpose(0, 2, 1, 3)
        k = (x @ Wk + bk).reshape(B, S, H, hd).transpose(0, 2, 1, 3)
        v = (x @ Wv + bv).reshape(B, S, H, hd).transpose(0, 2, 1, 3)
        inv_sqrt = 1.0 / float(np.sqrt(hd))
        scores = jnp.einsum('bhqd,bhkd->bhqk', q, k) * inv_sqrt
        idx = jnp.arange(S)
        band = jnp.abs(idx[:, None] - idx[None, :]) <= half
        scores = jnp.where(band[None, None], scores, -1e+30)
        attn = jax.nn.softmax(scores, axis=-1)
        out = jnp.einsum('bhqk,bhkd->bhqd', attn, v)
        out = jnp.einsum('bhqd,hdk->bhqk', out, W_o)
        out = out.transpose(0, 2, 1, 3).reshape(B, S, D)
        return out @ Wfc + bfc

    def _L0_ffn_ref(x, router_w, expert_bias, w1, w3, w2, sw1, sw3, sw2):
        import jax, jax.numpy as jnp
        import numpy as np
        B, S, DIM = (2, 256, 128)
        HID = 256
        E, NSH, TOPK = (8, 2, 2)

        def _ffn(x, w1, w2, w3):
            return jax.nn.silu(x @ w1.T) * (x @ w3.T) @ w2.T
        bs, sl, d = x.shape
        xf = x.reshape(-1, d)
        shared = jnp.zeros_like(xf)
        for i in range(sw1.shape[0]):
            shared = shared + _ffn(xf, sw1[i], sw2[i], sw3[i])
        logits = xf @ router_w.T + expert_bias
        rw, sel = jax.lax.top_k(logits, TOPK)
        rw = jax.nn.softmax(rw.astype(jnp.float32), axis=-1).astype(x.dtype)
        onehot = jax.nn.one_hot(sel, E, dtype=x.dtype)
        combine = jnp.einsum('tk,tke->te', rw, onehot)

        def body(acc, ew):
            e1, e3, e2, cw = ew
            acc = acc + cw[:, None] * _ffn(xf, e1, e2, e3)
            return (acc, None)
        out, _ = jax.lax.scan(body, jnp.zeros_like(xf), (w1, w3, w2, combine.T))
        out = out + shared
        return out.reshape(bs, sl, -1)

    def _L1_attn_ref(x, Wq, Wk, Wv, Wo):
        import jax, jax.numpy as jnp
        import numpy as np
        B, N, DM, H = (1, 256, 128, 16)
        CURV = 1.0
        b, n, d = x.shape
        hd = d // H

        def split_heads(t):
            return t.reshape(b, n, H, hd).transpose(0, 2, 1, 3)
        q = split_heads(x @ Wq.T)
        k = split_heads(x @ Wk.T)
        v = split_heads(x @ Wv.T)
        q_norm_sq = jnp.sum(q * q, axis=-1, keepdims=True)
        k_norm_sq = jnp.sum(k * k, axis=-1)[:, :, None, :]
        qk = jnp.einsum('bhnd,bhmd->bhnm', q, k)
        diff_sq = jnp.maximum(q_norm_sq + k_norm_sq - 2.0 * qk, 0.0)
        denom = jnp.maximum((1.0 - CURV * q_norm_sq) * (1.0 - CURV * k_norm_sq), 1e-06)
        cosh_arg = jnp.maximum(1.0 + 2.0 * CURV * diff_sq / denom, 1.0)
        distance = jnp.where(cosh_arg > 1.0, jnp.arccosh(jnp.maximum(cosh_arg, 1.0 + 1e-12)), 0.0)
        attn = jax.nn.softmax(-distance, axis=-1)
        out = jnp.einsum('bhnm,bhmd->bhnd', attn, v)
        out = out.transpose(0, 2, 1, 3).reshape(b, n, d)
        return out @ Wo.T

    def _L1_ffn_ref(x, w_g, c_fc, c_proj):
        import jax, jax.numpy as jnp
        import numpy as np
        TOP_K = 2
        CAP_FACTOR = 1.25
        MIN_CAPACITY = 4
        B, T, C = x.shape
        E = w_g.shape[0]
        N = B * T
        capacity = max(MIN_CAPACITY, int(CAP_FACTOR * N * TOP_K / E))
        xf = x.reshape(N, C)
        logits = xf @ w_g.T
        top_logits, top_idx = jax.lax.top_k(logits, TOP_K)
        router_probs = jax.nn.softmax(top_logits, axis=-1)
        oh = jax.nn.one_hot(top_idx, E, dtype=jnp.int32)
        oh_t = oh.transpose(1, 0, 2).reshape(TOP_K * N, E)
        pos = jnp.cumsum(oh_t, axis=0).reshape(TOP_K, N, E).transpose(1, 0, 2)
        rank = jnp.sum((pos - 1) * oh, axis=-1)
        valid = rank < capacity
        probs_masked = router_probs * valid.astype(router_probs.dtype)
        rank_c = jnp.clip(rank, 0, capacity - 1)
        contrib = xf[:, None, :] * valid[..., None].astype(xf.dtype)
        buf = jnp.zeros((E, capacity, C), dtype=xf.dtype).at[top_idx, rank_c].add(contrib)
        h = jnp.einsum('ecd,edf->ecf', buf, c_fc)
        h = jnp.square(jax.nn.relu(h))
        expert_out = jnp.einsum('ecf,efd->ecd', h, c_proj)
        gathered = expert_out[top_idx, rank_c]
        out = jnp.sum(gathered * probs_masked[..., None], axis=1)
        return out.reshape(B, T, C)
    x = L0_attn_x
    x = x + 0.5 * _L0_ffn_ref(_layernorm(x, axis=-1), L0_ffn_router_w, L0_ffn_expert_bias, L0_ffn_w1, L0_ffn_w3, L0_ffn_w2, L0_ffn_sw1, L0_ffn_sw3, L0_ffn_sw2)
    x = x + _L0_attn_ref(_layernorm(x, axis=-1), L0_attn_alpha, L0_attn_Wq, L0_attn_bq, L0_attn_Wk, L0_attn_bk, L0_attn_Wv, L0_attn_bv, L0_attn_W_o, L0_attn_Wfc, L0_attn_bfc)
    x = x + 0.5 * _L0_ffn_ref(_layernorm(x, axis=-1), L0_ffn_router_w, L0_ffn_expert_bias, L0_ffn_w1, L0_ffn_w3, L0_ffn_w2, L0_ffn_sw1, L0_ffn_sw3, L0_ffn_sw2)
    x = x + 0.5 * _L1_ffn_ref(_layernorm(x, axis=-1), L1_ffn_w_g, L1_ffn_c_fc, L1_ffn_c_proj)
    x = x + _L1_attn_ref(_layernorm(x, axis=-1), L1_attn_Wq, L1_attn_Wk, L1_attn_Wv, L1_attn_Wo)
    x = x + 0.5 * _L1_ffn_ref(_layernorm(x, axis=-1), L1_ffn_w_g, L1_ffn_c_fc, L1_ffn_c_proj)
    return x

_drawn_inputs = setup_inputs


def setup_inputs(seed=0):
    import zlib

    import numpy as np

    out = dict(_drawn_inputs(seed))
    spreads = {'L0_attn_bq': (0.0, 0.1),
     'L0_attn_bk': (0.0, 2.0),
     'L0_attn_bv': (0.0, 0.1),
     'L0_attn_bfc': (0.0, 0.1),
     'L0_ffn_expert_bias': (0.0, 0.8)}
    factors = {'L0_ffn_router_w': 8.0,
     'L0_ffn_w1': 8.0,
     'L0_ffn_w3': 8.0,
     'L0_ffn_w2': 8.0,
     'L0_ffn_sw1': 5.261,
     'L0_ffn_sw3': 5.2,
     'L0_ffn_sw2': 5.241,
     'L1_attn_Wq': 21.608,
     'L1_ffn_w_g': 3.74,
     'L1_ffn_c_fc': 3.655,
     'L1_ffn_c_proj': 3.339,
     'L1_attn_Wk': 8.0,
     'L1_attn_Wv': 3.681,
     'L1_attn_Wo': 4.231}
    for name, (base, spread) in spreads.items():
        noise = np.random.default_rng([zlib.crc32(name.encode()), seed]).standard_normal(out[name].shape)
        drawn = base * np.exp(spread * noise) if base else spread * noise
        out[name] = jnp.asarray(drawn.astype(out[name].dtype))
    for name, factor in factors.items():
        out[name] = (out[name] * factor).astype(out[name].dtype)
    return out
```

```python
from contextlib import ExitStack

import concourse.bass as bass
from concourse import mybir

ALU = mybir.AluOpType
ACT = mybir.ActivationFunctionType
AX = mybir.AxisListType
F32 = mybir.dt.float32
F32R = mybir.dt.float32r
BF16 = mybir.dt.bfloat16
I32 = mybir.dt.int32

P = 128
B, S, D = 8, 512, 128
TOK = B * S
TPC = S // P
TILES = TOK // P
H, HD = 16, 8
E = 8
NSH = 2
HID0, HID1 = 256, 512
HB0, HB1 = HID0 // P, HID1 // P
U0, U1 = NSH + E, E
CAP = int(1.25 * TOK * 2 / E)
EPS = 1e-5
NEG = -1e30
WIN = 2 * P
HALO = 64
INV_SQRT = 1.0 / float(HD) ** 0.5
CLAMP = 2e6
FAR = float(2 ** 21)


def macaron(nc, x, alpha, w_qkv0, bias_rows0, wo0, wo0_t, wfc0, router0, expert_bias, up0, down0,
            w_qkv1, wo1, router1, up1, down1, out, stop_after=99):
    ctx = ExitStack()
    with ctx:
        def sb(name, shape, dt=F32, stack=ctx):
            return stack.enter_context(nc.sbuf_tensor(name, shape, dt))

        def sem(name):
            return ctx.enter_context(nc.semaphore(name))

        ps = ctx.enter_context(nc.psum_tensor("ps", [P, 8, 512], F32))

        X = sb("X", [P, TILES, D])
        XT = sb("XT", [P, TOK])
        up1_hi = sb("up1_hi", [P, U1, HID1], F32R)
        up1_lo = sb("up1_lo", [P, U1, HID1], F32R)
        dn1 = sb("dn1", [P, U1, HB1, D])
        ident = sb("ident", [P, P])
        ident_b = sb("ident_b", [P, P], BF16)
        before = sb("before", [P, P], BF16)
        ones_b = sb("ones_b", [P, P], BF16)
        ones_f = sb("ones_f", [P, P])
        half_neg = sb("half_neg", [P, TPC])
        rw = [sb("rw0", [P, E]), sb("rw1", [P, E])]
        ebias = sb("ebias", [P, E])
        logits = sb("logits", [P, TILES, E])
        cw = sb("cw", [P, TILES, E])
        cw_c = sb("cw_c", [P, TPC, E])
        bn = sb("bn", [P, TPC, 6])
        mv = sb("mv", [P, TPC, 2])
        var_eps = sb("var_eps", [P, TPC])
        rstd = sb("rstd", [P, TPC])
        xn = sb("xn", [P, TPC, D])
        xT_c = sb("xT_c", [P, S])
        alpha_s = sb("alpha_s", [P, 1])
        col = sb("col", [P, 24])

        load = {k: sem(f"load_{k}") for k in ("x", "up0", "up1", "rest", "small")}
        staged_free = sem("staged_free")
        consts_ready = sem("consts_ready")
        bar = sem("phase_barrier")
        stored = sem("stored")
        step = sem("route_step")

        names = ["P", "F0a", "A0", "F0b", "F1a", "A1", "F1b"]
        sems = {}
        for n in names:
            kinds = ["tr_done", "xt_copied", "lg_done", "lg_copied", "var_ready", "rstd_ready", "xn_ready"]
            if n[0] == "F":
                kinds += ["up_done", "act_done", "h_ready", "dn_done", "acc_done"]
            if n[0] == "A":
                kinds += ["xs_ready", "pj_done", "asm_done", "qk_tr", "qk_copied", "sc_done", "sc_free", "m_ready",
                          "q2_tr", "q2_copied", "st_done", "p_ready", "pv_done", "ot_copied", "on_tr", "on_ready",
                          "oT_tr", "oT_ready", "o_done", "x_added", "dg_done", "dp_ready", "u_ready", "y_ready",
                          "s_ready", "t_ready", "pvh_done", "y_exp"]
            sems[n] = {k: sem(f"{n}_{k}") for k in kinds if not (k == "x" or (n == "A0" and k in (
                "dg_done", "dp_ready", "u_ready", "y_ready", "s_ready", "t_ready", "pvh_done", "y_exp")) or (n == "A1" and k in (
                    "sc_done", "sc_free", "m_ready", "q2_tr", "q2_copied", "st_done", "p_ready", "pv_done")))}

        ENGINES = 4

        def barrier(eng, k):
            eng.drain().then_inc(bar, 1)
            eng.wait_ge(bar, ENGINES * (k + 1))

        def norm_vector(eng, s, c, lay):
            eng.drain()
            for t in range(TPC):
                eng.bn_stats(bn[:, t, :], X[:, bass.ds(TPC * c + t, 1), :].rearrange("p a d -> p (a d)"))
            eng.drain()
            for t in range(TPC):
                eng.bn_aggr(mv[:, t, :], bn[:, t, :])
            eng.drain()
            eng.tensor_scalar(var_eps[:, :], mv[:, :, 1], EPS, None, ALU.add).then_inc(s["var_ready"], 1)
            eng.wait_ge(s["rstd_ready"], c + 1)
            eng.wait_ge(s["tr_done"], c + 1)
            for t in range(TPC):
                last = eng.tensor_scalar(xn[:, t, :], X[:, bass.ds(TPC * c + t, 1), :].rearrange("p a d -> p (a d)"),
                                         mv[:, t, 0:1], rstd[:, t:t + 1], ALU.subtract, ALU.mult)
            last.then_inc(s["xn_ready"], 1)
            if lay is not None:
                eng.wait_ge(s["lg_done"], c + 1)
                lg = ps[:, 7, 0:TPC * E].rearrange("p (t e) -> p t e", e=E)
                dst = logits[:, bass.ds(TPC * c, TPC), :]
                if lay == 0:
                    eng.tensor_tensor(dst, lg, ebias[:, :].unsqueeze(1).to_broadcast([P, TPC, E]),
                                      ALU.add).then_inc(s["lg_copied"], 1)
                else:
                    eng.tensor_copy(dst, lg).then_inc(s["lg_copied"], 1)

        def norm_gpsimd(eng, s, c):
            eng.wait_ge(s["var_ready"], c + 1)
            eng.tensor_tensor(rstd[:, :], var_eps[:, :], half_neg[:, :], ALU.pow).then_inc(s["rstd_ready"], 1)

        def norm_tensor(eng, s, c, lay):
            eng.wait_ge(s["xn_ready"], c + 1)
            eng.wait_ge(s["xt_copied"], 2 * c + 2)
            for t in range(TPC):
                last = eng.transpose(ps[:, 6, t * P:(t + 1) * P], xn[:, t, :], ident[:, :])
            last.then_inc(s["tr_done"], 1)
            if lay is not None:
                eng.wait_ge(s["xt_copied"], 2 * c + 4)
                eng.wait_ge(s["lg_copied"], c + 1)
                for t in range(TPC):
                    last = eng.matmul(ps[:, 7, t * E:(t + 1) * E], xT_c[:, t * P:(t + 1) * P], rw[lay][:, :],
                                      start=True, stop=True)
                last.then_inc(s["lg_done"], 1)

        def norm_scalar(eng, s, c, lay):
            eng.wait_ge(s["tr_done"], c + 2)
            if lay is not None:
                eng.wait_ge(s["lg_copied"], c + 1)
            eng.activation(xT_c[:, :], ps[:, 6, :], ACT.Copy).then_inc(s["xt_copied"], 1)
            eng.activation(XT[:, bass.ds(c * S, S)], ps[:, 6, :], ACT.Copy).then_inc(s["xt_copied"], 1)

        def norm_credits_tensor(eng, s):
            eng.sem_inc(s["tr_done"], 1)

        def norm_credits_scalar(eng, s):
            eng.sem_inc(s["xt_copied"], 2)

        def norm_credits_vector(eng, s, lay):
            if lay is not None:
                eng.sem_inc(s["lg_copied"], 1)

        def ffn_shape(lay):
            return (U0, HB0, 2, 2) if lay == 0 else (U1, HB1, 1, 4)

        def ffn_split(eng, XH, XL):
            eng.tensor_copy(XH[:, :], XT[:, :])
            eng.drain()
            eng.tensor_tensor(XL[:, :], XT[:, :], XH[:, :].bitcast(F32), ALU.subtract)
            eng.drain()

        def ffn_tensor(eng, s, lay, XH, XL, hT, w_hi, w_lo, dn, nxt):
            U, HB, G, RING = ffn_shape(lay)
            free = s["h_ready"] if lay == 0 else s["act_done"]
            norm_credits_tensor(eng, s)
            eng.sem_inc(s["dn_done"], 2)
            with eng.Fori(0, B) as c:
                for e in range(U + 1):
                    if e < U:
                        for hb in range(HB):
                            j = e * HB + hb
                            eng.wait_ge(free, c * (U * HB) + j + 1)
                            for g in range(G):
                                bank = (j * G + g) % 4
                                cols = slice((hb * G + g) * P, (hb * G + g + 1) * P)
                                rows = bass.ds(c * S, S)
                                eng.matmul(ps[:, bank, :], w_lo[:, e, cols], XH[:, rows], start=True, stop=False)
                                eng.matmul(ps[:, bank, :], w_hi[:, e, cols], XL[:, rows], start=False, stop=False)
                                last = eng.matmul(ps[:, bank, :], w_hi[:, e, cols], XH[:, rows],
                                                  start=False, stop=True)
                            last.then_inc(s["up_done"], 1)
                    if e > 0:
                        d = e - 1
                        eng.wait_ge(s["h_ready"], c * (U * HB) + (d + 1) * HB + RING)
                        eng.wait_ge(s["acc_done"], c * U + d + 1)
                        for t in range(TPC):
                            for hb in range(HB):
                                last = eng.matmul(ps[:, 4 + d % 2, t * P:(t + 1) * P],
                                                  hT[:, d % 2, hb, t * P:(t + 1) * P], dn[:, d, hb, :],
                                                  start=(hb == 0), stop=(hb == HB - 1))
                        last.then_inc(s["dn_done"], 1)
                if nxt != "end":
                    norm_tensor(eng, s, c, nxt)

        def ffn_scalar(eng, s, lay, act_out, nxt):
            U, HB, G, RING = ffn_shape(lay)
            norm_credits_scalar(eng, s)
            if lay == 1:
                eng.sem_inc(s["act_done"], RING)
            eng.preload_act_table(ACT.Silu)
            with eng.Fori(0, B) as c:
                for j in range(U * HB):
                    n = c * (U * HB) + j
                    eng.wait_ge(s["up_done"], n + 1)
                    eng.wait_ge(s["h_ready"], n + 1)
                    eng.activation(act_out[:, j % RING, :], ps[:, (j * G) % 4, :],
                                   ACT.Silu if lay == 0 else ACT.Relu).then_inc(s["act_done"], 1)
                if nxt != "end":
                    norm_scalar(eng, s, c, nxt)

        def ffn_vector(eng, s, lay, act_out, hT, acc, nxt):
            U, HB, G, RING = ffn_shape(lay)
            if nxt != "end":
                norm_credits_vector(eng, s, nxt)
            eng.sem_inc(s["h_ready"], RING)
            eng.sem_inc(s["acc_done"], 2)
            more = RING if lay == 1 else 0
            with eng.Fori(0, B) as c:
                eng.drain()
                eng.tensor_copy(cw_c[:, :, :], cw[:, bass.ds(TPC * c, TPC), :])
                for e in range(U + 1):
                    if e < U:
                        eng.wait_ge(s["dn_done"], c * U + e + 1)
                        for hb in range(HB):
                            j = e * HB + hb
                            eng.wait_ge(s["act_done"], c * (U * HB) + j + 1 + more)
                            a = act_out[:, j % RING, :]
                            b = ps[:, (j * G + 1) % 4, :] if lay == 0 else a
                            eng.tensor_tensor(hT[:, e % 2, hb, :], a, b, ALU.mult).then_inc(s["h_ready"], 1)
                    if e > 0:
                        d = e - 1
                        eng.drain()
                        eng.wait_ge(s["dn_done"], c * U + d + 3)
                        for t in range(TPC):
                            x_t = X[:, bass.ds(TPC * c + t, 1), :].rearrange("p a d -> p (a d)")
                            routed = d - (U - E)
                            last = eng.scalar_tensor_tensor(
                                out=x_t if d == U - 1 else acc[:, t, :],
                                in0=ps[:, 4 + d % 2, t * P:(t + 1) * P],
                                scalar=cw_c[:, t, routed:routed + 1] if routed >= 0 else 0.5,
                                in1=x_t if d == 0 else acc[:, t, :], op0=ALU.mult, op1=ALU.add)
                        last.then_inc(s["acc_done"], 1)
                if nxt != "end":
                    norm_vector(eng, s, c, nxt)

        def ffn_gpsimd(eng, s, nxt):
            if nxt != "end":
                with eng.Fori(0, B) as c:
                    norm_gpsimd(eng, s, c)

        def route_vector(eng, buf, n, lay):
            work, oh, oh_b, m, ex, pr, rank, tot, cum, incr = buf

            def be(a):
                return a.unsqueeze(2).to_broadcast([P, TILES, E])

            src = logits
            for k in range(2):
                eng.tensor_reduce(m[:, k, :], src[:, :, :], AX.X, ALU.max)
                eng.drain()
                eng.tensor_tensor(work[:, 0], src[:, :, :], be(m[:, k, :]), ALU.is_equal)
                eng.drain()
                eng.tensor_tensor(work[:, 1], work[:, 0], incr[:, :].unsqueeze(1).to_broadcast([P, TILES, E]), ALU.mult)
                eng.drain()
                eng.tensor_reduce(m[:, 2, :], work[:, 1], AX.X, ALU.max)
                eng.drain()
                eng.tensor_tensor(oh[:, k], work[:, 1], be(m[:, 2, :]), ALU.is_equal)
                eng.drain()
                if k == 0:
                    eng.scalar_tensor_tensor(out=work[:, 2].rearrange("p t e -> p (t e)"),
                                             in0=oh[:, 0].rearrange("p t e -> p (t e)"), scalar=NEG,
                                             in1=logits[:, :, :].rearrange("p t e -> p (t e)"),
                                             op0=ALU.mult, op1=ALU.add)
                    eng.drain()
                    src = work[:, 2]
            eng.tensor_tensor(ex[:, 0, :], m[:, 1, :], m[:, 0, :], ALU.subtract).then_inc(step, 1)
            for k in range(2):
                eng.tensor_copy(oh_b[:, k].rearrange("p e t -> p t e"), oh[:, k])
            eng.drain().then_inc(step, 1)
            eng.wait_ge(step, n + 3)
            eng.tensor_scalar(ex[:, 2, :], ex[:, 1, :], 1.0, None, ALU.add)
            eng.drain()
            eng.reciprocal(pr[:, 0, :], ex[:, 2, :])
            eng.drain()
            eng.tensor_tensor(pr[:, 1, :], ex[:, 1, :], pr[:, 0, :], ALU.mult)
            eng.drain()
            if lay == 1:
                eng.wait_ge(step, n + 4)
                w3 = ps[:, 0, :].rearrange("p (k e t) -> p k e t", k=2, e=E)
                t3 = ps[:, 1, :].rearrange("p (k e t) -> p k e t", k=2, e=E)
                for k in range(2):
                    eng.tensor_copy(tot[:, :, k, :], t3[:, k])
                eng.drain()
                for e in range(E):
                    eng.tensor_tensor_scan(cum[:, e, :], ones_f[:, 0:2 * TILES], tot[:, e].rearrange("p k t -> p (k t)"),
                                           0.0, ALU.mult, ALU.add)
                eng.drain()
                eng.tensor_tensor(cum[:, :, :], cum[:, :, :], tot[:, :, :, :].rearrange("p e k t -> p e (k t)"),
                                  ALU.subtract)
                eng.drain()
                for k in range(2):
                    eng.tensor_tensor(rank[:, k], cum[:, :, k * TILES:(k + 1) * TILES].rearrange("p e t -> p t e"),
                                      w3[:, k].rearrange("p e t -> p t e"), ALU.add)
                eng.drain()
                for k in range(2):
                    eng.scalar_tensor_tensor(out=oh[:, k].rearrange("p t e -> p (t e)"),
                                             in0=rank[:, k].rearrange("p t e -> p (t e)"), scalar=float(CAP),
                                             in1=oh[:, k].rearrange("p t e -> p (t e)"), op0=ALU.is_lt, op1=ALU.mult)
                eng.drain()
            for k in range(2):
                eng.tensor_tensor(work[:, k], oh[:, k], be(pr[:, k, :]), ALU.mult)
            eng.drain()
            eng.tensor_tensor(work[:, 2], work[:, 0], work[:, 1], ALU.add)
            eng.drain()
            eng.tensor_scalar(cw[:, :, :], work[:, 2], 0.5, None, ALU.mult)

        def route_scalar(eng, buf, n):
            ex = buf[4]
            eng.wait_ge(step, n + 2)
            eng.activation(ex[:, 1, :], ex[:, 0, :], ACT.Exp).then_inc(step, 1)

        def route_tensor(eng, buf, n, lay):
            oh_b = buf[2]
            if lay == 1:
                eng.wait_ge(step, n + 3)
                rhs = oh_b[:, :, :, :].rearrange("p k e t -> p (k e t)")
                eng.matmul(ps[:, 0, :], before[:, :], rhs, start=True, stop=True)
                eng.matmul(ps[:, 1, :], ones_b[:, :], rhs, start=True, stop=True).then_inc(step, 1)

        ROUTE_STEPS = [3, 4]

        def route_buffers(stack, phase):
            def b(name, shape, dt=F32):
                return sb(f"{phase}_{name}", shape, dt, stack)
            return [b("r_work", [P, 3, TILES, E]), b("r_oh", [P, 2, TILES, E]), b("r_ohb", [P, 2, E, TILES], BF16),
                    b("r_m", [P, 3, TILES]), b("r_ex", [P, 3, TILES]), b("r_pr", [P, 2, TILES]),
                    b("r_rank", [P, 2, TILES, E]), b("r_tot", [P, E, 2, TILES]), b("r_cum", [P, E, 2 * TILES]), incr]

        out_w1 = sb("out_w1", [P, D])
        qkv_w1_s = sb("qkv_w1_s", [P, 3 * D])
        incr = sb("incr", [P, E])

        def run(name, body):
            with nc.Block() as block:
                body(block)

        def project_tensor(eng, s, c, lay):
            eng.wait_ge(s["xs_ready"], c + 1)
            for t in range(TPC):
                if t >= 2:
                    eng.wait_ge(s["asm_done"], c * TPC + t - 1)
                eng.matmul(ps[:, 6 + t % 2, 0:3 * D], xT_c[:, t * P:(t + 1) * P], qkv_w[lay][:, :],
                           start=True, stop=True).then_inc(s["pj_done"], 1)

        def tail_scalar(eng, s, c, OT, oT):
            for t in range(TPC):
                eng.wait_ge(s["oT_tr"], c * TPC + t + 1)
                eng.activation(oT[:, t % 2, :], ps[:, 5, 0:P], ACT.Copy).then_inc(s["oT_ready"], 1)

        def tail_tensor(eng, s, c, lay, OT, on, oT):
            for t in range(TPC):
                eng.wait_ge(s["ot_copied"], (c + 1) * 4)
                if t >= 1:
                    eng.wait_ge(s["x_added"], c * TPC + t)
                for g in range(4):
                    last = eng.transpose(ps[:, 4, g * P:(g + 1) * P], OT[:, g, t * P:(t + 1) * P], ident[:, :])
                last.then_inc(s["on_tr"], 1)
                eng.wait_ge(s["on_ready"], c * TPC + t + 1)
                eng.transpose(ps[:, 5, 0:P], on[:, :], ident[:, :]).then_inc(s["oT_tr"], 1)
                eng.wait_ge(s["oT_ready"], c * TPC + t + 1)
                eng.matmul(ps[:, 5, P:2 * P], oT[:, t % 2, :], out_w[lay][:, :], start=True,
                           stop=True).then_inc(s["o_done"], 1)

        def tail_vector(eng, s, c, lay, on, rden):
            for t in range(TPC):
                eng.wait_ge(s["on_tr"], c * TPC + t + 1)
                v = ps[:, 4, :].rearrange("p (h r) -> p h r", r=32)
                eng.reciprocal(rden[:, :], v[:, :, HD])
                eng.drain()
                eng.tensor_tensor(on[:, :].rearrange("p (h d) -> p h d", d=HD), v[:, :, 0:HD],
                                  rden[:, :].unsqueeze(2).to_broadcast([P, H, HD]), ALU.mult).then_inc(s["on_ready"], 1)
                eng.wait_ge(s["o_done"], c * TPC + t + 1)
                x_t = X[:, bass.ds(TPC * c + t, 1), :].rearrange("p a d -> p (a d)")
                if lay == 0:
                    eng.tensor_tensor(x_t, x_t, bfc[:, :], ALU.add)
                    eng.drain()
                eng.tensor_tensor(x_t, x_t, ps[:, 5, P:2 * P], ALU.add).then_inc(s["x_added"], 1)

        r0 = ExitStack()
        wfc = sb("wfc", [P, D], F32, r0)
        wo_t = sb("wo_t", [P, P], F32, r0)
        bq_s, bk, bv, bfc = (sb(n, [P, D], F32, r0) for n in ("bq_s", "bk", "bv", "bfc"))
        qkv_w = [sb("qkv_w0_s", [P, 3 * D], F32, r0), qkv_w1_s]
        out_w = [sb("out_w0", [P, D], F32, r0), out_w1]
        up0_hi = sb("up0_hi", [P, U0, 2 * HID0], F32R, r0)
        up0_lo = sb("up0_lo", [P, U0, 2 * HID0], F32R, r0)
        dn0 = sb("dn0", [P, U0, HB0, D], F32, r0)

        with ExitStack() as st:
            stage = sb("stage", [P, U0 * 2 * HID0], F32, st)
            stage1 = sb("stage1", [P, U1 * HID1], F32, st)
            wo_bd = sb("wo_bd", [P, P], F32, st)
            iota_i = sb("iota_i", [P, E], I32, st)

            def body(block):
                s = sems["P"]

                @block.sync
                def _(eng):
                    eng.dma_start(X[:, :, :], x).then_inc(load["x"], 16)
                    for dst, src in ((rw[0], router0), (rw[1], router1), (wfc, wfc0), (qkv_w[0], w_qkv0),
                                     (qkv_w[1], w_qkv1), (out_w[1], wo1)):
                        eng.dma_start(dst[:, :], src).then_inc(load["small"], 16)
                    eng.dma_start(ebias[:, :], expert_bias.to_broadcast([P, E])).then_inc(load["small"], 16)
                    eng.dma_start(alpha_s[:, :], alpha.to_broadcast([P, 1])).then_inc(load["small"], 16)
                    for n, dst in enumerate((bq_s, bk, bv, bfc)):
                        eng.dma_start(dst[:, :], bias_rows0[n:n + 1, :].to_broadcast([P, D])).then_inc(load["small"], 16)
                    eng.wait_ge(consts_ready, 1)
                    for h in range(H):
                        eng.dma_start(wo_t[h * HD:(h + 1) * HD, h * HD:(h + 1) * HD], wo0_t[h]).then_inc(load["small"], 16)
                    eng.dma_start(stage[:, :], up0).then_inc(load["up0"], 16)
                    eng.dma_start(dn0[:, :, :, :], down0).then_inc(load["rest"], 16)
                    eng.dma_start(stage1[:, :], up1).then_inc(load["up1"], 16)
                    eng.dma_start(dn1[:, :, :, :], down1).then_inc(load["rest"], 16)

                @block.gpsimd
                def _(eng):
                    eng.memset(wo_t[:, :], 0.0)
                    eng.drain().then_inc(consts_ready, 1)
                    eng.memset(ident[:, :], 0.0)
                    eng.memset(ones_f[:, :], 1.0)
                    eng.memset(ones_b[:, :], 1.0)
                    eng.memset(half_neg[:, :], -0.5)
                    eng.iota(iota_i[:, :], pattern=[[-1, E]], base=E, channel_multiplier=0)
                    eng.drain()
                    eng.affine_select(out=ident[:, :], in_=ident[:, :], compare_op=ALU.not_equal, fill=1.0, base=0,
                                      pattern=[[-1, P]], channel_multiplier=1)
                    eng.affine_select(out=before[:, :], in_=ones_b[:, :], compare_op=ALU.is_gt, fill=0.0, base=0,
                                      pattern=[[1, P]], channel_multiplier=-1)
                    eng.drain()
                    eng.tensor_copy(ident_b[:, :], ident[:, :])
                    eng.tensor_copy(incr[:, :], iota_i[:, :])
                    eng.drain().then_inc(consts_ready, 1)
                    with eng.Fori(0, B) as c:
                        norm_gpsimd(eng, s, c)
                    eng.wait_ge(load["up1"], 16)
                    eng.tensor_copy(up1_hi[:, :, :].rearrange("p u n -> p (u n)"), stage1[:, :])
                    eng.drain()
                    eng.tensor_tensor(up1_lo[:, :, :].rearrange("p u n -> p (u n)"), stage1[:, :],
                                      up1_hi[:, :, :].rearrange("p u n -> p (u n)").bitcast(F32), ALU.subtract)
                    barrier(eng, 0)

                @block.tensor
                def _(eng):
                    norm_credits_tensor(eng, s)
                    eng.wait_ge(consts_ready, 2)
                    eng.wait_ge(load["small"], 16 * (12 + H))
                    with eng.Fori(0, B) as c:
                        norm_tensor(eng, s, c, 0)
                    eng.matmul(ps[:, 0, 0:D], wo_t[:, :], wfc[:, :], start=True, stop=True).then_inc(step, 1)
                    barrier(eng, 0)

                @block.scalar
                def _(eng):
                    norm_credits_scalar(eng, s)
                    with eng.Fori(0, B) as c:
                        norm_scalar(eng, s, c, 0)
                    eng.wait_ge(step, 1)
                    eng.activation(out_w[0][:, :], ps[:, 0, 0:D], ACT.Copy)
                    barrier(eng, 0)

                @block.vector
                def _(eng):
                    norm_credits_vector(eng, s, 0)
                    eng.wait_ge(load["x"], 16)
                    eng.wait_ge(load["small"], 16 * (12 + H))
                    with eng.Fori(0, B) as c:
                        norm_vector(eng, s, c, 0)
                    eng.tensor_scalar(bq_s[:, :], bq_s[:, :], INV_SQRT, None, ALU.mult)
                    eng.wait_ge(load["up0"], 16)
                    eng.tensor_copy(up0_hi[:, :, :].rearrange("p u n -> p (u n)"), stage[:, :])
                    eng.drain()
                    eng.tensor_tensor(up0_lo[:, :, :].rearrange("p u n -> p (u n)"), stage[:, :],
                                      up0_hi[:, :, :].rearrange("p u n -> p (u n)").bitcast(F32), ALU.subtract)
                    eng.wait_ge(load["rest"], 32)
                    barrier(eng, 0)

            run("P", body)

        state = {"step": 1, "bar": 1}

        def ffn_phase(name, lay, nxt):
            s = sems[name]
            n0, b0 = state["step"], state["bar"]
            state["step"] += ROUTE_STEPS[lay]
            state["bar"] += 1
            U, HB, G, RING = ffn_shape(lay)
            w_hi, w_lo, dn = (up0_hi, up0_lo, dn0) if lay == 0 else (up1_hi, up1_lo, dn1)
            with ExitStack() as st:
                XH = sb(f"{name}_xh", [P, TOK], F32R, st)
                XL = sb(f"{name}_xl", [P, TOK], F32R, st)
                act_out = sb(f"{name}_act", [P, RING, S], F32, st)
                acc = sb(f"{name}_acc", [P, TPC, D], F32, st)
                hT = sb(f"{name}_hT", [P, 2, HB, S], F32, st)
                with ExitStack() as st2:
                    buf = route_buffers(st2, name)
                    route_done = sem(f"{name}_route_done")

                    def body_r(block):
                        @block.vector
                        def _(eng):
                            route_vector(eng, buf, n0, lay)
                            ffn_split(eng, XH, XL)
                            eng.drain().then_inc(route_done, 1)
                            eng.wait_ge(route_done, 3)

                        @block.scalar
                        def _(eng):
                            route_scalar(eng, buf, n0)
                            eng.drain().then_inc(route_done, 1)
                            eng.wait_ge(route_done, 3)

                        @block.tensor
                        def _(eng):
                            route_tensor(eng, buf, n0, lay)
                            eng.drain().then_inc(route_done, 1)
                            eng.wait_ge(route_done, 3)

                    run(name, body_r)

                def body(block):
                    @block.tensor
                    def _(eng):
                        ffn_tensor(eng, s, lay, XH, XL, hT, w_hi, w_lo, dn, nxt)
                        barrier(eng, b0)

                    @block.scalar
                    def _(eng):
                        ffn_scalar(eng, s, lay, act_out, nxt)
                        barrier(eng, b0)

                    @block.vector
                    def _(eng):
                        ffn_vector(eng, s, lay, act_out, hT, acc, nxt)
                        barrier(eng, b0)

                    @block.gpsimd
                    def _(eng):
                        ffn_gpsimd(eng, s, nxt)
                        barrier(eng, b0)

                run(name, body)

        def window(t):
            lo, hi = max(0, t * P - HALO), min(S, t * P - HALO + WIN)
            return lo, hi, lo - (t * P - HALO), hi - (t * P - HALO)

        def unit_head(u, r, b):
            return 2 * (u // 2) + r, 2 * (u % 2) + b

        def attn0():
            name, lay, nxt = "A0", 0, 0
            s = sems[name]
            b0, n0 = state["bar"], state["step"]
            state["bar"] += 1
            state["step"] += 5
            with ExitStack() as st:
                def ab(n, shape, dt=F32):
                    return sb(f"{name}_{n}", shape, dt, st)
                xa = ab("xa", [P, S])
                QA = ab("QA", [P, TPC, H, 32], F32R)
                KA = ab("KA", [P, TPC, H, 32], F32R)
                VA = ab("VA", [P, TPC, H, 32])
                QT = ab("QT", [P, 4, S], F32R)
                KT = ab("KT", [P, 4, S], F32R)
                PT = ab("PT", [P, 2, 2, 2, WIN])
                OT = ab("OT", [P, 4, S])
                qs = ab("qs", [P, 2, D])
                nmax = ab("nmax", [P, TPC, 2, 2, 2, 2])
                on = ab("on", [P, D])
                oT = ab("oT", [P, 2, P])
                rden = ab("rden", [P, H])
                dist = OT[:, 0:2, :].rearrange("p a q -> p (a q)").rearrange("p (a w) -> p a w", w=WIN)
                dist_i = OT[:, 2, 0:WIN].bitcast(I32)
                mask = ab("mask", [P, WIN], BF16)
                pad_ready = sem("A0_pad_ready")

                def body(block):
                    @block.gpsimd
                    def _(eng):
                        eng.iota(dist_i, pattern=[[1, WIN]], base=-HALO, channel_multiplier=-1)
                        for a in (QA, KA, VA):
                            eng.memset(a[:, :, :, :].rearrange("p t h r -> p (t h r)").bitcast(F32), 0.0)
                        eng.drain()
                        eng.memset(KA[:, :, :, 24:26].bitcast(F32), 1.0)
                        eng.memset(VA[:, :, :, HD:HD + 1], 1.0)
                        eng.drain().then_inc(pad_ready, 1)
                        with eng.Fori(0, B) as c:
                            norm_gpsimd(eng, s, c)
                        barrier(eng, b0)

                    @block.scalar
                    def _(eng):
                        norm_credits_scalar(eng, s)
                        eng.preload_act_table(ACT.Exp)
                        eng.activation(col[:, 17:18], alpha_s[:, :], ACT.Exp, scale=-1.0).then_inc(step, 1)
                        eng.wait_ge(step, n0 + 3)
                        eng.activation(col[:, 22:23], ps[:, 0, 0:1], ACT.Exp, scale=-1.0).then_inc(step, 1)
                        eng.sem_inc(s["p_ready"], 2)
                        with eng.Fori(0, B) as c:
                            eng.activation(xa[:, :], XT[:, bass.ds(c * S, S)], ACT.Copy).then_inc(s["xs_ready"], 1)
                            for t in range(TPC):
                                eng.wait_ge(s["qk_tr"], c * TPC + t + 1)
                                for bank, dst in ((4, QT), (5, KT)):
                                    eng.activation(dst[:, :, t * P:(t + 1) * P],
                                                   ps[:, bank, :].rearrange("p (g q) -> p g q", g=4),
                                                   ACT.Copy).then_inc(s["qk_copied"], 1)
                            for t in range(TPC):
                                eng.wait_ge(s["q2_tr"], c * TPC + t + 1)
                                eng.activation(QT[:, :, t * P:(t + 1) * P],
                                               ps[:, 4, :].rearrange("p (g q) -> p g q", g=4),
                                               ACT.Copy).then_inc(s["q2_copied"], 1)
                            for n in range(4 * TPC):
                                _, _, w0, w1 = window(n % TPC)
                                b = 2 * (n % 2)
                                eng.wait_ge(s["st_done"], c * 16 + n + 1)
                                eng.wait_ge(s["pv_done"], c * 16 + n + 1)
                                eng.activation(PT[:, n % 2, :, :, w0:w1],
                                               ps[:, b:b + 2, :].rearrange("p b (r w) -> p b r w", r=2)[:, :, :, w0:w1],
                                               ACT.Exp).then_inc(s["p_ready"], 1)
                            tail_scalar(eng, s, c, OT, oT)
                            norm_scalar(eng, s, c, nxt)
                        barrier(eng, b0)

                    @block.vector
                    def _(eng):
                        norm_credits_vector(eng, s, nxt)
                        eng.sem_inc(s["sc_free"], 2)
                        ends = XT[:, :].rearrange("p (b s) -> p b s", b=B)
                        eng.wait_ge(step, n0 + 1)
                        eng.tensor_tensor(col[:, 0:B], ends[:, :, S - 1], ends[:, :, S - 2], ALU.subtract)
                        eng.tensor_scalar(col[:, 18:19], col[:, 17:18], 1.0, None, ALU.add)
                        eng.drain()
                        eng.scalar_tensor_tensor(out=col[:, 8:16], in0=col[:, 0:B], scalar=-1.0, in1=col[:, 0:B],
                                                 op0=ALU.mult, op1=ALU.max)
                        eng.reciprocal(col[:, 19:20], col[:, 18:19])
                        eng.drain()
                        eng.tensor_reduce(col[:, 16:17], col[:, 8:16], AX.X, ALU.add)
                        eng.tensor_scalar(col[:, 20:21], col[:, 19:20], -1.0, 1.0, ALU.mult, ALU.add)
                        eng.drain()
                        eng.tensor_tensor(col[:, 18:19], col[:, 20:21], col[:, 8:9], ALU.mult)
                        eng.tensor_scalar(col[:, 21:22], col[:, 16:17], col[:, 19:20], 1.0 / (B * D), ALU.mult, ALU.mult)
                        eng.drain()
                        eng.scalar_tensor_tensor(out=col[:, 20:21], in0=col[:, 18:19], scalar=ident[:, 0:1],
                                                 in1=col[:, 21:22], op0=ALU.mult, op1=ALU.add)
                        eng.drain().then_inc(step, 1)
                        eng.wait_ge(pad_ready, 1)
                        eng.tensor_copy(dist[:, 0, :], dist_i)
                        eng.drain()
                        eng.scalar_tensor_tensor(out=dist[:, 1, :], in0=dist[:, 0, :], scalar=-1.0, in1=dist[:, 0, :],
                                                 op0=ALU.mult, op1=ALU.max)
                        eng.drain()
                        eng.tensor_scalar(dist[:, 2, :], dist[:, 1, :], 2.0, None, ALU.mult)
                        eng.wait_ge(step, n0 + 4)
                        eng.tensor_scalar(col[:, 18:19], col[:, 22:23], 1.0, None, ALU.add)
                        eng.drain()
                        eng.reciprocal(col[:, 19:20], col[:, 18:19])
                        eng.drain()
                        eng.tensor_scalar(col[:, 21:22], col[:, 19:20], 96.0, 24.0, ALU.mult, ALU.add)
                        eng.drain()
                        eng.tensor_scalar(mask[:, :], dist[:, 2, :], col[:, 21:22], NEG, ALU.is_gt, ALU.mult)
                        eng.drain().then_inc(step, 1)
                        with eng.Fori(0, B) as c:
                            for t in range(TPC):
                                eng.wait_ge(s["pj_done"], c * TPC + t + 1)
                                pj = ps[:, 6 + t % 2, :]
                                eng.scalar_tensor_tensor(out=qs[:, 0, :], in0=pj[:, 0:D], scalar=INV_SQRT,
                                                         in1=bq_s[:, :], op0=ALU.mult, op1=ALU.add)
                                eng.tensor_tensor(qs[:, 1, :], pj[:, D:2 * D], bk[:, :], ALU.add)
                                eng.tensor_tensor(VA[:, t, :, 0:HD], pj[:, 2 * D:3 * D].rearrange("p (h d) -> p h d", d=HD),
                                                  bv[:, :].rearrange("p (h d) -> p h d", d=HD), ALU.add)
                                eng.drain()
                                q3 = qs[:, 0, :].rearrange("p (h d) -> p h d", d=HD)
                                k3 = qs[:, 1, :].rearrange("p (h d) -> p h d", d=HD)
                                eng.tensor_copy(QA[:, t, :, 0:HD], q3)
                                eng.tensor_copy(QA[:, t, :, HD:2 * HD], q3)
                                eng.tensor_copy(KA[:, t, :, 0:HD], k3)
                                eng.tensor_copy(KA[:, t, :, 2 * HD:3 * HD], k3)
                                eng.drain()
                                eng.tensor_tensor(QA[:, t, :, 2 * HD:3 * HD], q3, QA[:, t, :, 0:HD].bitcast(F32),
                                                  ALU.subtract)
                                eng.tensor_tensor(KA[:, t, :, HD:2 * HD], k3, KA[:, t, :, 0:HD].bitcast(F32),
                                                  ALU.subtract)
                                eng.drain().then_inc(s["asm_done"], 1)
                            for n in range(4 * TPC):
                                t, g = n // 4, n % 4
                                _, _, w0, w1 = window(t)
                                b = 2 * (n % 2)
                                eng.wait_ge(s["sc_done"], c * 16 + n + 1)
                                eng.tensor_reduce(
                                    nmax[:, t, g // 2, :, g % 2, :].rearrange("p r b -> p b r"),
                                    ps[:, b:b + 2, :].rearrange("p b (r w) -> p b r w", r=2)[:, :, :, w0:w1],
                                    AX.X, ALU.max, negate=True).then_inc(s["sc_free"], 1)
                                if g == 3:
                                    m16 = nmax[:, t].rearrange("p g r j b -> p (g r j b)").unsqueeze(2)
                                    eng.drain()
                                    eng.tensor_copy(QA[:, t, :, 24:25], m16)
                                    eng.drain()
                                    eng.tensor_tensor(QA[:, t, :, 25:26], m16, QA[:, t, :, 24:25].bitcast(F32),
                                                      ALU.subtract)
                                    eng.drain().then_inc(s["m_ready"], 1)
                            for g in range(4):
                                eng.wait_ge(s["pv_done"], c * 16 + 8 * (g // 2) + 8 + 2)
                                eng.tensor_copy(OT[:, g, :], ps[:, 6 + g % 2, :]).then_inc(s["ot_copied"], 1)
                            tail_vector(eng, s, c, lay, on, rden)
                            norm_vector(eng, s, c, nxt)
                        barrier(eng, b0)

                    @block.tensor
                    def _(eng):
                        norm_credits_tensor(eng, s)
                        eng.sem_inc(s["qk_copied"], 2)
                        eng.sem_inc(s["q2_copied"], 1)
                        eng.sem_inc(s["pv_done"], 2)
                        eng.wait_ge(step, n0 + 2)
                        eng.matmul(ps[:, 0, 0:1], ones_f[:, :], col[:, 20:21], start=True, stop=True).then_inc(step, 1)
                        eng.wait_ge(step, n0 + 5)
                        eng.wait_ge(pad_ready, 1)

                        def scores(bank, lhs, rhs, rows, u, t):
                            lo, hi, w0, w1 = window(t)
                            for r in range(2):
                                for b in range(2):
                                    g, j = unit_head(u, r, b)
                                    eng.matmul(ps[:, bank + b, r * WIN + w0:r * WIN + w1],
                                               lhs[32 * j:32 * j + rows, g, t * P:(t + 1) * P],
                                               rhs[32 * j:32 * j + rows, g, lo:hi], start=True, stop=False)
                                for b in range(2):
                                    last = eng.matmul(ps[:, bank + b, r * WIN + w0:r * WIN + w1], ident_b[:, :],
                                                      mask[:, w0:w1], start=False, stop=True)
                            return last

                        with eng.Fori(0, B) as c:
                            eng.wait_ge(s["lg_copied"], c + 1)
                            eng.wait_ge(s["xs_ready"], c + 1)
                            for t in range(TPC):
                                if t >= 2:
                                    eng.wait_ge(s["asm_done"], c * TPC + t - 1)
                                eng.matmul(ps[:, 6 + t % 2, 0:3 * D], xa[:, t * P:(t + 1) * P], qkv_w[lay][:, :],
                                           start=True, stop=True).then_inc(s["pj_done"], 1)
                            for t in range(TPC):
                                eng.wait_ge(s["asm_done"], c * TPC + t + 1)
                                eng.wait_ge(s["qk_copied"], 2 * (c * TPC + t) + 2)
                                for bank, src in ((4, QA), (5, KA)):
                                    for g in range(4):
                                        last = eng.transpose(
                                            ps[:, bank, g * P:(g + 1) * P],
                                            src[:, t, 4 * g:4 * g + 4, :].rearrange("p h r -> p (h r)").bitcast(F32),
                                            ident[:, :])
                                last.then_inc(s["qk_tr"], 1)
                            eng.wait_ge(s["qk_copied"], 2 * TPC * (c + 1) + 2)
                            for t in range(TPC + 1):
                                if t < TPC:
                                    for g in range(4):
                                        n = 4 * t + g
                                        eng.wait_ge(s["sc_free"], c * 16 + n + 1)
                                        scores(2 * (n % 2), QT, KT, 24, g, t).then_inc(s["sc_done"], 1)
                                if t > 0:
                                    eng.wait_ge(s["m_ready"], c * TPC + t)
                                    eng.wait_ge(s["q2_copied"], c * TPC + t)
                                    for g in range(4):
                                        last = eng.transpose(
                                            ps[:, 4, g * P:(g + 1) * P],
                                            QA[:, t - 1, 4 * g:4 * g + 4, :].rearrange("p h r -> p (h r)").bitcast(F32),
                                            ident[:, :])
                                    last.then_inc(s["q2_tr"], 1)
                            eng.wait_ge(s["q2_copied"], TPC * (c + 1) + 1)
                            for n in range(4 * TPC + 1):
                                if n < 4 * TPC:
                                    eng.wait_ge(s["p_ready"], c * 16 + n + 1)
                                    scores(2 * (n % 2), KT, QT, 26, n // 4, n % 4).then_inc(s["st_done"], 1)
                                if n > 0:
                                    u, t = (n - 1) // 4, (n - 1) % 4
                                    lo, hi, w0, w1 = window(t)
                                    eng.wait_ge(s["p_ready"], c * 16 + n + 2)
                                    if u == 2 and t == 0:
                                        eng.wait_ge(s["ot_copied"], c * 4 + 2)
                                    for r in range(2):
                                        for b in range(2):
                                            g, j = unit_head(u, r, b)
                                            last = eng.matmul(ps[32 * j:32 * j + 32, 6 + r, lo:hi], VA[:, t, 4 * g + j, :],
                                                              PT[:, (n - 1) % 2, b, r, w0:w1], start=(t == 0),
                                                              stop=(t == TPC - 1), skip_group_check=True)
                                    last.then_inc(s["pv_done"], 1)
                            tail_tensor(eng, s, c, lay, OT, on, oT)
                            norm_tensor(eng, s, c, nxt)
                        barrier(eng, b0)

                run(name, body)

        def attn1():
            name, lay, nxt = "A1", 1, 1
            s = sems[name]
            b0 = state["bar"]
            state["bar"] += 1
            GR = H // 2
            UR, YR = 3, 4
            with ExitStack() as st:
                def ab(n, shape, dt=F32):
                    return sb(f"{name}_{n}", shape, dt, st)
                QA = ab("QA", [P, H, 64], F32R)
                KA = ab("KA", [P, H, 64], F32R)
                VA = ab("VA", [P, TPC, H, 32])
                QT = ab("QT", [P, GR, S], F32R)
                KT = ab("KT", [P, GR, S], F32R)
                OT = ab("OT", [P, 4, S])
                Um = ab("U", [P, UR, TPC, S])
                Y = ab("Y", [P, YR, TPC, S])
                dpos = ab("dpos", [P, 2, S])
                xa = Y[:, YR - 1, TPC - 1, :]
                qk = OT[:, 0, 0:2 * D].rearrange("p (a d) -> p a d", d=D)
                sq = OT[:, 1, 0:2 * D].rearrange("p (a d) -> p a d", d=D)
                nrm = OT[:, 2, 0:18 * H].rearrange("p (n a h) -> p n a h", a=2, h=H)
                oT = Um[:, 0, 0, 0:2 * P].rearrange("p (a q) -> p a q", q=P)
                on = ab("on", [P, D])
                rden = ab("rden", [P, H])
                pad_ready = sem("A1_pad_ready")

                def body(block):
                    @block.gpsimd
                    def _(eng):
                        for a in (QA[:, :, :], KA[:, :, :]):
                            eng.memset(a.rearrange("p h r -> p (h r)").bitcast(F32), 0.0)
                        eng.memset(VA[:, :, :, :].rearrange("p t h r -> p (t h r)"), 0.0)
                        eng.drain()
                        eng.memset(VA[:, :, :, HD:HD + 1], 1.0)
                        eng.memset(QA[:, :, 26:28].bitcast(F32), 1.0)
                        eng.memset(KA[:, :, 24:26].bitcast(F32), 1.0)
                        eng.memset(KA[:, :, 40:41].bitcast(F32), FAR)
                        eng.drain().then_inc(pad_ready, 1)
                        eng.sem_inc(s["t_ready"], UR)
                        with eng.Fori(0, B) as c:
                            for h in range(H):
                                eng.wait_ge(s["s_ready"], c * H + h + 1)
                                y = Y[:, h % YR].rearrange("p t q -> p (t q)")
                                eng.tensor_tensor(y, y, Um[:, h % UR].rearrange("p t q -> p (t q)"),
                                                  ALU.add).then_inc(s["t_ready"], 1)
                            norm_gpsimd(eng, s, c)
                        barrier(eng, b0)

                    @block.scalar
                    def _(eng):
                        norm_credits_scalar(eng, s)
                        eng.sem_inc(s["dp_ready"], 2)
                        with eng.Fori(0, B) as c:
                            eng.activation(xa, XT[:, bass.ds(c * S, S)], ACT.Copy).then_inc(s["xs_ready"], 1)
                            for t in range(TPC):
                                for n, dst in enumerate((QT, KT)):
                                    eng.wait_ge(s["qk_tr"], 2 * (c * TPC + t) + n + 3)
                                    eng.activation(dst[:, :, t * P:(t + 1) * P],
                                                   ps[:, 4:6, :].rearrange("p b (g q) -> p (b g) q", q=P),
                                                   ACT.Copy).then_inc(s["qk_copied"], 1)
                            for pair in range(H // 2 + 1):
                                if pair < H // 2:
                                    for m in range(8 * pair, 8 * pair + 8):
                                        eng.wait_ge(s["dg_done"], c * 64 + m + 1)
                                        eng.wait_ge(s["u_ready"], c * 64 + m + 1)
                                        eng.activation(dpos[:, m % 2, :], ps[:, m % 2, :],
                                                       ACT.Relu).then_inc(s["dp_ready"], 1)
                                if pair > 0:
                                    eng.preload_act_table_set("natural_log_exp_and_others")
                                    for h in (2 * pair - 2, 2 * pair - 1):
                                        y = Y[:, h % YR].rearrange("p t q -> p (t q)")
                                        eng.wait_ge(s["t_ready"], c * H + h + 1 + UR)
                                        eng.activation(y, y, ACT.Ln, bias=1.0)
                                        eng.drain()
                                        eng.activation(y, y, ACT.Exp, scale=-1.0).then_inc(s["y_exp"], 1)
                                if pair < H // 2:
                                    for h in (2 * pair, 2 * pair + 1):
                                        y = Y[:, h % YR].rearrange("p t q -> p (t q)")
                                        eng.wait_ge(s["y_ready"], c * H + h + 1)
                                        eng.activation(y, y, ACT.Sqrt).then_inc(s["s_ready"], 1)
                            tail_scalar(eng, s, c, OT, oT)
                            norm_scalar(eng, s, c, nxt)
                        barrier(eng, b0)

                    @block.vector
                    def _(eng):
                        norm_credits_vector(eng, s, nxt)
                        eng.sem_inc(s["u_ready"], 2)
                        eng.wait_ge(pad_ready, 1)

                        def split(dst_hi, dst_lo, src):
                            for d in dst_hi:
                                eng.tensor_copy(d, src)
                            eng.drain()
                            eng.tensor_tensor(dst_lo, src, dst_hi[0].bitcast(F32), ALU.subtract)

                        with eng.Fori(0, B) as c:
                            for t in range(TPC):
                                eng.wait_ge(s["pj_done"], c * TPC + t + 1)
                                pj = ps[:, 6 + t % 2, :]
                                eng.tensor_copy(qk[:, 0, :], pj[:, 0:D])
                                eng.tensor_scalar(qk[:, 1, :], pj[:, D:2 * D], -2.0, None, ALU.mult)
                                eng.tensor_copy(VA[:, t, :, 0:HD], pj[:, 2 * D:3 * D].rearrange("p (h d) -> p h d", d=HD))
                                eng.drain()
                                eng.tensor_tensor(sq[:, :, :], qk[:, :, :], qk[:, :, :], ALU.mult)
                                eng.drain()
                                eng.tensor_reduce(nrm[:, 0], sq[:, :, :].rearrange("p a (h d) -> p a h d", d=HD), AX.X,
                                                  ALU.add)
                                eng.drain()
                                eng.tensor_scalar(nrm[:, 0, 1], nrm[:, 0, 1], 0.25, None, ALU.mult)
                                eng.drain()
                                eng.tensor_scalar(nrm[:, 1], nrm[:, 0], -1.0, 1.0, ALU.mult, ALU.add)
                                eng.drain()
                                eng.tensor_scalar(nrm[:, 2], nrm[:, 1], 0.0, None, ALU.is_gt)
                                eng.tensor_scalar(nrm[:, 3], nrm[:, 1], 0.0, None, ALU.is_lt)
                                eng.tensor_scalar(nrm[:, 4], nrm[:, 1], 0.0, None, ALU.is_equal)
                                eng.drain()
                                eng.tensor_tensor(nrm[:, 5], nrm[:, 1], nrm[:, 4], ALU.add)
                                eng.drain()
                                eng.reciprocal(nrm[:, 6], nrm[:, 5])
                                eng.drain()
                                eng.tensor_scalar(nrm[:, 6, 1], nrm[:, 6, 1], 2.0, None, ALU.mult)
                                eng.drain()
                                eng.tensor_tensor(nrm[:, 7], nrm[:, 6], nrm[:, 2], ALU.mult)
                                eng.scalar_tensor_tensor(out=nrm[:, 8].rearrange("p a h -> p (a h)"),
                                                         in0=nrm[:, 6].rearrange("p a h -> p (a h)"), scalar=-1.0,
                                                         in1=nrm[:, 3].rearrange("p a h -> p (a h)"),
                                                         op0=ALU.mult, op1=ALU.mult)
                                eng.drain()
                                eng.wait_ge(s["qk_tr"], 2 * (c * TPC + t) + 2)

                                def q1(i):
                                    return nrm[:, i, 0].unsqueeze(2)

                                def k1(i):
                                    return nrm[:, i, 1].unsqueeze(2)

                                q3 = qk[:, 0, :].rearrange("p (h d) -> p h d", d=HD)
                                k3 = qk[:, 1, :].rearrange("p (h d) -> p h d", d=HD)
                                split([QA[:, :, 0:8], QA[:, :, 8:16]], QA[:, :, 16:24], q3)
                                split([KA[:, :, 0:8], KA[:, :, 16:24]], KA[:, :, 8:16], k3)
                                split([QA[:, :, 24:25]], QA[:, :, 25:26], q1(0))
                                split([KA[:, :, 26:27]], KA[:, :, 27:28], k1(0))
                                for i, o in ((7, 32), (8, 35)):
                                    split([QA[:, :, o:o + 1], QA[:, :, o + 1:o + 2]], QA[:, :, o + 2:o + 3], q1(i))
                                    split([KA[:, :, o:o + 1], KA[:, :, o + 2:o + 3]], KA[:, :, o + 1:o + 2], k1(i))
                                for n in range(3):
                                    eng.tensor_copy(QA[:, :, 38 + n:39 + n], q1(2 + n))
                                for n in range(2):
                                    eng.tensor_scalar(KA[:, :, 38 + n:39 + n], k1(2 + n), -FAR, FAR, ALU.mult, ALU.add)
                                eng.drain().then_inc(s["asm_done"], 1)
                            for h in range(H):
                                eng.wait_ge(s["t_ready"], c * H + h + 1)
                                for kt in range(TPC):
                                    m = 4 * h + kt
                                    eng.wait_ge(s["dp_ready"], c * 64 + m + 3)
                                    eng.scalar_tensor_tensor(out=Um[:, h % UR, kt, :], in0=ps[:, 2 + m % 2, :],
                                                             scalar=CLAMP, in1=dpos[:, m % 2, :], op0=ALU.min,
                                                             op1=ALU.mult).then_inc(s["u_ready"], 1)
                                eng.drain()
                                eng.wait_ge(s["pvh_done"], c * (H // 2) + h // 2 + 1)
                                u = Um[:, h % UR].rearrange("p t q -> p (t q)")
                                eng.scalar_tensor_tensor(out=Y[:, h % YR].rearrange("p t q -> p (t q)"), in0=u, scalar=2.0,
                                                         in1=u, op0=ALU.add, op1=ALU.mult).then_inc(s["y_ready"], 1)
                                if h % 4 == 3 and h > 4:
                                    g = h // 4 - 1
                                    eng.wait_ge(s["pvh_done"], c * (H // 2) + 2 * g + 4)
                                    eng.tensor_copy(OT[:, g, :], ps[:, 6 + g % 2, :]).then_inc(s["ot_copied"], 1)
                            eng.wait_ge(s["pvh_done"], (c + 1) * (H // 2) + 2)
                            eng.tensor_copy(OT[:, 3, :], ps[:, 7, :]).then_inc(s["ot_copied"], 1)
                            tail_vector(eng, s, c, lay, on, rden)
                            norm_vector(eng, s, c, nxt)
                        barrier(eng, b0)

                    def turn(eng, c, t):
                        for n, src in enumerate((QA, KA)):
                            eng.wait_ge(s["asm_done"], c * TPC + t + 1)
                            eng.wait_ge(s["qk_copied"], 2 * (c * TPC + t) + n + 1)
                            for g in range(GR):
                                last = eng.transpose(
                                    ps[:, 4 + g // 4, (g % 4) * P:(g % 4 + 1) * P],
                                    src[:, 2 * g:2 * g + 2, :].rearrange("p h r -> p (h r)").bitcast(F32), ident[:, :])
                            last.then_inc(s["qk_tr"], 1)

                    @block.tensor
                    def _(eng):
                        norm_credits_tensor(eng, s)
                        eng.sem_inc(s["qk_tr"], 2)
                        eng.sem_inc(s["qk_copied"], 1)
                        eng.sem_inc(s["pvh_done"], 2)
                        with eng.Fori(0, B) as c:
                            eng.wait_ge(s["lg_copied"], c + 1)
                            eng.wait_ge(s["xs_ready"], c + 1)
                            for t in range(TPC):
                                if t >= 2:
                                    eng.wait_ge(s["asm_done"], c * TPC + t - 1)
                                eng.matmul(ps[:, 6 + t % 2, 0:3 * D], xa[:, t * P:(t + 1) * P], qkv_w[lay][:, :],
                                           start=True, stop=True).then_inc(s["pj_done"], 1)
                                if t >= 1:
                                    turn(eng, c, t - 1)
                            turn(eng, c, TPC - 1)
                            eng.wait_ge(s["qk_copied"], 2 * TPC * (c + 1) + 1)
                            for pair in range(H // 2 + 1):
                                if pair < H // 2:
                                    for m in range(8 * pair, 8 * pair + 8):
                                        h, kt = m // 4, m % 4
                                        g, r = h // 2, 64 * (h % 2)
                                        eng.wait_ge(s["dp_ready"], c * 64 + m + 1)
                                        eng.wait_ge(s["u_ready"], c * 64 + m + 1)
                                        eng.matmul(ps[:, m % 2, :], KT[r:r + 28, g, kt * P:(kt + 1) * P],
                                                   QT[r:r + 28, g, :], start=True, stop=True)
                                        eng.matmul(ps[:, 2 + m % 2, :], KT[r + 32:r + 41, g, kt * P:(kt + 1) * P],
                                                   QT[r + 32:r + 41, g, :], start=True, stop=True)\
                                            .then_inc(s["dg_done"], 1)
                                if pair > 0:
                                    h0 = 2 * pair - 2
                                    g = h0 // 4
                                    eng.wait_ge(s["y_exp"], c * H + h0 + 2)
                                    if g >= 2 and h0 % 4 == 0:
                                        eng.wait_ge(s["ot_copied"], c * 4 + g - 1)
                                    for kt in range(TPC):
                                        for h in (h0, h0 + 1):
                                            j = 32 * (h % 4)
                                            last = eng.matmul(ps[j:j + 32, 6 + g % 2, :], VA[:, kt, h, :],
                                                              Y[:, h % YR, kt, :], start=(kt == 0), stop=(kt == TPC - 1))
                                    last.then_inc(s["pvh_done"], 1)
                            tail_tensor(eng, s, c, lay, OT, on, oT)
                            norm_tensor(eng, s, c, nxt)
                        barrier(eng, b0)

                run(name, body)


        phases = [("F0a", lambda: ffn_phase("F0a", 0, None)), ("A0", lambda: attn0()),
                  ("F0b", lambda: ffn_phase("F0b", 0, 1)), ("F1a", lambda: ffn_phase("F1a", 1, None)),
                  ("A1", lambda: attn1()), ("F1b", lambda: ffn_phase("F1b", 1, "end"))]
        for n, (name, f) in enumerate(phases):
            if n >= stop_after:
                break
            f()
            if name == "F0b":
                r0.close()
        if stop_after < 3:
            r0.close()

        with nc.Block() as block:
            @block.sync
            def _(eng):
                eng.wait_ge(bar, ENGINES * state["bar"])
                eng.dma_start(out, X[:, :, :]).then_inc(stored, 16)
                eng.wait_ge(stored, 16)


def kernel(stop_after=99, **inputs):
    import numpy as np
    import concourse.bacc as bacc
    from concourse.bass_utils import run_bass_kernel_spmd

    a = {k: np.asarray(v) for k, v in inputs.items()}
    E_, HID_ = 8, 256

    def up_pair(w1, w3):
        w = np.stack([w1, w3], 1).reshape(w1.shape[0], 2, 2, 128, 128)
        return w.transpose(4, 0, 2, 1, 3).reshape(128, -1)

    w1 = np.concatenate([a["L0_ffn_sw1"], a["L0_ffn_w1"]], 0)
    w3 = np.concatenate([a["L0_ffn_sw3"], a["L0_ffn_w3"]], 0)
    w2 = np.concatenate([a["L0_ffn_sw2"], a["L0_ffn_w2"]], 0)
    arrays = {
        "x": a["L0_attn_x"].reshape(32, 128, 128).transpose(1, 0, 2),
        "alpha": a["L0_attn_alpha"].reshape(1, 1),
        "w_qkv0": np.concatenate([a["L0_attn_Wq"], a["L0_attn_Wk"], a["L0_attn_Wv"]], 1),
        "bias_rows0": np.stack([a["L0_attn_bq"], a["L0_attn_bk"], a["L0_attn_bv"], a["L0_attn_bfc"]], 0),
        "wo0": a["L0_attn_W_o"],
        "wo0_t": a["L0_attn_W_o"].transpose(0, 2, 1),
        "wfc0": a["L0_attn_Wfc"],
        "router0": a["L0_ffn_router_w"].T,
        "expert_bias": a["L0_ffn_expert_bias"].reshape(1, 8),
        "up0": up_pair(w1, w3),
        "down0": w2.reshape(10, 128, 2, 128).transpose(3, 0, 2, 1),
        "w_qkv1": np.concatenate([a["L1_attn_Wq"].T, a["L1_attn_Wk"].T, a["L1_attn_Wv"].T], 1),
        "wo1": a["L1_attn_Wo"].T,
        "router1": a["L1_ffn_w_g"].T,
        "up1": a["L1_ffn_c_fc"].transpose(1, 0, 2).reshape(128, -1),
        "down1": a["L1_ffn_c_proj"].reshape(8, 4, 128, 128).transpose(2, 0, 1, 3),
    }
    nc = bacc.Bacc("TRN2", target_bir_lowering=False, num_devices=1)
    feed, args = {}, []
    for name, v in arrays.items():
        v = np.ascontiguousarray(v)
        feed[f"in_{name}"] = v
        args.append(nc.dram_tensor(f"in_{name}", v.shape, mybir.dt.from_np(v.dtype), kind="ExternalInput").ap())
    out = nc.dram_tensor("out_x", (128, 32, 128), mybir.dt.float32, kind="ExternalOutput").ap()
    macaron(nc, *args, out, stop_after=stop_after)
    r = run_bass_kernel_spmd(nc, [feed], core_ids=[0])
    return r.results[0]["out_x"].transpose(1, 0, 2).reshape(8, 512, 128)
```

```python
from contextlib import ExitStack

import concourse.bass as bass
from concourse import mybir

ALU = mybir.AluOpType
ACT = mybir.ActivationFunctionType
AX = mybir.AxisListType
F32 = mybir.dt.float32
F32R = mybir.dt.float32r
BF16 = mybir.dt.bfloat16
I32 = mybir.dt.int32

P = 128
B, S, D = 8, 512, 128
TOK = B * S
TPC = S // P
TILES = TOK // P
H, HD = 16, 8
E = 8
NSH = 2
HID0, HID1 = 256, 512
HB0, HB1 = HID0 // P, HID1 // P
U0, U1 = NSH + E, E
CAP = int(1.25 * TOK * 2 / E)
EPS = 1e-5
NEG = -1e30
WIN = 2 * P
HALO = 64
INV_SQRT = 1.0 / float(HD) ** 0.5
CLAMP = 2e6
FAR = float(2 ** 21)


def macaron(nc, x, alpha, w_qkv0, bias_rows0, wo0, wo0_t, wfc0, router0, expert_bias, up0, down0,
            w_qkv1, wo1, router1, up1, down1, out, stop_after=99):
    ctx = ExitStack()
    with ctx:
        def sb(name, shape, dt=F32, stack=ctx):
            return stack.enter_context(nc.sbuf_tensor(name, shape, dt))

        def sem(name):
            return ctx.enter_context(nc.semaphore(name))

        ps = ctx.enter_context(nc.psum_tensor("ps", [P, 8, 512], F32))

        X = sb("X", [P, TILES, D])
        XT = sb("XT", [P, TOK])
        up1_hi = sb("up1_hi", [P, U1, HID1], F32R)
        up1_lo = sb("up1_lo", [P, U1, HID1], F32R)
        dn1 = sb("dn1", [P, U1, HB1, D])
        ident = sb("ident", [P, P])
        ident_b = sb("ident_b", [P, P], BF16)
        before = sb("before", [P, P], BF16)
        ones_b = sb("ones_b", [P, P], BF16)
        ones_f = sb("ones_f", [P, P])
        half_neg = sb("half_neg", [P, TPC])
        rw = [sb("rw0", [P, E]), sb("rw1", [P, E])]
        ebias = sb("ebias", [P, 2, E])
        logits = sb("logits", [P, TILES, E])
        cw = sb("cw", [P, TILES, E])
        cw_c = sb("cw_c", [P, TPC, E])
        bn = sb("bn", [P, TPC, 6])
        mv = sb("mv", [P, TPC, 2])
        var_eps = sb("var_eps", [P, TPC])
        rstd = sb("rstd", [P, TPC])
        xn = sb("xn", [P, TPC, D])
        xT_c = sb("xT_c", [P, S])
        alpha_s = sb("alpha_s", [P, 1])
        col = sb("col", [P, 24])

        load = {k: sem(f"load_{k}") for k in ("x", "up0", "up1", "rest", "small", "up1_again", "dn1")}
        up1_top, up1_split = sem("up1_top"), sem("up1_split")
        staged_free = sem("staged_free")
        consts_ready = sem("consts_ready")
        bar = sem("phase_barrier")
        stored = sem("stored")
        step = sem("route_step")

        names = ["P", "F0a", "A0", "F0b", "F1a", "A1", "F1b"]
        sems = {}
        for n in names:
            kinds = ["tr_done", "xt_copied", "lg_done", "lg_copied", "var_ready", "rstd_ready", "xn_ready"]
            if n[0] == "F":
                kinds += ["xs_free", "split_done", "up_done", "act_done", "h_ready", "dn_done", "acc_done"]
            if n[0] == "A":
                kinds += ["xs_ready", "pj_done", "asm_done", "qk_tr", "q_copied", "k_copied", "ot_copied", "on_tr",
                          "on_ready", "oT_tr", "oT_ready", "o_done", "x_added"]
            if n == "A0":
                kinds += ["sc_done", "unit_begun", "m_ready", "exp_done", "pt_done", "pa_copied", "pb_copied", "pv_done"]
            if n == "A1":
                kinds += ["turned_vector", "turned_scalar", "v_ready", "g_done", "dp_vector", "dp_scalar", "u_ready", "y_ready", "s_ready",
                          "t_ready", "y_exp", "pvh_done"]
            sems[n] = {k: sem(f"{n}_{k}") for k in kinds}

        ENGINES = 4

        def barrier(eng, k):
            eng.drain().then_inc(bar, 1)
            eng.wait_ge(bar, ENGINES * (k + 1))

        def tiles_of(c):
            return X[:, bass.ds(TPC * c, TPC), :]

        def norm_stats_vector(eng, s, i, c):
            eng.drain()
            for t in range(TPC):
                eng.bn_stats(bn[:, t, :], X[:, bass.ds(TPC * c + t, 1), :].rearrange("p a d -> p (a d)"))
            eng.drain()
            for t in range(TPC):
                eng.bn_aggr(mv[:, t, :], bn[:, t, :])
            eng.drain()
            eng.tensor_scalar(var_eps[:, :], mv[:, :, 1], EPS, None, ALU.add).then_inc(s["var_ready"], 1)

        def norm_apply_vector(eng, s, i, c):
            eng.wait_ge(s["rstd_ready"], i + 1)
            eng.wait_ge(s["tr_done"], i + 1)
            for t in range(TPC):
                last = eng.tensor_scalar(xn[:, t, :], X[:, bass.ds(TPC * c + t, 1), :].rearrange("p a d -> p (a d)"),
                                         mv[:, t, 0:1], rstd[:, t:t + 1], ALU.subtract, ALU.mult)
            last.then_inc(s["xn_ready"], 1)

        def norm_logits_vector(eng, s, i, c, lay):
            eng.wait_ge(s["lg_done"], i + 1)
            lg = ps[:, 7, 0:TPC * E].rearrange("p (t e) -> p t e", e=E)
            dst = logits[:, bass.ds(TPC * c, TPC), :]
            eng.tensor_tensor(dst, lg, ebias[:, lay, :].unsqueeze(1).to_broadcast([P, TPC, E]),
                              ALU.add).then_inc(s["lg_copied"], 1)

        def norm_gpsimd(eng, s, i):
            eng.wait_ge(s["var_ready"], i + 1)
            eng.tensor_tensor(rstd[:, :], var_eps[:, :], half_neg[:, :], ALU.pow).then_inc(s["rstd_ready"], 1)

        def norm_turn_tensor(eng, s, i, bank=6):
            eng.wait_ge(s["xn_ready"], i + 1)
            eng.wait_ge(s["xt_copied"], 2 * i + 2)
            for t in range(TPC):
                last = eng.transpose(ps[:, bank, t * P:(t + 1) * P], xn[:, t, :], ident[:, :])
            last.then_inc(s["tr_done"], 1)

        def norm_logits_tensor(eng, s, i, lay):
            eng.wait_ge(s["xt_copied"], 2 * i + 4)
            eng.wait_ge(s["lg_copied"], i + 1)
            for t in range(TPC):
                last = eng.matmul(ps[:, 7, t * E:(t + 1) * E], xT_c[:, t * P:(t + 1) * P], rw[lay][:, :],
                                  start=True, stop=True)
            last.then_inc(s["lg_done"], 1)

        def norm_scalar(eng, s, i, c, lay, bank=6):
            eng.wait_ge(s["tr_done"], i + 2)
            if lay is not None:
                eng.wait_ge(s["lg_copied"], i + 1)
            eng.activation(xT_c[:, :], ps[:, bank, :], ACT.Copy).then_inc(s["xt_copied"], 1)
            eng.activation(XT[:, bass.ds(c * S, S)], ps[:, bank, :], ACT.Copy).then_inc(s["xt_copied"], 1)

        def norm_credits_tensor(eng, s):
            eng.sem_inc(s["tr_done"], 1)

        def norm_credits_scalar(eng, s):
            eng.sem_inc(s["xt_copied"], 2)

        def norm_credits_vector(eng, s, lay):
            if lay is not None:
                eng.sem_inc(s["lg_copied"], 1)

        def norm_vector(eng, s, i, c, lay):
            norm_stats_vector(eng, s, i, c)
            norm_apply_vector(eng, s, i, c)
            if lay is not None:
                norm_logits_vector(eng, s, i, c, lay)

        def norm_tensor(eng, s, i, lay):
            norm_turn_tensor(eng, s, i)
            if lay is not None:
                norm_logits_tensor(eng, s, i, lay)

        def last_chunk(c):
            return (c + (B - 1)) % B

        def ffn_shape(lay):
            return (U0, HB0, 2, 2) if lay == 0 else (U1, HB1, 1, 4)

        def split_gpsimd(eng, s, XS, i, c):
            eng.wait_ge(s["xs_free"], i + 1)
            hi = XS[:, bass.ds((i % 2) * 2 * S, S)]
            lo = XS[:, bass.ds((i % 2) * 2 * S + S, S)]
            xt = XT[:, bass.ds(c * S, S)]
            eng.tensor_copy(hi, xt)
            eng.drain()
            eng.tensor_tensor(lo, xt, hi.bitcast(F32), ALU.subtract).then_inc(s["split_done"], 1)

        def ffn_tensor(eng, s, lay, XS, hT, w_hi, w_lo, dn, nxt):
            U, HB, G, RING = ffn_shape(lay)
            free = s["h_ready"] if lay == 0 else s["act_done"]
            norm_credits_tensor(eng, s)
            eng.sem_inc(s["dn_done"], 2)
            eng.sem_inc(s["xs_free"], 2)
            with eng.Fori(0, B) as c:
                eng.wait_ge(s["split_done"], c + 1)
                xh = XS[:, bass.ds((c % 2) * 2 * S, S)]
                xl = XS[:, bass.ds((c % 2) * 2 * S + S, S)]
                for e in range(U + 1):
                    if e < U:
                        for hb in range(HB):
                            j = e * HB + hb
                            eng.wait_ge(free, c * (U * HB) + j + 1)
                            for g in range(G):
                                bank = (j * G + g) % 4
                                cols = slice((hb * G + g) * P, (hb * G + g + 1) * P)
                                eng.matmul(ps[:, bank, :], w_lo[:, e, cols], xh, start=True, stop=False)
                                eng.matmul(ps[:, bank, :], w_hi[:, e, cols], xl, start=False, stop=False)
                                last = eng.matmul(ps[:, bank, :], w_hi[:, e, cols], xh, start=False, stop=True)
                            last.then_inc(s["up_done"], 1)
                    if e > 0:
                        d = e - 1
                        eng.wait_ge(s["h_ready"], c * (U * HB) + (d + 1) * HB + RING)
                        eng.wait_ge(s["acc_done"], c * U + d + 1)
                        for t in range(TPC):
                            for hb in range(HB):
                                last = eng.matmul(ps[:, 4 + d % 2, t * P:(t + 1) * P],
                                                  hT[:, d % 2, hb, t * P:(t + 1) * P], dn[:, d, hb, :],
                                                  start=(hb == 0), stop=(hb == HB - 1))
                                if e == U - 1 and t == 0 and hb == 0:
                                    last.then_inc(s["xs_free"], 1)
                        last.then_inc(s["dn_done"], 1)
                    if nxt != "end":
                        if e == 3:
                            norm_turn_tensor(eng, s, c)
                        if e == 5 and nxt is not None:
                            norm_logits_tensor(eng, s, c, nxt)
            if nxt != "end":
                norm_tensor(eng, s, B, nxt)

        def ffn_scalar(eng, s, lay, act_out, nxt):
            U, HB, G, RING = ffn_shape(lay)
            norm_credits_scalar(eng, s)
            if lay == 1:
                eng.sem_inc(s["act_done"], RING)
            eng.preload_act_table(ACT.Silu)
            with eng.Fori(0, B) as c:
                for j in range(U * HB):
                    n = c * (U * HB) + j
                    eng.wait_ge(s["up_done"], n + 1)
                    eng.wait_ge(s["h_ready"], n + 1)
                    eng.activation(act_out[:, j % RING, :], ps[:, (j * G) % 4, :],
                                   ACT.Silu if lay == 0 else ACT.Relu).then_inc(s["act_done"], 1)
                    if nxt != "end" and j == 5 * HB - 1:
                        norm_scalar(eng, s, c, last_chunk(c), nxt)
            if nxt != "end":
                norm_scalar(eng, s, B, B - 1, nxt)

        def ffn_vector(eng, s, lay, act_out, hT, acc, nxt):
            U, HB, G, RING = ffn_shape(lay)
            if nxt != "end":
                norm_credits_vector(eng, s, nxt)
            eng.sem_inc(s["h_ready"], RING)
            eng.sem_inc(s["acc_done"], 2)
            more = RING if lay == 1 else 0
            with eng.Fori(0, B) as c:
                eng.drain()
                eng.tensor_copy(cw_c[:, :, :], cw[:, bass.ds(TPC * c, TPC), :])
                for e in range(U + 1):
                    if e < U:
                        eng.wait_ge(s["dn_done"], c * U + e + 1)
                        for hb in range(HB):
                            j = e * HB + hb
                            eng.wait_ge(s["act_done"], c * (U * HB) + j + 1 + more)
                            a = act_out[:, j % RING, :]
                            b = ps[:, (j * G + 1) % 4, :] if lay == 0 else a
                            eng.tensor_tensor(hT[:, e % 2, hb, :], a, b, ALU.mult).then_inc(s["h_ready"], 1)
                    if e > 0:
                        d = e - 1
                        eng.drain()
                        eng.wait_ge(s["dn_done"], c * U + d + 3)
                        for t in range(TPC):
                            x_t = X[:, bass.ds(TPC * c + t, 1), :].rearrange("p a d -> p (a d)")
                            routed = d - (U - E)
                            last = eng.scalar_tensor_tensor(
                                out=x_t if d == U - 1 else acc[:, t, :],
                                in0=ps[:, 4 + d % 2, t * P:(t + 1) * P],
                                scalar=cw_c[:, t, routed:routed + 1] if routed >= 0 else 0.5,
                                in1=x_t if d == 0 else acc[:, t, :], op0=ALU.mult, op1=ALU.add)
                        last.then_inc(s["acc_done"], 1)
                    if nxt != "end":
                        if e == 0:
                            norm_stats_vector(eng, s, c, last_chunk(c))
                        if e == 2:
                            norm_apply_vector(eng, s, c, last_chunk(c))
                        if e == 6 and nxt is not None:
                            norm_logits_vector(eng, s, c, last_chunk(c), nxt)
            if nxt != "end":
                norm_vector(eng, s, B, B - 1, nxt)

        def ffn_gpsimd(eng, s, XS, nxt):
            split_gpsimd(eng, s, XS, 0, 0)
            with eng.Fori(0, B) as c:
                if nxt != "end":
                    norm_gpsimd(eng, s, c)
                split_gpsimd(eng, s, XS, c + 1, (c + 1) % B)
            if nxt != "end":
                norm_gpsimd(eng, s, B)

        def route_vector(eng, buf, n, lay):
            work, oh, oh_b, m, ex, pr, rank, tot, cum, incr = buf

            def be(a):
                return a.unsqueeze(2).to_broadcast([P, TILES, E])

            src = logits
            for k in range(2):
                eng.tensor_reduce(m[:, k, :], src[:, :, :], AX.X, ALU.max)
                eng.drain()
                eng.tensor_tensor(work[:, 0], src[:, :, :], be(m[:, k, :]), ALU.is_equal)
                eng.drain()
                eng.tensor_tensor(work[:, 1], work[:, 0], incr[:, :].unsqueeze(1).to_broadcast([P, TILES, E]), ALU.mult)
                eng.drain()
                eng.tensor_reduce(m[:, 2, :], work[:, 1], AX.X, ALU.max)
                eng.drain()
                eng.tensor_tensor(oh[:, k], work[:, 1], be(m[:, 2, :]), ALU.is_equal)
                eng.drain()
                if k == 0:
                    eng.scalar_tensor_tensor(out=work[:, 2].rearrange("p t e -> p (t e)"),
                                             in0=oh[:, 0].rearrange("p t e -> p (t e)"), scalar=NEG,
                                             in1=logits[:, :, :].rearrange("p t e -> p (t e)"),
                                             op0=ALU.mult, op1=ALU.add)
                    eng.drain()
                    src = work[:, 2]
            eng.tensor_tensor(ex[:, 0, :], m[:, 1, :], m[:, 0, :], ALU.subtract).then_inc(step, 1)
            for k in range(2):
                eng.tensor_copy(oh_b[:, k].rearrange("p e t -> p t e"), oh[:, k])
            eng.drain().then_inc(step, 1)
            eng.wait_ge(step, n + 3)
            eng.tensor_scalar(ex[:, 2, :], ex[:, 1, :], 1.0, None, ALU.add)
            eng.drain()
            eng.reciprocal(pr[:, 0, :], ex[:, 2, :])
            eng.drain()
            eng.tensor_tensor(pr[:, 1, :], ex[:, 1, :], pr[:, 0, :], ALU.mult)
            eng.drain()
            if lay == 1:
                eng.wait_ge(step, n + 4)
                w3 = ps[:, 0, :].rearrange("p (k e t) -> p k e t", k=2, e=E)
                t3 = ps[:, 1, :].rearrange("p (k e t) -> p k e t", k=2, e=E)
                for k in range(2):
                    eng.tensor_copy(tot[:, :, k, :], t3[:, k])
                eng.drain()
                for e in range(E):
                    eng.tensor_tensor_scan(cum[:, e, :], ones_f[:, 0:2 * TILES], tot[:, e].rearrange("p k t -> p (k t)"),
                                           0.0, ALU.mult, ALU.add)
                eng.drain()
                eng.tensor_tensor(cum[:, :, :], cum[:, :, :], tot[:, :, :, :].rearrange("p e k t -> p e (k t)"),
                                  ALU.subtract)
                eng.drain()
                for k in range(2):
                    eng.tensor_tensor(rank[:, k], cum[:, :, k * TILES:(k + 1) * TILES].rearrange("p e t -> p t e"),
                                      w3[:, k].rearrange("p e t -> p t e"), ALU.add)
                eng.drain()
                for k in range(2):
                    eng.scalar_tensor_tensor(out=oh[:, k].rearrange("p t e -> p (t e)"),
                                             in0=rank[:, k].rearrange("p t e -> p (t e)"), scalar=float(CAP),
                                             in1=oh[:, k].rearrange("p t e -> p (t e)"), op0=ALU.is_lt, op1=ALU.mult)
                eng.drain()
            for k in range(2):
                eng.tensor_tensor(work[:, k], oh[:, k], be(pr[:, k, :]), ALU.mult)
            eng.drain()
            eng.tensor_tensor(work[:, 2], work[:, 0], work[:, 1], ALU.add)
            eng.drain()
            eng.tensor_scalar(cw[:, :, :], work[:, 2], 0.5, None, ALU.mult)

        def route_scalar(eng, buf, n):
            ex = buf[4]
            eng.wait_ge(step, n + 2)
            eng.activation(ex[:, 1, :], ex[:, 0, :], ACT.Exp).then_inc(step, 1)

        def route_tensor(eng, buf, n, lay):
            oh_b = buf[2]
            if lay == 1:
                eng.wait_ge(step, n + 3)
                rhs = oh_b[:, :, :, :].rearrange("p k e t -> p (k e t)")
                eng.matmul(ps[:, 0, :], before[:, :], rhs, start=True, stop=True)
                eng.matmul(ps[:, 1, :], ones_b[:, :], rhs, start=True, stop=True).then_inc(step, 1)

        ROUTE_STEPS = [3, 4]

        def route_buffers(stack, phase):
            def b(name, shape, dt=F32):
                return sb(f"{phase}_{name}", shape, dt, stack)
            return [b("r_work", [P, 3, TILES, E]), b("r_oh", [P, 2, TILES, E]), b("r_ohb", [P, 2, E, TILES], BF16),
                    b("r_m", [P, 3, TILES]), b("r_ex", [P, 3, TILES]), b("r_pr", [P, 2, TILES]),
                    b("r_rank", [P, 2, TILES, E]), b("r_tot", [P, E, 2, TILES]), b("r_cum", [P, E, 2 * TILES]), incr]

        out_w1 = sb("out_w1", [P, D])
        qkv_w1_s = sb("qkv_w1_s", [P, 3 * D])
        incr = sb("incr", [P, E])

        def run(name, body):
            with nc.Block() as block:
                body(block)

        def project_tensor(eng, s, c, lay, xa):
            eng.wait_ge(s["xs_ready"], c + 1)
            for t in range(TPC):
                last = eng.matmul(ps[:, t, 0:3 * D], xa[:, t * P:(t + 1) * P], qkv_w[lay][:, :],
                                  start=True, stop=True)
            last.then_inc(s["pj_done"], 1)

        def tail_tensor(eng, s, c, lay, OT, on, oT):
            eng.wait_ge(s["ot_copied"], (c + 1) * 4)
            for t in range(TPC):
                for g in range(4):
                    last = eng.transpose(ps[:, t, g * P:(g + 1) * P], OT[:, t, g * P:(g + 1) * P], ident[:, :])
            last.then_inc(s["on_tr"], 1)
            eng.wait_ge(s["on_ready"], c + 1)
            for t in range(TPC):
                last = eng.transpose(ps[:, 4, t * P:(t + 1) * P], on[:, t * P:(t + 1) * P], ident[:, :])
            last.then_inc(s["oT_tr"], 1)
            eng.wait_ge(s["oT_ready"], c + 1)
            for t in range(TPC):
                last = eng.matmul(ps[:, 5, t * P:(t + 1) * P], oT[:, t * P:(t + 1) * P], out_w[lay][:, :],
                                  start=True, stop=True)
            last.then_inc(s["o_done"], 1)

        def tail_scalar(eng, s, c, oT):
            eng.wait_ge(s["oT_tr"], c + 1)
            eng.activation(oT[:, :], ps[:, 4, :], ACT.Copy).then_inc(s["oT_ready"], 1)

        def tail_vector(eng, s, c, lay, on, rden):
            eng.wait_ge(s["on_tr"], c + 1)
            v = ps[:, 0:4, :].rearrange("p t (h r) -> p (t h) r", r=32)
            eng.reciprocal(rden[:, :], v[:, :, HD])
            eng.drain()
            eng.tensor_tensor(on[:, :].rearrange("p (h d) -> p h d", d=HD), v[:, :, 0:HD],
                              rden[:, :].unsqueeze(2).to_broadcast([P, TPC * H, HD]), ALU.mult)\
                .then_inc(s["on_ready"], 1)
            x_c = tiles_of(c)
            if lay == 0:
                eng.tensor_tensor(x_c, x_c, bfc[:, :].unsqueeze(1).to_broadcast([P, TPC, D]), ALU.add)
            eng.drain()
            eng.wait_ge(s["o_done"], c + 1)
            eng.tensor_tensor(x_c, x_c, ps[:, 5, :].rearrange("p (t d) -> p t d", d=D), ALU.add).then_inc(s["x_added"], 1)

        r0 = ExitStack()
        bq_s, bk, bv, bfc = (sb(n, [P, D], F32, r0) for n in ("bq_s", "bk", "bv", "bfc"))
        qkv_w = [sb("qkv_w0_s", [P, 3 * D], F32, r0), qkv_w1_s]
        out_w = [sb("out_w0", [P, D], F32, r0), out_w1]
        up0_hi = sb("up0_hi", [P, U0, 2 * HID0], F32R, r0)
        up0_lo = sb("up0_lo", [P, U0, 2 * HID0], F32R, r0)
        dn0 = sb("dn0", [P, U0, HB0, D], F32, r0)

        with ExitStack() as st:
            stage = sb("stage", [P, U0 * 2 * HID0], F32, st)
            stage1 = sb("stage1", [P, U1 * HID1], F32, st)
            wfc = sb("wfc", [P, D], F32, st)
            wo_t = sb("wo_t", [P, P], F32, st)
            iota_i = sb("iota_i", [P, E], I32, st)

            def body(block):
                s = sems["P"]

                @block.sync
                def _(eng):
                    eng.dma_start(X[:, :, :], x).then_inc(load["x"], 16)
                    for dst, src in ((rw[0], router0), (rw[1], router1), (wfc, wfc0), (qkv_w[0], w_qkv0),
                                     (qkv_w[1], w_qkv1), (out_w[1], wo1)):
                        eng.dma_start(dst[:, :], src).then_inc(load["small"], 16)
                    eng.dma_start(ebias[:, 0, :], expert_bias.to_broadcast([P, E])).then_inc(load["small"], 16)
                    eng.dma_start(alpha_s[:, :], alpha.to_broadcast([P, 1])).then_inc(load["small"], 16)
                    for n, dst in enumerate((bq_s, bk, bv, bfc)):
                        eng.dma_start(dst[:, :], bias_rows0[n:n + 1, :].to_broadcast([P, D])).then_inc(load["small"], 16)
                    eng.wait_ge(consts_ready, 1)
                    for h in range(H):
                        eng.dma_start(wo_t[h * HD:(h + 1) * HD, h * HD:(h + 1) * HD], wo0_t[h]).then_inc(load["small"], 16)
                    eng.dma_start(stage[:, :], up0).then_inc(load["up0"], 16)
                    eng.dma_start(dn0[:, :, :, :], down0).then_inc(load["rest"], 16)
                    eng.dma_start(stage1[:, :], up1).then_inc(load["up1"], 16)

                @block.gpsimd
                def _(eng):
                    eng.memset(wo_t[:, :], 0.0)
                    eng.drain().then_inc(consts_ready, 1)
                    eng.memset(ident[:, :], 0.0)
                    eng.memset(ones_f[:, :], 1.0)
                    eng.memset(ones_b[:, :], 1.0)
                    eng.memset(half_neg[:, :], -0.5)
                    eng.memset(ebias[:, 1, :], 0.0)
                    eng.iota(iota_i[:, :], pattern=[[-1, E]], base=E, channel_multiplier=0)
                    eng.drain()
                    eng.affine_select(out=ident[:, :], in_=ident[:, :], compare_op=ALU.not_equal, fill=1.0, base=0,
                                      pattern=[[-1, P]], channel_multiplier=1)
                    eng.affine_select(out=before[:, :], in_=ones_b[:, :], compare_op=ALU.is_gt, fill=0.0, base=0,
                                      pattern=[[1, P]], channel_multiplier=-1)
                    eng.drain()
                    eng.tensor_copy(ident_b[:, :], ident[:, :])
                    eng.tensor_copy(incr[:, :], iota_i[:, :])
                    eng.drain().then_inc(consts_ready, 1)
                    with eng.Fori(0, B) as c:
                        norm_gpsimd(eng, s, c)
                    eng.wait_ge(load["up1"], 16)
                    eng.tensor_copy(up1_hi[:, :, :].rearrange("p u n -> p (u n)"), stage1[:, :])
                    eng.drain()
                    eng.tensor_tensor(up1_lo[:, :, :].rearrange("p u n -> p (u n)"), stage1[:, :],
                                      up1_hi[:, :, :].rearrange("p u n -> p (u n)").bitcast(F32), ALU.subtract)
                    barrier(eng, 0)

                @block.tensor
                def _(eng):
                    norm_credits_tensor(eng, s)
                    eng.wait_ge(consts_ready, 2)
                    eng.wait_ge(load["small"], 16 * (12 + H))
                    with eng.Fori(0, B) as c:
                        norm_tensor(eng, s, c, 0)
                    eng.matmul(ps[:, 0, 0:D], wo_t[:, :], wfc[:, :], start=True, stop=True).then_inc(step, 1)
                    barrier(eng, 0)

                @block.scalar
                def _(eng):
                    norm_credits_scalar(eng, s)
                    with eng.Fori(0, B) as c:
                        norm_scalar(eng, s, c, c, 0)
                    eng.wait_ge(step, 1)
                    eng.activation(out_w[0][:, :], ps[:, 0, 0:D], ACT.Copy)
                    barrier(eng, 0)

                @block.vector
                def _(eng):
                    norm_credits_vector(eng, s, 0)
                    eng.wait_ge(load["x"], 16)
                    eng.wait_ge(load["small"], 16 * (12 + H))
                    with eng.Fori(0, B) as c:
                        norm_vector(eng, s, c, c, 0)
                    eng.tensor_scalar(bq_s[:, :], bq_s[:, :], INV_SQRT, None, ALU.mult)
                    eng.wait_ge(load["up0"], 16)
                    eng.tensor_copy(up0_hi[:, :, :].rearrange("p u n -> p (u n)"), stage[:, :])
                    eng.drain()
                    eng.tensor_tensor(up0_lo[:, :, :].rearrange("p u n -> p (u n)"), stage[:, :],
                                      up0_hi[:, :, :].rearrange("p u n -> p (u n)").bitcast(F32), ALU.subtract)
                    eng.wait_ge(load["rest"], 16)
                    barrier(eng, 0)

            run("P", body)

        state = {"step": 1, "bar": 1}

        def ffn_phase(name, lay, nxt):
            s = sems[name]
            n0, b0 = state["step"], state["bar"]
            state["step"] += ROUTE_STEPS[lay]
            state["bar"] += 1
            U, HB, G, RING = ffn_shape(lay)
            w_hi, w_lo, dn = (up0_hi, up0_lo, dn0) if lay == 0 else (up1_hi, up1_lo, dn1)
            with ExitStack() as st:
                XS = sb(f"{name}_xs", [P, 2 * 2 * S], F32R, st)
                act_out = sb(f"{name}_act", [P, RING, S], F32, st)
                acc = sb(f"{name}_acc", [P, TPC, D], F32, st)
                hT = sb(f"{name}_hT", [P, 2, HB, S], F32, st)
                with ExitStack() as st2:
                    buf = route_buffers(st2, name)
                    route_done = sem(f"{name}_route_done")

                    def body_r(block):
                        if name == "F1a":
                            @block.sync
                            def _(eng):
                                eng.wait_ge(bar, ENGINES * b0)
                                eng.dma_start(dn1[:, :, :, :], down1).then_inc(load["dn1"], 16)

                        if name == "F1b":
                            w_raw = sb("F1b_up1", [P, U1 * HID1], F32, st2)
                            w_top, w_rest = (a[:, :, :].rearrange("p u n -> p (u n)") for a in (up1_hi, up1_lo))

                            @block.sync
                            def _(eng):
                                eng.wait_ge(bar, ENGINES * b0)
                                eng.dma_start(w_raw[:, :], up1).then_inc(load["up1_again"], 16)
                                eng.dma_start(dn1[:, :, :, :], down1).then_inc(load["dn1"], 16)

                            @block.gpsimd
                            def _(eng):
                                eng.wait_ge(up1_top, 1)
                                eng.tensor_tensor(w_rest, w_raw[:, :], w_top.bitcast(F32),
                                                  ALU.subtract).then_inc(up1_split, 1)

                        @block.vector
                        def _(eng):
                            route_vector(eng, buf, n0, lay)
                            eng.drain().then_inc(route_done, 1)
                            eng.wait_ge(route_done, 3)

                        @block.scalar
                        def _(eng):
                            route_scalar(eng, buf, n0)
                            if name == "F1b":
                                eng.wait_ge(load["up1_again"], 16)
                                eng.activation(w_top, w_raw[:, :], ACT.Copy).then_inc(up1_top, 1)
                            eng.drain().then_inc(route_done, 1)
                            eng.wait_ge(route_done, 3)

                        @block.tensor
                        def _(eng):
                            route_tensor(eng, buf, n0, lay)
                            if name == "F1a":
                                eng.wait_ge(load["dn1"], 16)
                            if name == "F1b":
                                eng.wait_ge(load["dn1"], 32)
                                eng.wait_ge(up1_split, 1)
                            eng.drain().then_inc(route_done, 1)
                            eng.wait_ge(route_done, 3)

                    run(name, body_r)

                def body(block):
                    @block.tensor
                    def _(eng):
                        ffn_tensor(eng, s, lay, XS, hT, w_hi, w_lo, dn, nxt)
                        barrier(eng, b0)

                    @block.scalar
                    def _(eng):
                        ffn_scalar(eng, s, lay, act_out, nxt)
                        barrier(eng, b0)

                    @block.vector
                    def _(eng):
                        ffn_vector(eng, s, lay, act_out, hT, acc, nxt)
                        barrier(eng, b0)

                    @block.gpsimd
                    def _(eng):
                        ffn_gpsimd(eng, s, XS, nxt)
                        barrier(eng, b0)

                run(name, body)

        def window(t):
            lo, hi = max(0, t * P - HALO), min(S, t * P - HALO + WIN)
            return lo, hi, lo - (t * P - HALO), hi - (t * P - HALO)

        def unit_head(u, r, b):
            return 2 * (u // 2) + r, 2 * (u % 2) + b

        def bank_of(t, side):
            return ((0, 1), (4, 5))[t % 2][side]

        def attn0():
            name, lay, nxt = "A0", 0, 0
            UNITS = 4 * TPC
            MR, PR = 3, 4
            VB = TPC + 1
            s = sems[name]
            b0, n0 = state["bar"], state["step"]
            state["bar"] += 1
            state["step"] += 5
            with ExitStack() as st:
                def ab(n, shape, dt=F32):
                    return sb(f"{name}_{n}", shape, dt, st)
                QA = ab("QA", [P, TPC, H, 32], F32R)
                KA = ab("KA", [P, TPC, H, 32], F32R)
                VA = ab("VA", [P, VB, H, 32])
                QT = ab("QT", [P, 4, S], F32R)
                KT = ab("KT", [P, 4, S], F32R)
                M = ab("M", [P, MR, 2, 2, WIN])
                OT = ab("OT", [P, TPC, S])
                nmax = ab("nmax", [P, MR, 2, 2])
                rden = ab("rden", [P, TPC * H])
                PT = dn1[:, :, :, :].rearrange("p u b d -> p (u b d)").rearrange("p (n k q) -> p n k q", n=PR, k=2)
                qs = M[:, 0].rearrange("p b r w -> p (b r w)").rearrange("p (a t d) -> p a t d", a=2, t=TPC)
                xa = M[:, 1, 0].rearrange("p r w -> p (r w)")
                on = M[:, 1, 1].rearrange("p r w -> p (r w)")
                oT = M[:, 2, 0].rearrange("p r w -> p (r w)")
                dist = OT[:, 0:2, :].rearrange("p a q -> p (a q)").rearrange("p (a w) -> p a w", w=WIN)
                dist_i = OT[:, 2, 0:WIN].bitcast(I32)
                mask = ab("mask", [P, WIN])
                pad_ready = sem("A0_pad_ready")

                def blocks(t):
                    _, _, w0, w1 = window(t)
                    return (w0, P), (P, w1)

                def copy_turned(eng, c, n, k, done):
                    k0, k1 = blocks(n // 4)[k]
                    eng.wait_ge(s["pt_done"], c * UNITS + n + 1)
                    if n >= PR:
                        eng.wait_ge(s["pv_done"], c * (UNITS // 2) + (n - PR) // 2 + 1)
                    dst, src = PT[0:k1 - k0, n % PR, k, :], ps[0:k1 - k0, 4 + k, :]
                    if k == 0:
                        eng.activation(dst, src, ACT.Copy).then_inc(done, 1)
                    else:
                        eng.tensor_copy(dst, src).then_inc(done, 1)

                def copy_out(eng, c, t):
                    eng.wait_ge(s["pv_done"], c * (UNITS // 2) + 2 * t + 2)
                    eng.activation(OT[:, t, :], ps[:, 6 + t % 2, :], ACT.Copy).then_inc(s["ot_copied"], 1)

                def body(block):
                    @block.gpsimd
                    def _(eng):
                        eng.iota(dist_i, pattern=[[1, WIN]], base=-HALO, channel_multiplier=-1)
                        for a in (QA, KA, VA):
                            eng.memset(a[:, :, :, :].rearrange("p t h r -> p (t h r)").bitcast(F32), 0.0)
                        eng.memset(PT.rearrange("p n k q -> p (n k q)"), 0.0)
                        eng.drain()
                        eng.memset(VA[:, :, :, HD:HD + 1], 1.0)
                        eng.drain()
                        eng.memset(VA[HALO:P, 0:VB:VB - 1, :, HD:HD + 1], 0.0)
                        eng.drain().then_inc(pad_ready, 1)
                        with eng.Fori(0, B) as c:
                            norm_gpsimd(eng, s, c)
                        norm_gpsimd(eng, s, B)
                        barrier(eng, b0)

                    @block.scalar
                    def _(eng):
                        norm_credits_scalar(eng, s)
                        eng.preload_act_table(ACT.Exp)
                        eng.activation(col[:, 17:18], alpha_s[:, :], ACT.Exp, scale=-1.0).then_inc(step, 1)
                        eng.wait_ge(step, n0 + 3)
                        eng.activation(col[:, 22:23], ps[:, 0, 0:1], ACT.Exp, scale=-1.0).then_inc(step, 1)
                        with eng.Fori(0, B) as c:
                            eng.activation(xa[:, :], XT[:, bass.ds(c * S, S)], ACT.Copy).then_inc(s["xs_ready"], 1)
                            for t in range(TPC):
                                eng.wait_ge(s["qk_tr"], 2 * (c * TPC + t) + 1)
                                eng.activation(QT[:, :, t * P:(t + 1) * P],
                                               ps[:, bank_of(t, 0), :].rearrange("p (g q) -> p g q", g=4),
                                               ACT.Copy).then_inc(s["q_copied"], 1)
                            norm_scalar(eng, s, c, last_chunk(c), nxt)

                            for n in range(UNITS + 2):
                                if n >= 2:
                                    copy_turned(eng, c, n - 2, 0, s["pa_copied"])
                                if n < UNITS:
                                    _, _, w0, w1 = window(n // 4)
                                    eng.wait_ge(s["m_ready"], c * UNITS + n + 1)
                                    for b in range(2):
                                        for r in range(2):
                                            m = M[:, n % MR, b, r, w0:w1]
                                            last = eng.activation(m, m, ACT.Exp, scale=-1.0,
                                                                  bias=nmax[:, n % MR, b, r:r + 1])
                                    last.then_inc(s["exp_done"], 1)
                                if n >= 7 and (n - 7) % 4 == 0:
                                    copy_out(eng, c, (n - 7) // 4)
                            copy_out(eng, c, TPC - 1)
                            tail_scalar(eng, s, c, oT)
                        norm_scalar(eng, s, B, B - 1, nxt)
                        barrier(eng, b0)

                    @block.vector
                    def _(eng):
                        norm_credits_vector(eng, s, nxt)
                        ends = XT[:, :].rearrange("p (b s) -> p b s", b=B)
                        eng.wait_ge(step, n0 + 1)
                        eng.tensor_tensor(col[:, 0:B], ends[:, :, S - 1], ends[:, :, S - 2], ALU.subtract)
                        eng.tensor_scalar(col[:, 18:19], col[:, 17:18], 1.0, None, ALU.add)
                        eng.drain()
                        eng.scalar_tensor_tensor(out=col[:, 8:16], in0=col[:, 0:B], scalar=-1.0, in1=col[:, 0:B],
                                                 op0=ALU.mult, op1=ALU.max)
                        eng.reciprocal(col[:, 19:20], col[:, 18:19])
                        eng.drain()
                        eng.tensor_reduce(col[:, 16:17], col[:, 8:16], AX.X, ALU.add)
                        eng.tensor_scalar(col[:, 20:21], col[:, 19:20], -1.0, 1.0, ALU.mult, ALU.add)
                        eng.drain()
                        eng.tensor_tensor(col[:, 18:19], col[:, 20:21], col[:, 8:9], ALU.mult)
                        eng.tensor_scalar(col[:, 21:22], col[:, 16:17], col[:, 19:20], 1.0 / (B * D), ALU.mult, ALU.mult)
                        eng.drain()
                        eng.scalar_tensor_tensor(out=col[:, 20:21], in0=col[:, 18:19], scalar=ident[:, 0:1],
                                                 in1=col[:, 21:22], op0=ALU.mult, op1=ALU.add)
                        eng.drain().then_inc(step, 1)
                        eng.wait_ge(pad_ready, 1)
                        eng.tensor_copy(dist[:, 0, :], dist_i)
                        eng.drain()
                        eng.scalar_tensor_tensor(out=dist[:, 1, :], in0=dist[:, 0, :], scalar=-1.0, in1=dist[:, 0, :],
                                                 op0=ALU.mult, op1=ALU.max)
                        eng.drain()
                        eng.tensor_scalar(dist[:, 2, :], dist[:, 1, :], 2.0, None, ALU.mult)
                        eng.wait_ge(step, n0 + 4)
                        eng.tensor_scalar(col[:, 18:19], col[:, 22:23], 1.0, None, ALU.add)
                        eng.drain()
                        eng.reciprocal(col[:, 19:20], col[:, 18:19])
                        eng.drain()
                        eng.tensor_scalar(col[:, 21:22], col[:, 19:20], 96.0, 24.0, ALU.mult, ALU.add)
                        eng.drain()
                        eng.tensor_scalar(mask[:, :], dist[:, 2, :], col[:, 21:22], NEG, ALU.is_gt, ALU.mult)
                        eng.drain().then_inc(step, 1)
                        with eng.Fori(0, B) as c:
                            norm_stats_vector(eng, s, c, last_chunk(c))
                            eng.wait_ge(s["pj_done"], c + 1)
                            pj = ps[:, 0:4, :]
                            eng.scalar_tensor_tensor(out=qs[:, 0], in0=pj[:, :, 0:D], scalar=INV_SQRT,
                                                     in1=bq_s[:, :].unsqueeze(1).to_broadcast([P, TPC, D]),
                                                     op0=ALU.mult, op1=ALU.add)
                            eng.tensor_tensor(qs[:, 1], pj[:, :, D:2 * D],
                                              bk[:, :].unsqueeze(1).to_broadcast([P, TPC, D]), ALU.add)
                            for v, m in ((pj[:, 1:TPC, 2 * D:3 * D], VA[:, 1:TPC, :, 0:HD]),
                                         (ps[0:HALO, TPC, 0:2 * D].rearrange("p (t d) -> p t d", d=D),
                                          VA[0:HALO, 0:VB:VB - 1, :, 0:HD])):
                                rows, nb = v.shape[0], v.shape[1]
                                eng.tensor_tensor(m, v.rearrange("p t (h d) -> p t h d", d=HD),
                                                  bv[0:rows, :].rearrange("p (h d) -> p h d", d=HD).unsqueeze(1)
                                                  .to_broadcast([rows, nb, H, HD]), ALU.add)
                            norm_apply_vector(eng, s, c, last_chunk(c))
                            eng.drain()
                            q3 = qs[:, 0].rearrange("p t (h d) -> p (t h) d", d=HD)
                            k3 = qs[:, 1].rearrange("p t (h d) -> p (t h) d", d=HD)
                            qa = QA[:, :, :, :].rearrange("p t h r -> p (t h) r")
                            ka = KA[:, :, :, :].rearrange("p t h r -> p (t h) r")
                            eng.tensor_copy(qa[:, :, 0:HD], q3)
                            eng.tensor_copy(qa[:, :, HD:2 * HD], q3)
                            eng.tensor_copy(ka[:, :, 0:HD], k3)
                            eng.tensor_copy(ka[:, :, 2 * HD:3 * HD], k3)
                            eng.drain()
                            eng.tensor_tensor(qa[:, :, 2 * HD:3 * HD], q3, qa[:, :, 0:HD].bitcast(F32), ALU.subtract)
                            eng.tensor_tensor(ka[:, :, HD:2 * HD], k3, ka[:, :, 0:HD].bitcast(F32), ALU.subtract)
                            eng.drain().then_inc(s["asm_done"], 1)
                            for t in range(TPC):
                                eng.wait_ge(s["qk_tr"], 2 * (c * TPC + t) + 2)
                                eng.tensor_copy(KT[:, :, t * P:(t + 1) * P],
                                                ps[:, bank_of(t, 1), :].rearrange("p (g q) -> p g q", g=4))\
                                    .then_inc(s["k_copied"], 1)
                            norm_logits_vector(eng, s, c, last_chunk(c), nxt)

                            for n in range(UNITS + 2):
                                if n < UNITS:
                                    _, _, w0, w1 = window(n // 4)
                                    eng.wait_ge(s["sc_done"], c * UNITS + n + 1)
                                    if n >= MR:
                                        eng.wait_ge(s["pt_done"], c * UNITS + n - MR + 1)
                                    eng.sem_inc(s["unit_begun"], 1)
                                    for b in range(2):
                                        for r in range(2):
                                            last = eng.tensor_tensor_reduce(
                                                M[:, n % MR, b, r, w0:w1],
                                                ps[:, 2 * (n % 2) + b, r * WIN + w0:r * WIN + w1], mask[:, w0:w1],
                                                -1.0, 3e38, ALU.add, ALU.min, nmax[:, n % MR, b, r:r + 1])
                                    last.then_inc(s["m_ready"], 1)
                                if n >= 2:
                                    copy_turned(eng, c, n - 2, 1, s["pb_copied"])
                            tail_vector(eng, s, c, lay, on, rden)
                        norm_vector(eng, s, B, B - 1, nxt)
                        barrier(eng, b0)

                    @block.tensor
                    def _(eng):
                        norm_credits_tensor(eng, s)
                        eng.wait_ge(step, n0 + 2)
                        eng.matmul(ps[:, 0, 0:1], ones_f[:, :], col[:, 20:21], start=True, stop=True).then_inc(step, 1)
                        eng.wait_ge(step, n0 + 5)
                        eng.wait_ge(pad_ready, 1)

                        def scores(n):
                            t, u = n // 4, n % 4
                            lo, hi, w0, w1 = window(t)
                            for r in range(2):
                                for b in range(2):
                                    g, j = unit_head(u, r, b)
                                    last = eng.matmul(ps[:, 2 * (n % 2) + b, r * WIN + w0:r * WIN + w1],
                                                      QT[32 * j:32 * j + 24, g, t * P:(t + 1) * P],
                                                      KT[32 * j:32 * j + 24, g, lo:hi], start=True, stop=True)
                            return last

                        def turn(n):
                            whole_first = sorted(enumerate(blocks(n // 4)), key=lambda b: b[1][0] - b[1][1])
                            for k, (k0, k1) in whole_first:
                                for b in range(2):
                                    for r in range(2):
                                        i = 2 * b + r
                                        last = eng.transpose(ps[0:k1 - k0, 4 + k, i * P:(i + 1) * P],
                                                             M[:, n % MR, b, r, k0:k1], ident[:, :])
                            return last

                        def outputs(d):
                            t = d // 2
                            for r in range(2):
                                for k in range(2):
                                    for n in (2 * d, 2 * d + 1):
                                        for b in range(2):
                                            g, j = unit_head(n % 4, r, b)
                                            i = 2 * b + r
                                            last = eng.matmul(ps[32 * j:32 * j + 32, 6 + t % 2, g * P:(g + 1) * P],
                                                              VA[:, t + k, 4 * g + j, :],
                                                              PT[:, n % PR, k, i * P:(i + 1) * P], start=(k == 0),
                                                              stop=(k == 1), skip_group_check=True)
                            return last

                        def weigh(eng, c, d):
                            eng.wait_ge(s["pa_copied"], c * UNITS + 2 * d + 2)
                            eng.wait_ge(s["pb_copied"], c * UNITS + 2 * d + 2)
                            if d >= 4 and d % 2 == 0:
                                eng.wait_ge(s["ot_copied"], c * TPC + d // 2 - 1)
                            outputs(d).then_inc(s["pv_done"], 1)

                        with eng.Fori(0, B) as c:
                            eng.wait_ge(s["xs_ready"], c + 1)
                            for t in range(TPC):
                                eng.matmul(ps[:, t, 0:2 * D], xa[:, t * P:(t + 1) * P], qkv_w[lay][:, 0:2 * D],
                                           start=True, stop=True)
                            for m in range(VB):
                                k0, k1 = max(m * P - HALO, 0), min(m * P + HALO, S)
                                dst = ps[:, m, 2 * D:3 * D] if k1 - k0 == P else ps[0:HALO, TPC, (m > 0) * D:(m > 0) * D + D]
                                last = eng.matmul(dst, xa[:, k0:k1], qkv_w[lay][:, 2 * D:3 * D], start=True, stop=True)
                            last.then_inc(s["pj_done"], 1)
                            eng.wait_ge(s["asm_done"], c + 1)
                            for t in range(TPC):
                                for side, src in enumerate((QA, KA)):
                                    for g in range(4):
                                        last = eng.transpose(
                                            ps[:, bank_of(t, side), g * P:(g + 1) * P],
                                            src[:, t, 4 * g:4 * g + 4, :].rearrange("p h r -> p (h r)").bitcast(F32),
                                            ident[:, :])
                                    last.then_inc(s["qk_tr"], 1)
                                if t == 1:
                                    norm_turn_tensor(eng, s, c)
                                    eng.wait_ge(s["q_copied"], c * TPC + 2)
                                    eng.wait_ge(s["k_copied"], c * TPC + 2)
                            norm_logits_tensor(eng, s, c, nxt)
                            eng.wait_ge(s["q_copied"], TPC * (c + 1))
                            eng.wait_ge(s["k_copied"], TPC * (c + 1))
                            for n in range(UNITS + 2):
                                if n < UNITS:
                                    if n >= 2:
                                        eng.wait_ge(s["m_ready"], c * UNITS + n - 1)
                                    scores(n).then_inc(s["sc_done"], 1)
                                if n >= 2:
                                    eng.wait_ge(s["exp_done"], c * UNITS + n - 1)
                                    if n >= 3:
                                        eng.wait_ge(s["pa_copied"], c * UNITS + n - 2)
                                        eng.wait_ge(s["pb_copied"], c * UNITS + n - 2)
                                    turn(n - 2).then_inc(s["pt_done"], 1)
                                if n >= 4 and n % 2 == 0:
                                    d = (n - 4) // 2
                                    weigh(eng, c, d)
                            weigh(eng, c, UNITS // 2 - 1)
                            tail_tensor(eng, s, c, lay, OT, on, oT)
                        norm_tensor(eng, s, B, nxt)
                        barrier(eng, b0)

                run(name, body)

        def attn1():
            name, lay, nxt = "A1", 1, 1
            s = sems[name]
            b0 = state["bar"]
            state["bar"] += 1
            GR = H // 2
            UR, YR = 4, 6
            SETS = H // 4
            OUT = 7
            D_BANK = (6, 0, 1, 2)
            TWO = 4
            NM = 4 * H
            with ExitStack() as st:
                def ab(n, shape, dt=F32):
                    return sb(f"{name}_{n}", shape, dt, st)
                xa = ab("xa", [P, S])
                v_new = ab("v_new", [P, TPC, D])
                rden = ab("rden", [P, H])
                VA = ab("VA", [P, TPC, H, 32])
                QT = ab("QT", [P, GR, S], F32R)
                KT = ab("KT", [P, GR, S], F32R)
                OT = ab("OT", [P, SETS, S])
                Um = ab("U", [P, UR, TPC, S])
                Y = ab("Y", [P, YR - 2, TPC, S])
                y_more = dn1[:, :, :, :].rearrange("p u b d -> p (u b d)").rearrange("p (n t q) -> p n t q", n=2, t=TPC)

                def y_slot(h):
                    n = h % YR
                    return Y[:, n] if n < YR - 2 else y_more[:, n - (YR - 2)]

                def tiles_scalar(h):
                    return h + min(h, TWO)

                def tiles_vector(h):
                    return TPC * h - tiles_scalar(h)

                def flat(a):
                    return a.rearrange("p t q -> p (t q)")

                QA = up1_hi[:, :, :].rearrange("p u n -> p (u n)").rearrange("p (h r) -> p h r", r=64)
                KA = up1_lo[:, :, :].rearrange("p u n -> p (u n)").rearrange("p (h r) -> p h r", r=64)
                qk = Um[:, 0, 0:2, :]
                sq = Um[:, 0, 2:4, :]
                nrm = Um[:, 1, 0:3].rearrange("p a q -> p (a q)")[:, 0:9 * 2 * TPC * H]\
                    .rearrange("p (n a h) -> p n a h", a=2, h=TPC * H)
                on = xn
                pad_ready = sem("A1_pad_ready")

                ACT_TURNS = (7,)

                def pair_of(i):
                    return ((4, 5), (0, 1), (2, 3))[i % 3]

                def turned(i):
                    b = pair_of(i)[0]
                    return ps[:, b:b + 2, :].rearrange("p b (g q) -> p (b g) q", q=P)

                def rows_vector(eng, k):
                    q3 = qk[:, 0, :].rearrange("p (h d) -> p h d", d=HD)
                    k3 = qk[:, 1, :].rearrange("p (h d) -> p h d", d=HD)
                    pj = ps[:, 0:TPC, :]
                    eng.wait_ge(s["pj_done"], k + 1)
                    if not (isinstance(k, int) and k == 0):
                        eng.wait_ge(s["t_ready"], k * H - 2 + UR)
                    eng.tensor_copy(qk[:, 0, :].rearrange("p (t d) -> p t d", d=D), pj[:, :, 0:D])
                    eng.tensor_scalar(qk[:, 1, :].rearrange("p (t d) -> p t d", d=D), pj[:, :, D:2 * D], -2.0, None,
                                      ALU.mult)
                    eng.tensor_copy(v_new[:, :, :], pj[:, :, 2 * D:3 * D])
                    eng.drain()
                    eng.tensor_copy(QA[:, :, 0:8], q3)
                    eng.tensor_copy(KA[:, :, 0:8], k3)
                    eng.tensor_copy(QA[:, :, 8:16], q3)
                    eng.tensor_copy(KA[:, :, 16:24], k3)
                    eng.tensor_tensor(sq, qk, qk, ALU.mult)
                    eng.drain()
                    eng.tensor_tensor(QA[:, :, 16:24], q3, QA[:, :, 0:8].bitcast(F32), ALU.subtract)
                    eng.tensor_tensor(KA[:, :, 8:16], k3, KA[:, :, 0:8].bitcast(F32), ALU.subtract)
                    eng.tensor_reduce(nrm[:, 0], sq.rearrange("p a (h d) -> p a h d", d=HD), AX.X, ALU.add)
                    eng.drain()
                    eng.tensor_scalar(nrm[:, 0, 1], nrm[:, 0, 1], 0.25, None, ALU.mult)
                    eng.drain()
                    eng.tensor_scalar(nrm[:, 1], nrm[:, 0], -1.0, 1.0, ALU.mult, ALU.add)
                    eng.drain()
                    eng.tensor_scalar(nrm[:, 2], nrm[:, 1], 0.0, None, ALU.is_gt)
                    eng.tensor_scalar(nrm[:, 3], nrm[:, 1], 0.0, None, ALU.is_lt)
                    eng.tensor_scalar(nrm[:, 4], nrm[:, 1], 0.0, None, ALU.is_equal)
                    eng.drain()
                    eng.tensor_tensor(nrm[:, 5], nrm[:, 1], nrm[:, 4], ALU.add)
                    eng.drain()
                    eng.reciprocal(nrm[:, 6], nrm[:, 5])
                    eng.drain()
                    eng.tensor_scalar(nrm[:, 6, 1], nrm[:, 6, 1], 2.0, None, ALU.mult)
                    eng.drain()
                    eng.tensor_tensor(nrm[:, 7], nrm[:, 6], nrm[:, 2], ALU.mult)
                    eng.scalar_tensor_tensor(out=nrm[:, 8].rearrange("p a h -> p (a h)"),
                                             in0=nrm[:, 6].rearrange("p a h -> p (a h)"), scalar=-1.0,
                                             in1=nrm[:, 3].rearrange("p a h -> p (a h)"),
                                             op0=ALU.mult, op1=ALU.mult)
                    eng.drain()

                    def numbers(i0, i1, a):
                        return nrm[:, i0:i1, a, :].rearrange("p n h -> p h n")

                    def place(dst, part):
                        return dst[:, :, 32:38].rearrange("p h (n r) -> p h n r", r=3)[:, :, :, part]

                    eng.tensor_copy(QA[:, :, 24:25], numbers(0, 1, 0))
                    eng.tensor_copy(KA[:, :, 26:27], numbers(0, 1, 1))
                    eng.tensor_copy(place(QA, 0), numbers(7, 9, 0))
                    eng.tensor_copy(place(KA, 0), numbers(7, 9, 1))
                    eng.tensor_copy(place(QA, 1), numbers(7, 9, 0))
                    eng.tensor_copy(place(KA, 2), numbers(7, 9, 1))
                    eng.tensor_copy(QA[:, :, 38:41], numbers(2, 5, 0))
                    eng.tensor_scalar(KA[:, :, 38:40], numbers(2, 4, 1), -FAR, FAR, ALU.mult, ALU.add)
                    eng.drain()
                    eng.tensor_tensor(QA[:, :, 25:26], numbers(0, 1, 0), QA[:, :, 24:25].bitcast(F32), ALU.subtract)
                    eng.tensor_tensor(KA[:, :, 27:28], numbers(0, 1, 1), KA[:, :, 26:27].bitcast(F32), ALU.subtract)
                    eng.tensor_tensor(place(QA, 2), numbers(7, 9, 0), place(QA, 0).bitcast(F32), ALU.subtract)
                    eng.tensor_tensor(place(KA, 1), numbers(7, 9, 1), place(KA, 0).bitcast(F32), ALU.subtract)
                    eng.drain().then_inc(s["asm_done"], 1)
                    for i in range(2 * TPC):
                        if i not in ACT_TURNS:
                            t, dst = i // 2, (QT, KT)[i % 2]
                            eng.wait_ge(s["qk_tr"], 2 * TPC * k + i + 1)
                            eng.tensor_copy(dst[:, :, t * P:(t + 1) * P], turned(i)).then_inc(s["turned_vector"], 1)

                def rows_scalar(eng, k):
                    for i in ACT_TURNS:
                        t, dst = i // 2, (QT, KT)[i % 2]
                        eng.wait_ge(s["qk_tr"], 2 * TPC * k + i + 1)
                        eng.activation(dst[:, :, t * P:(t + 1) * P], turned(i), ACT.Copy).then_inc(s["turned_scalar"], 1)

                def wait_turned(eng, k, i):
                    before_i = len([j for j in ACT_TURNS if j <= i])
                    if i in ACT_TURNS:
                        eng.wait_ge(s["turned_scalar"], len(ACT_TURNS) * k + before_i)
                    else:
                        eng.wait_ge(s["turned_vector"], (2 * TPC - len(ACT_TURNS)) * k + i + 1 - before_i)

                def rows_tensor(eng, k, between):
                    project_tensor(eng, s, k, lay, xa)
                    between()
                    eng.wait_ge(s["asm_done"], k + 1)
                    for i in range(2 * TPC):
                        t, src = i // 2, (QA, KA)[i % 2]
                        if i >= 3:
                            wait_turned(eng, k, i - 3)
                        for g in range(GR):
                            last = eng.transpose(
                                ps[:, pair_of(i)[g // 4], (g % 4) * P:(g % 4 + 1) * P],
                                src[:, t * H + 2 * g:t * H + 2 * g + 2, :].rearrange("p h r -> p (h r)")
                                .bitcast(F32), ident[:, :])
                        last.then_inc(s["qk_tr"], 1)
                    wait_turned(eng, k, 2 * TPC - 2)
                    wait_turned(eng, k, 2 * TPC - 1)

                def input_scalar(eng, k, chunk):
                    eng.activation(xa[:, :], XT[:, bass.ds(chunk * S, S)], ACT.Copy).then_inc(s["xs_ready"], 1)

                def out_copy_vector(eng, c, g):
                    eng.wait_ge(s["pvh_done"], c * (H // 2) + 2 * g + 3)
                    eng.tensor_copy(OT[:, g, :], ps[:, OUT, :]).then_inc(s["ot_copied"], 1)

                def turn_out_tensor(eng, n, t):
                    eng.wait_ge(s["ot_copied"], SETS * n)
                    eng.wait_ge(s["on_ready"], TPC * n + t)
                    for g in range(SETS):
                        last = eng.transpose(ps[:, OUT, g * P:(g + 1) * P], OT[:, g, t * P:(t + 1) * P], ident[:, :])
                    last.then_inc(s["on_tr"], 1)

                def divide_vector(eng, n, t):
                    eng.wait_ge(s["on_tr"], TPC * n + t + 1)
                    v = ps[:, OUT, :].rearrange("p (h r) -> p h r", r=32)
                    eng.reciprocal(rden[:, :], v[:, :, HD])
                    eng.drain()
                    eng.tensor_tensor(on[:, t, :].rearrange("p (h d) -> p h d", d=HD), v[:, :, 0:HD],
                                      rden[:, :].unsqueeze(2).to_broadcast([P, H, HD]), ALU.mult)\
                        .then_inc(s["on_ready"], 1)

                def turn_back_tensor(eng, n):
                    eng.wait_ge(s["on_ready"], TPC * (n + 1))
                    for t in range(TPC):
                        last = eng.transpose(ps[:, OUT, t * P:(t + 1) * P], on[:, t, :], ident[:, :])
                    last.then_inc(s["oT_tr"], 1)

                def copy_back_scalar(eng, n):
                    eng.wait_ge(s["oT_tr"], n)
                    eng.activation(xa[:, :], ps[:, OUT, :], ACT.Copy).then_inc(s["oT_ready"], 1)

                def project_out_tensor(eng, n):
                    eng.wait_ge(s["oT_ready"], n)
                    for t in range(TPC):
                        last = eng.matmul(ps[:, OUT, t * P:(t + 1) * P], xa[:, t * P:(t + 1) * P], out_w[lay][:, :],
                                          start=True, stop=True)
                    last.then_inc(s["o_done"], 1)

                def residual_vector(eng, n, chunk):
                    eng.wait_ge(s["o_done"], n)
                    x_c = tiles_of(chunk)
                    eng.tensor_tensor(x_c, x_c, ps[:, OUT, :].rearrange("p (t d) -> p t d", d=D),
                                      ALU.add).then_inc(s["x_added"], 1)

                def body(block):
                    @block.gpsimd
                    def _(eng):
                        eng.memset(QA.rearrange("p h r -> p (h r)").bitcast(F32), 0.0)
                        eng.memset(KA.rearrange("p h r -> p (h r)").bitcast(F32), 0.0)
                        eng.memset(VA[:, :, :, :].rearrange("p t h r -> p (t h r)"), 0.0)
                        eng.drain()
                        eng.memset(QA[:, :, 26:28].bitcast(F32), 1.0)
                        eng.memset(KA[:, :, 24:26].bitcast(F32), 1.0)
                        eng.memset(KA[:, :, 40:41].bitcast(F32), FAR)
                        eng.memset(VA[:, :, :, HD:HD + 1], 1.0)
                        eng.drain().then_inc(pad_ready, 1)
                        eng.sem_inc(s["t_ready"], UR)
                        eng.sem_inc(s["rstd_ready"], 1)

                        def main(c, first):
                            for h in range(H):
                                if h == 2 and not first:
                                    norm_gpsimd(eng, s, c)
                                eng.wait_ge(s["s_ready"], c * H + h + 1)
                                eng.tensor_tensor(flat(y_slot(h)), flat(y_slot(h)), flat(Um[:, h % UR]),
                                                  ALU.add).then_inc(s["t_ready"], 1)

                        main(0, True)
                        with eng.Fori(1, B) as c:
                            main(c, False)
                        norm_gpsimd(eng, s, B)
                        barrier(eng, b0)

                    @block.scalar
                    def _(eng):
                        norm_credits_scalar(eng, s)
                        eng.sem_inc(s["xt_copied"], 2)

                        def main(c, first):
                            def relu(h):
                                if h < H:
                                    eng.wait_ge(s["t_ready"], c * H + h + 1)
                                    eng.wait_ge(s["g_done"], c * NM + max(4 * h, 1))
                                    for kt in range(2 if h < TWO else 1):
                                        if kt == 1:
                                            eng.wait_ge(s["g_done"], c * NM + 4 * h + 1)
                                        eng.activation(Um[:, h % UR, kt, :], ps[:, D_BANK[kt], :],
                                                       ACT.Relu).then_inc(s["dp_scalar"], 1)

                            relu(0)
                            relu(1)
                            for heads in (range(0, 4), range(4, 8), range(8, 12), (12, 13), (14, 15)):
                                for h in heads:
                                    if h % 4 == 3:
                                        relu(h + 1)
                                    eng.wait_ge(s["y_ready"], c * H + h + 1)
                                    eng.activation(flat(y_slot(h)), flat(y_slot(h)), ACT.Sqrt).then_inc(s["s_ready"], 1)
                                    if h == 0:
                                        relu(2)
                                    if h == 1:
                                        if not first:
                                            copy_back_scalar(eng, c)
                                        relu(3)
                                    if h == 2 and not first:
                                        norm_scalar(eng, s, c, last_chunk(c), nxt, OUT)
                                    if h == 3:
                                        eng.wait_ge(s["pvh_done"], c * (H // 2) + 1)
                                        eng.wait_ge(s["asm_done"], c + 1)
                                        eng.activation(VA[:, :, :, 0:HD],
                                                       v_new[:, :, :].rearrange("p t (h d) -> p t h d", d=HD),
                                                       ACT.Copy).then_inc(s["v_ready"], 1)
                                eng.preload_act_table_set("natural_log_exp_and_others")
                                for h in heads:
                                    y = flat(y_slot(h))
                                    eng.wait_ge(s["t_ready"], c * H + h + 1 + UR)
                                    eng.activation(y, y, ACT.Ln, bias=1.0)
                                    eng.drain()
                                    eng.activation(y, y, ACT.Exp, scale=-1.0).then_inc(s["y_exp"], 1)
                                    if h == 7:
                                        input_scalar(eng, c + 1, (c + 1) % B)
                                    if h % 4 != 2:
                                        relu(h + 5 - (h % 4 == 3))
                            rows_scalar(eng, c + 1)

                        input_scalar(eng, 0, 0)
                        rows_scalar(eng, 0)
                        eng.wait_ge(pad_ready, 1)
                        main(0, True)
                        with eng.Fori(1, B) as c:
                            main(c, False)
                        copy_back_scalar(eng, B)
                        norm_scalar(eng, s, B, B - 1, nxt, OUT)
                        barrier(eng, b0)

                    @block.vector
                    def _(eng):
                        norm_credits_vector(eng, s, nxt)
                        eng.sem_inc(s["lg_copied"], 1)
                        eng.sem_inc(s["var_ready"], 1)
                        eng.sem_inc(s["xn_ready"], 1)
                        eng.sem_inc(s["on_ready"], TPC)

                        def main(c, first):
                            for h in range(H):
                                eng.wait_ge(s["t_ready"], c * H + h + 1)

                                def relu(kt):
                                    eng.wait_ge(s["g_done"], c * NM + 4 * h + kt)
                                    eng.tensor_scalar(Um[:, h % UR, kt, :], ps[:, D_BANK[kt], :], 0.0, None,
                                                      ALU.max).then_inc(s["dp_vector"], 1)

                                def scale(kt):
                                    m = 4 * h + kt
                                    eng.wait_ge(s["g_done"], c * NM + m + 1)
                                    mine = 2 if h < TWO else 1
                                    if kt < mine:
                                        eng.wait_ge(s["dp_scalar"], c * tiles_scalar(H) + tiles_scalar(h) + kt + 1)
                                    else:
                                        eng.wait_ge(s["dp_vector"],
                                                    c * tiles_vector(H) + tiles_vector(h) + kt + 1 - mine)
                                    eng.scalar_tensor_tensor(out=Um[:, h % UR, kt, :], in0=ps[:, 3 + m % 3, :],
                                                             scalar=CLAMP, in1=Um[:, h % UR, kt, :], op0=ALU.min,
                                                             op1=ALU.mult).then_inc(s["u_ready"], 1)

                                tail = not first
                                if h >= TWO:
                                    relu(1)
                                relu(2)
                                if tail and h == 1:
                                    divide_vector(eng, c, 0)
                                if tail and h == 2:
                                    divide_vector(eng, c, 3)
                                if tail and h == 3:
                                    norm_apply_vector(eng, s, c, last_chunk(c))
                                scale(0)
                                scale(1)
                                relu(3)
                                if tail and h == 1:
                                    divide_vector(eng, c, 1)
                                scale(2)
                                scale(3)
                                if tail and h == 1:
                                    divide_vector(eng, c, 2)
                                if tail and h == 2:
                                    residual_vector(eng, c, last_chunk(c))
                                    norm_stats_vector(eng, s, c, last_chunk(c))
                                if tail and h == 4:
                                    norm_logits_vector(eng, s, c, last_chunk(c), nxt)
                                u = flat(Um[:, h % UR])
                                eng.drain()
                                if h >= YR:
                                    eng.wait_ge(s["pvh_done"], c * (H // 2) + (h - YR) // 2 + 2)
                                elif tail and h < 4:
                                    eng.wait_ge(s["pvh_done"], c * (H // 2) + h // 2)
                                eng.scalar_tensor_tensor(out=flat(y_slot(h)), in0=u, scalar=2.0, in1=u, op0=ALU.add,
                                                         op1=ALU.mult).then_inc(s["y_ready"], 1)
                                if tail and h == 0:
                                    out_copy_last(c)
                                if h % 4 == 0 and h >= 8:
                                    out_copy_vector(eng, c, h // 4 - 2)
                            out_copy_vector(eng, c, SETS - 2)
                            rows_vector(eng, c + 1)

                        def out_copy_last(n):
                            eng.wait_ge(s["pvh_done"], n * (H // 2) + 1)
                            eng.tensor_copy(OT[:, SETS - 1, :], ps[:, OUT, :]).then_inc(s["ot_copied"], 1)

                        eng.wait_ge(pad_ready, 1)
                        rows_vector(eng, 0)
                        main(0, True)
                        with eng.Fori(1, B) as c:
                            main(c, False)
                        out_copy_last(B)
                        for t in range(TPC):
                            divide_vector(eng, B, t)
                        residual_vector(eng, B, B - 1)
                        norm_vector(eng, s, B, B - 1, nxt)
                        barrier(eng, b0)

                    @block.tensor
                    def _(eng):
                        norm_credits_tensor(eng, s)
                        eng.sem_inc(s["tr_done"], 1)
                        eng.sem_inc(s["lg_done"], 1)
                        eng.sem_inc(s["on_tr"], TPC)
                        eng.sem_inc(s["pvh_done"], 1)

                        def outputs(c, pair, kt):
                            if kt == 0:
                                eng.wait_ge(s["y_exp"], c * H + 2 * pair + 2)
                                if pair % 2 == 0 and pair > 0:
                                    eng.wait_ge(s["ot_copied"], c * SETS + pair // 2)
                            for h in (2 * pair, 2 * pair + 1):
                                j = 32 * (h % 4)
                                last = eng.matmul(ps[j:j + 32, OUT, :], VA[:, kt, h, :], y_slot(h)[:, kt, :],
                                                  start=(kt == 0), stop=(kt == TPC - 1))
                            if kt == TPC - 1:
                                last.then_inc(s["pvh_done"], 1)

                        def last_outputs(n):
                            eng.wait_ge(s["y_exp"], n * H)
                            for kt in range(TPC):
                                for h in (H - 2, H - 1):
                                    j = 32 * (h % 4)
                                    last = eng.matmul(ps[j:j + 32, OUT, :], VA[:, kt, h, :], y_slot(h)[:, kt, :],
                                                      start=(kt == 0), stop=(kt == TPC - 1))
                            last.then_inc(s["pvh_done"], 1)

                        def main(c, first):
                            def difference(h, kt):
                                if h == H:
                                    return
                                theirs = 2 if h - 1 < TWO else 1
                                if h > 0 and kt < theirs:
                                    eng.wait_ge(s["dp_scalar"], c * tiles_scalar(H) + tiles_scalar(h - 1) + kt + 1)
                                elif h > 0:
                                    eng.wait_ge(s["dp_vector"],
                                                c * tiles_vector(H) + tiles_vector(h - 1) + kt + 1 - theirs)
                                r = 64 * (h % 2)
                                eng.matmul(ps[:, D_BANK[kt], :], KT[r:r + 28, h // 2, kt * P:(kt + 1) * P],
                                           QT[r:r + 28, h // 2, :], start=True, stop=True)

                            difference(0, 0)
                            for h in range(H):
                                g, r = h // 2, 64 * (h % 2)
                                for kt in range(TPC):
                                    m = 4 * h + kt
                                    difference(h + (kt + 1) // 4, (kt + 1) % 4)
                                    if m >= 3:
                                        eng.wait_ge(s["u_ready"], c * NM + m - 2)
                                    eng.matmul(ps[:, 3 + m % 3, :], KT[r + 32:r + 41, g, kt * P:(kt + 1) * P],
                                               QT[r + 32:r + 41, g, :], start=True, stop=True)\
                                        .then_inc(s["g_done"], 1)
                                    if h >= 6 and h % 4 >= 2 and kt >= 2:
                                        if (h, kt) == (6, 2):
                                            eng.wait_ge(s["v_ready"], c + 1)
                                            if not first:
                                                eng.wait_ge(s["lg_copied"], c + 2)
                                        pair = 2 * (h // 4 - 1) + h % 2
                                        outputs(c, pair, 2 * (kt - 2))
                                        outputs(c, pair, 2 * (kt - 2) + 1)
                                    if not first:
                                        if (h, kt) == (0, 2):
                                            last_outputs(c)
                                        if (h, kt) == (1, 2):
                                            turn_out_tensor(eng, c, 0)
                                            turn_out_tensor(eng, c, 1)
                                        if (h, kt) == (1, 3):
                                            turn_out_tensor(eng, c, 2)
                                        if (h, kt) == (2, 2):
                                            turn_out_tensor(eng, c, 3)
                                            turn_back_tensor(eng, c)
                                        if (h, kt) == (3, 0):
                                            project_out_tensor(eng, c)
                                        if (h, kt) == (3, 2):
                                            norm_turn_tensor(eng, s, c, OUT)
                                        if (h, kt) == (4, 0):
                                            norm_logits_tensor(eng, s, c, nxt)
                            eng.wait_ge(s["u_ready"], (c + 1) * NM)
                            rows_tensor(eng, c + 1, lambda: [outputs(c, H // 2 - 2, kt) for kt in range(TPC)])

                        rows_tensor(eng, 0, lambda: None)
                        main(0, True)
                        with eng.Fori(1, B) as c:
                            main(c, False)
                        last_outputs(B)
                        for t in range(TPC):
                            turn_out_tensor(eng, B, t)
                        turn_back_tensor(eng, B)
                        project_out_tensor(eng, B)
                        norm_turn_tensor(eng, s, B, OUT)
                        norm_logits_tensor(eng, s, B, nxt)
                        barrier(eng, b0)

                run(name, body)

        phases = [("F0a", lambda: ffn_phase("F0a", 0, None)), ("A0", lambda: attn0()),
                  ("F0b", lambda: ffn_phase("F0b", 0, 1)), ("F1a", lambda: ffn_phase("F1a", 1, None)),
                  ("A1", lambda: attn1()), ("F1b", lambda: ffn_phase("F1b", 1, "end"))]
        for n, (name, f) in enumerate(phases):
            if n >= stop_after:
                break
            f()
            if name == "F0b":
                r0.close()
        if stop_after < 3:
            r0.close()

        with nc.Block() as block:
            @block.sync
            def _(eng):
                eng.wait_ge(bar, ENGINES * state["bar"])
                eng.dma_start(out, X[:, :, :]).then_inc(stored, 16)
                eng.wait_ge(stored, 16)


def kernel(stop_after=99, **inputs):
    import numpy as np
    import concourse.bacc as bacc
    from concourse.bass_utils import run_bass_kernel_spmd

    a = {k: np.asarray(v) for k, v in inputs.items()}
    E_, HID_ = 8, 256

    def up_pair(w1, w3):
        w = np.stack([w1, w3], 1).reshape(w1.shape[0], 2, 2, 128, 128)
        return w.transpose(4, 0, 2, 1, 3).reshape(128, -1)

    w1 = np.concatenate([a["L0_ffn_sw1"], a["L0_ffn_w1"]], 0)
    w3 = np.concatenate([a["L0_ffn_sw3"], a["L0_ffn_w3"]], 0)
    w2 = np.concatenate([a["L0_ffn_sw2"], a["L0_ffn_w2"]], 0)
    arrays = {
        "x": a["L0_attn_x"].reshape(32, 128, 128).transpose(1, 0, 2),
        "alpha": a["L0_attn_alpha"].reshape(1, 1),
        "w_qkv0": np.concatenate([a["L0_attn_Wq"], a["L0_attn_Wk"], a["L0_attn_Wv"]], 1),
        "bias_rows0": np.stack([a["L0_attn_bq"], a["L0_attn_bk"], a["L0_attn_bv"], a["L0_attn_bfc"]], 0),
        "wo0": a["L0_attn_W_o"],
        "wo0_t": a["L0_attn_W_o"].transpose(0, 2, 1),
        "wfc0": a["L0_attn_Wfc"],
        "router0": a["L0_ffn_router_w"].T,
        "expert_bias": a["L0_ffn_expert_bias"].reshape(1, 8),
        "up0": up_pair(w1, w3),
        "down0": w2.reshape(10, 128, 2, 128).transpose(3, 0, 2, 1),
        "w_qkv1": np.concatenate([a["L1_attn_Wq"].T, a["L1_attn_Wk"].T, a["L1_attn_Wv"].T], 1),
        "wo1": a["L1_attn_Wo"].T,
        "router1": a["L1_ffn_w_g"].T,
        "up1": a["L1_ffn_c_fc"].transpose(1, 0, 2).reshape(128, -1),
        "down1": a["L1_ffn_c_proj"].reshape(8, 4, 128, 128).transpose(2, 0, 1, 3),
    }
    nc = bacc.Bacc("TRN2", target_bir_lowering=False, num_devices=1)
    feed, args = {}, []
    for name, v in arrays.items():
        v = np.ascontiguousarray(v)
        feed[f"in_{name}"] = v
        args.append(nc.dram_tensor(f"in_{name}", v.shape, mybir.dt.from_np(v.dtype), kind="ExternalInput").ap())
    out = nc.dram_tensor("out_x", (128, 32, 128), mybir.dt.float32, kind="ExternalOutput").ap()
    macaron(nc, *args, out, stop_after=stop_after)
    r = run_bass_kernel_spmd(nc, [feed], core_ids=[0])
    return r.results[0]["out_x"].transpose(1, 0, 2).reshape(8, 512, 128)
```

```python
from contextlib import ExitStack

import concourse.bass as bass
from concourse import mybir

ALU = mybir.AluOpType
ACT = mybir.ActivationFunctionType
AX = mybir.AxisListType
F32 = mybir.dt.float32
F32R = mybir.dt.float32r
BF16 = mybir.dt.bfloat16
I32 = mybir.dt.int32

P = 128
B, S, D = 8, 512, 128
TOK = B * S
TPC = S // P
TILES = TOK // P
H, HD = 16, 8
E = 8
NSH = 2
HID0, HID1 = 256, 512
HB0, HB1 = HID0 // P, HID1 // P
U0, U1 = NSH + E, E
CAP = int(1.25 * TOK * 2 / E)
EPS = 1e-5
NEG = -1e30
WIN = 2 * P
HALO = 64
INV_SQRT = 1.0 / float(HD) ** 0.5
CLAMP = 2e6
FAR = float(2 ** 21)


def macaron(nc, x, alpha, w_qkv0, bias_rows0, wo0, wo0_t, wfc0, router0, expert_bias, up0, down0,
            w_qkv1, wo1, router1, up1, down1, out, stop_after=99):
    ctx = ExitStack()
    with ctx:
        def sb(name, shape, dt=F32, stack=ctx):
            return stack.enter_context(nc.sbuf_tensor(name, shape, dt))

        def sem(name):
            return ctx.enter_context(nc.semaphore(name))

        ps = ctx.enter_context(nc.psum_tensor("ps", [P, 8, 512], F32))

        X = sb("X", [P, TILES, D])
        XT = sb("XT", [P, TOK])
        dn1 = sb("dn1", [P, U1, HB1, D])
        ident = sb("ident", [P, P])
        ident_b = sb("ident_b", [P, P], BF16)
        before = sb("before", [P, P], BF16)
        ones_b = sb("ones_b", [P, P], BF16)
        ones_f = sb("ones_f", [P, P])
        half_neg = sb("half_neg", [P, TPC])
        rw = [sb("rw0", [P, E]), sb("rw1", [P, E])]
        ebias = sb("ebias", [P, 2, E])
        logits = sb("logits", [P, TILES, E])
        cw = sb("cw", [P, TILES, E])
        cw_c = sb("cw_c", [P, TPC, E])
        bn = sb("bn", [P, TPC, 6])
        mv = sb("mv", [P, TPC, 2])
        var_eps = sb("var_eps", [P, TPC])
        rstd = sb("rstd", [P, TPC])
        xn = sb("xn", [P, TPC, D])
        xT_c = sb("xT_c", [P, S])
        alpha_s = sb("alpha_s", [P, 1])
        col = sb("col", [P, 24])

        load = {k: sem(f"load_{k}") for k in ("x", "up0", "up1", "rest", "small", "dn1")}
        up1_top, up1_split = sem("up1_top"), sem("up1_split")
        staged_free = sem("staged_free")
        consts_ready = sem("consts_ready")
        bar = sem("phase_barrier")
        stored = sem("stored")
        step = sem("route_step")

        names = ["P", "F0a", "A0", "F0b", "F1a", "A1", "F1b"]
        sems = {}
        for n in names:
            kinds = ["tr_done", "xt_copied", "lg_done", "lg_copied", "var_ready", "rstd_ready", "xn_ready"]
            if n[0] in "PF":
                kinds += ["xs_free", "split_done", "up_done", "act_done", "h_ready", "dn_done", "acc_done"]
            if n[0] == "A":
                kinds += ["xs_ready", "pj_done", "asm_done", "qk_tr", "q_copied", "k_copied", "ot_copied", "on_tr",
                          "on_ready", "oT_tr", "oT_ready", "o_done", "x_added"]
            if n == "A0":
                kinds += ["va_ready", "sc_done", "unit_begun", "m_ready", "exp_done", "pt_done", "pa_copied", "pb_copied", "pv_done"]
            if n == "A1":
                kinds += ["turned_vector", "turned_scalar", "v_ready", "g_done", "dp_vector", "dp_scalar", "u_ready", "y_ready", "s_ready",
                          "t_ready", "y_exp", "pvh_done"]
            sems[n] = {k: sem(f"{n}_{k}") for k in kinds}

        ENGINES = 4

        def barrier(eng, k):
            eng.drain().then_inc(bar, 1)
            eng.wait_ge(bar, ENGINES * (k + 1))

        def tiles_of(c):
            return X[:, bass.ds(TPC * c, TPC), :]

        def norm_stats_vector(eng, s, i, c):
            eng.drain()
            for t in range(TPC):
                eng.bn_stats(bn[:, t, :], X[:, bass.ds(TPC * c + t, 1), :].rearrange("p a d -> p (a d)"))
            eng.drain()
            for t in range(TPC):
                eng.bn_aggr(mv[:, t, :], bn[:, t, :])
            eng.drain()
            eng.tensor_scalar(var_eps[:, :], mv[:, :, 1], EPS, None, ALU.add).then_inc(s["var_ready"], 1)

        def norm_apply_vector(eng, s, i, c):
            eng.wait_ge(s["rstd_ready"], i + 1)
            eng.wait_ge(s["tr_done"], i + 1)
            for t in range(TPC):
                last = eng.tensor_scalar(xn[:, t, :], X[:, bass.ds(TPC * c + t, 1), :].rearrange("p a d -> p (a d)"),
                                         mv[:, t, 0:1], rstd[:, t:t + 1], ALU.subtract, ALU.mult)
            last.then_inc(s["xn_ready"], 1)

        def norm_logits_vector(eng, s, i, c, lay, bank=7):
            eng.wait_ge(s["lg_done"], i + 1)
            lg = ps[:, bank, 0:TPC * E].rearrange("p (t e) -> p t e", e=E)
            dst = logits[:, bass.ds(TPC * c, TPC), :]
            eng.tensor_tensor(dst, lg, ebias[:, lay, :].unsqueeze(1).to_broadcast([P, TPC, E]),
                              ALU.add).then_inc(s["lg_copied"], 1)

        def norm_gpsimd(eng, s, i):
            eng.wait_ge(s["var_ready"], i + 1)
            eng.tensor_tensor(rstd[:, :], var_eps[:, :], half_neg[:, :], ALU.pow).then_inc(s["rstd_ready"], 1)

        def norm_turn_tensor(eng, s, i, bank=6):
            eng.wait_ge(s["xn_ready"], i + 1)
            eng.wait_ge(s["xt_copied"], 2 * i + 2)
            for t in range(TPC):
                last = eng.transpose(ps[:, bank, t * P:(t + 1) * P], xn[:, t, :], ident[:, :])
            last.then_inc(s["tr_done"], 1)

        def norm_logits_tensor(eng, s, i, lay, bank=7):
            eng.wait_ge(s["xt_copied"], 2 * i + 4)
            eng.wait_ge(s["lg_copied"], i + 1)
            for t in range(TPC):
                last = eng.matmul(ps[:, bank, t * E:(t + 1) * E], xT_c[:, t * P:(t + 1) * P], rw[lay][:, :],
                                  start=True, stop=True)
            last.then_inc(s["lg_done"], 1)

        def norm_scalar(eng, s, i, c, lay, bank=6):
            eng.wait_ge(s["tr_done"], i + 2)
            if lay is not None:
                eng.wait_ge(s["lg_copied"], i + 1)
            eng.activation(xT_c[:, :], ps[:, bank, :], ACT.Copy).then_inc(s["xt_copied"], 1)
            eng.activation(XT[:, bass.ds(c * S, S)], ps[:, bank, :], ACT.Copy).then_inc(s["xt_copied"], 1)

        def norm_credits_tensor(eng, s):
            eng.sem_inc(s["tr_done"], 1)

        def norm_credits_scalar(eng, s):
            eng.sem_inc(s["xt_copied"], 2)

        def norm_credits_vector(eng, s, lay):
            if lay is not None:
                eng.sem_inc(s["lg_copied"], 1)

        def norm_vector(eng, s, i, c, lay):
            norm_stats_vector(eng, s, i, c)
            norm_apply_vector(eng, s, i, c)
            if lay is not None:
                norm_logits_vector(eng, s, i, c, lay)

        def norm_tensor(eng, s, i, lay):
            norm_turn_tensor(eng, s, i)
            if lay is not None:
                norm_logits_tensor(eng, s, i, lay)

        def last_chunk(c):
            return (c + (B - 1)) % B

        def ffn_shape(lay):
            return (U0, HB0, 2, 2) if lay == 0 else (U1, HB1, 1, 4)

        def split_gpsimd(eng, s, XS, i, c):
            eng.wait_ge(s["xs_free"], i + 1)
            hi = XS[:, bass.ds((i % 2) * 2 * S, S)]
            lo = XS[:, bass.ds((i % 2) * 2 * S + S, S)]
            xt = XT[:, bass.ds(c * S, S)]
            eng.tensor_copy(hi, xt)
            eng.drain()
            eng.tensor_tensor(lo, xt, hi.bitcast(F32), ALU.subtract).then_inc(s["split_done"], 1)

        def ffn_tensor(eng, s, lay, XS, hT, w_hi, w_lo, dn, nxt):
            U, HB, G, RING = ffn_shape(lay)
            free = s["h_ready"] if lay == 0 else s["act_done"]
            norm_credits_tensor(eng, s)
            eng.sem_inc(s["dn_done"], 2)
            eng.sem_inc(s["xs_free"], 2)
            with eng.Fori(0, B) as c:
                eng.wait_ge(s["split_done"], c + 1)
                xh = XS[:, bass.ds((c % 2) * 2 * S, S)]
                xl = XS[:, bass.ds((c % 2) * 2 * S + S, S)]
                for e in range(U + 1):
                    if e < U:
                        for hb in range(HB):
                            j = e * HB + hb
                            eng.wait_ge(free, c * (U * HB) + j + 1)
                            for g in range(G):
                                bank = (j * G + g) % 4
                                cols = slice((hb * G + g) * P, (hb * G + g + 1) * P)
                                eng.matmul(ps[:, bank, :], w_lo[:, e, cols], xh, start=True, stop=False)
                                eng.matmul(ps[:, bank, :], w_hi[:, e, cols], xl, start=False, stop=False)
                                last = eng.matmul(ps[:, bank, :], w_hi[:, e, cols], xh, start=False, stop=True)
                            last.then_inc(s["up_done"], 1)
                    if e > 0:
                        d = e - 1
                        eng.wait_ge(s["h_ready"], c * (U * HB) + (d + 1) * HB + RING)
                        eng.wait_ge(s["acc_done"], c * U + d + 1)
                        for t in range(TPC):
                            for hb in range(HB):
                                last = eng.matmul(ps[:, 4 + d % 2, t * P:(t + 1) * P],
                                                  hT[:, d % 2, hb, t * P:(t + 1) * P], dn[:, d, hb, :],
                                                  start=(hb == 0), stop=(hb == HB - 1))
                                if e == U - 1 and t == 0 and hb == 0:
                                    last.then_inc(s["xs_free"], 1)
                        last.then_inc(s["dn_done"], 1)
                    if nxt != "end":
                        if e == 3:
                            norm_turn_tensor(eng, s, c)
                        if e == 5 and nxt is not None:
                            norm_logits_tensor(eng, s, c, nxt)
            if nxt != "end":
                norm_tensor(eng, s, B, nxt)

        def ffn_scalar(eng, s, lay, act_out, nxt):
            U, HB, G, RING = ffn_shape(lay)
            norm_credits_scalar(eng, s)
            if lay == 1:
                eng.sem_inc(s["act_done"], RING)
            eng.preload_act_table(ACT.Silu)
            with eng.Fori(0, B) as c:
                for j in range(U * HB):
                    n = c * (U * HB) + j
                    eng.wait_ge(s["up_done"], n + 1)
                    eng.wait_ge(s["h_ready"], n + 1)
                    eng.activation(act_out[:, j % RING, :], ps[:, (j * G) % 4, :],
                                   ACT.Silu if lay == 0 else ACT.Relu).then_inc(s["act_done"], 1)
                    if nxt != "end" and j == 5 * HB - 1:
                        norm_scalar(eng, s, c, last_chunk(c), nxt)
            if nxt != "end":
                norm_scalar(eng, s, B, B - 1, nxt)

        def ffn_vector(eng, s, lay, act_out, hT, acc, nxt):
            U, HB, G, RING = ffn_shape(lay)
            if nxt != "end":
                norm_credits_vector(eng, s, nxt)
            eng.sem_inc(s["h_ready"], RING)
            eng.sem_inc(s["acc_done"], 2)
            more = RING if lay == 1 else 0
            with eng.Fori(0, B) as c:
                eng.drain()
                eng.tensor_copy(cw_c[:, :, :], cw[:, bass.ds(TPC * c, TPC), :])
                for e in range(U + 1):
                    if e < U:
                        eng.wait_ge(s["dn_done"], c * U + e + 1)
                        for hb in range(HB):
                            j = e * HB + hb
                            eng.wait_ge(s["act_done"], c * (U * HB) + j + 1 + more)
                            a = act_out[:, j % RING, :]
                            b = ps[:, (j * G + 1) % 4, :] if lay == 0 else a
                            eng.tensor_tensor(hT[:, e % 2, hb, :], a, b, ALU.mult).then_inc(s["h_ready"], 1)
                    if e > 0:
                        d = e - 1
                        eng.drain()
                        eng.wait_ge(s["dn_done"], c * U + d + 3)
                        for t in range(TPC):
                            x_t = X[:, bass.ds(TPC * c + t, 1), :].rearrange("p a d -> p (a d)")
                            routed = d - (U - E)
                            last = eng.scalar_tensor_tensor(
                                out=x_t if d == U - 1 else acc[:, t, :],
                                in0=ps[:, 4 + d % 2, t * P:(t + 1) * P],
                                scalar=cw_c[:, t, routed:routed + 1] if routed >= 0 else 0.5,
                                in1=x_t if d == 0 else acc[:, t, :], op0=ALU.mult, op1=ALU.add)
                        last.then_inc(s["acc_done"], 1)
                    if nxt != "end":
                        if e == 0:
                            norm_stats_vector(eng, s, c, last_chunk(c))
                        if e == 2:
                            norm_apply_vector(eng, s, c, last_chunk(c))
                        if e == 6 and nxt is not None:
                            norm_logits_vector(eng, s, c, last_chunk(c), nxt)
            if nxt != "end":
                norm_vector(eng, s, B, B - 1, nxt)

        def ffn_gpsimd(eng, s, XS, nxt):
            split_gpsimd(eng, s, XS, 0, 0)
            with eng.Fori(0, B) as c:
                if nxt != "end":
                    norm_gpsimd(eng, s, c)
                split_gpsimd(eng, s, XS, c + 1, (c + 1) % B)
            if nxt != "end":
                norm_gpsimd(eng, s, B)

        def route_vector(eng, buf, n, lay):
            work, oh, oh_b, m, ex, pr, rank, tot, cum, incr = buf

            def be(a):
                return a.unsqueeze(2).to_broadcast([P, TILES, E])

            src = logits
            for k in range(2):
                eng.tensor_reduce(m[:, k, :], src[:, :, :], AX.X, ALU.max)
                eng.drain()
                eng.tensor_tensor(work[:, 0], src[:, :, :], be(m[:, k, :]), ALU.is_equal)
                eng.drain()
                eng.tensor_tensor(work[:, 1], work[:, 0], incr[:, :].unsqueeze(1).to_broadcast([P, TILES, E]), ALU.mult)
                eng.drain()
                eng.tensor_reduce(m[:, 2, :], work[:, 1], AX.X, ALU.max)
                eng.drain()
                eng.tensor_tensor(oh[:, k], work[:, 1], be(m[:, 2, :]), ALU.is_equal)
                eng.drain()
                if k == 0:
                    eng.scalar_tensor_tensor(out=work[:, 2].rearrange("p t e -> p (t e)"),
                                             in0=oh[:, 0].rearrange("p t e -> p (t e)"), scalar=NEG,
                                             in1=logits[:, :, :].rearrange("p t e -> p (t e)"),
                                             op0=ALU.mult, op1=ALU.add)
                    eng.drain()
                    src = work[:, 2]
            eng.tensor_tensor(ex[:, 0, :], m[:, 1, :], m[:, 0, :], ALU.subtract).then_inc(step, 1)
            for k in range(2):
                eng.tensor_copy(oh_b[:, k].rearrange("p e t -> p t e"), oh[:, k])
            eng.drain().then_inc(step, 1)
            eng.wait_ge(step, n + 3)
            eng.tensor_scalar(ex[:, 2, :], ex[:, 1, :], 1.0, None, ALU.add)
            eng.drain()
            eng.reciprocal(pr[:, 0, :], ex[:, 2, :])
            eng.drain()
            eng.tensor_tensor(pr[:, 1, :], ex[:, 1, :], pr[:, 0, :], ALU.mult)
            eng.drain()
            if lay == 1:
                eng.wait_ge(step, n + 4)
                w3 = ps[:, 0, :].rearrange("p (k e t) -> p k e t", k=2, e=E)
                t3 = ps[:, 1, :].rearrange("p (k e t) -> p k e t", k=2, e=E)
                for k in range(2):
                    eng.tensor_copy(tot[:, :, k, :], t3[:, k])
                eng.drain()
                for e in range(E):
                    eng.tensor_tensor_scan(cum[:, e, :], ones_f[:, 0:2 * TILES], tot[:, e].rearrange("p k t -> p (k t)"),
                                           0.0, ALU.mult, ALU.add)
                eng.drain()
                eng.tensor_tensor(cum[:, :, :], cum[:, :, :], tot[:, :, :, :].rearrange("p e k t -> p e (k t)"),
                                  ALU.subtract)
                eng.drain()
                for k in range(2):
                    eng.tensor_tensor(rank[:, k], cum[:, :, k * TILES:(k + 1) * TILES].rearrange("p e t -> p t e"),
                                      w3[:, k].rearrange("p e t -> p t e"), ALU.add)
                eng.drain()
                for k in range(2):
                    eng.scalar_tensor_tensor(out=oh[:, k].rearrange("p t e -> p (t e)"),
                                             in0=rank[:, k].rearrange("p t e -> p (t e)"), scalar=float(CAP),
                                             in1=oh[:, k].rearrange("p t e -> p (t e)"), op0=ALU.is_lt, op1=ALU.mult)
                eng.drain()
            for k in range(2):
                eng.tensor_tensor(work[:, k], oh[:, k], be(pr[:, k, :]), ALU.mult)
            eng.drain()
            eng.tensor_tensor(work[:, 2], work[:, 0], work[:, 1], ALU.add)
            eng.drain()
            eng.tensor_scalar(cw[:, :, :], work[:, 2], 0.5, None, ALU.mult)

        def route_scalar(eng, buf, n):
            ex = buf[4]
            eng.wait_ge(step, n + 2)
            eng.activation(ex[:, 1, :], ex[:, 0, :], ACT.Exp).then_inc(step, 1)

        def route_tensor(eng, buf, n, lay):
            oh_b = buf[2]
            if lay == 1:
                eng.wait_ge(step, n + 3)
                rhs = oh_b[:, :, :, :].rearrange("p k e t -> p (k e t)")
                eng.matmul(ps[:, 0, :], before[:, :], rhs, start=True, stop=True)
                eng.matmul(ps[:, 1, :], ones_b[:, :], rhs, start=True, stop=True).then_inc(step, 1)

        ROUTE_STEPS = [3, 4]

        def route_buffers(stack, phase):
            def b(name, shape, dt=F32):
                return sb(f"{phase}_{name}", shape, dt, stack)
            return [b("r_work", [P, 3, TILES, E]), b("r_oh", [P, 2, TILES, E]), b("r_ohb", [P, 2, E, TILES], BF16),
                    b("r_m", [P, 3, TILES]), b("r_ex", [P, 3, TILES]), b("r_pr", [P, 2, TILES]),
                    b("r_rank", [P, 2, TILES, E]), b("r_tot", [P, E, 2, TILES]), b("r_cum", [P, E, 2 * TILES]), incr]

        out_w1 = sb("out_w1", [P, D])
        qkv_w1_s = sb("qkv_w1_s", [P, 3 * D])
        incr = sb("incr", [P, E])

        def run(name, body):
            with nc.Block() as block:
                body(block)

        OUT = 7

        def project_tensor(eng, s, c, lay, xa):
            eng.wait_ge(s["xs_ready"], c + 1)
            for t in range(TPC):
                last = eng.matmul(ps[:, t, 0:3 * D], xa[:, t * P:(t + 1) * P], qkv_w[lay][:, :],
                                  start=True, stop=True)
            last.then_inc(s["pj_done"], 1)

        def tail_steps(s, lay, rows_of, on, oT, rden):
            def turn_out_tensor(eng, n, t):
                eng.wait_ge(s["ot_copied"], TPC * n)
                eng.wait_ge(s["on_ready"], TPC * n + t)
                for g in range(4):
                    last = eng.transpose(ps[:, OUT, g * P:(g + 1) * P], rows_of(t, g), ident[:, :])
                last.then_inc(s["on_tr"], 1)

            def divide_vector(eng, n, t):
                eng.wait_ge(s["on_tr"], TPC * n + t + 1)
                v = ps[:, OUT, :].rearrange("p (h r) -> p h r", r=32)
                eng.reciprocal(rden, v[:, :, HD])
                eng.drain()
                eng.tensor_tensor(on[:, t, :].rearrange("p (h d) -> p h d", d=HD), v[:, :, 0:HD],
                                  rden.unsqueeze(2).to_broadcast([P, H, HD]), ALU.mult).then_inc(s["on_ready"], 1)

            def turn_back_tensor(eng, n):
                eng.wait_ge(s["on_ready"], TPC * (n + 1))
                for t in range(TPC):
                    last = eng.transpose(ps[:, OUT, t * P:(t + 1) * P], on[:, t, :], ident[:, :])
                last.then_inc(s["oT_tr"], 1)

            def copy_back_scalar(eng, n):
                eng.wait_ge(s["oT_tr"], n)
                eng.activation(oT[:, :], ps[:, OUT, :], ACT.Copy).then_inc(s["oT_ready"], 1)

            def project_out_tensor(eng, n):
                eng.wait_ge(s["oT_ready"], n)
                for t in range(TPC):
                    last = eng.matmul(ps[:, OUT, t * P:(t + 1) * P], oT[:, t * P:(t + 1) * P], out_w[lay][:, :],
                                      start=True, stop=True)
                last.then_inc(s["o_done"], 1)

            def residual_vector(eng, n, chunk):
                eng.wait_ge(s["o_done"], n)
                x_c = tiles_of(chunk)
                eng.tensor_tensor(x_c, x_c, ps[:, OUT, :].rearrange("p (t d) -> p t d", d=D),
                                  ALU.add).then_inc(s["x_added"], 1)

            return (turn_out_tensor, divide_vector, turn_back_tensor, copy_back_scalar, project_out_tensor,
                    residual_vector)

        r0 = ExitStack()
        bq_s, bk, bv, bfc = (sb(n, [P, D], F32, r0) for n in ("bq_s", "bk", "bv", "bfc"))
        qkv_w = [sb("qkv_w0_s", [P, 3 * D], F32, r0), qkv_w1_s]
        out_w = [sb("out_w0", [P, D], F32, r0), out_w1]
        up0_hi = sb("up0_hi", [P, U0, 2 * HID0], F32R, r0)
        up0_lo = sb("up0_lo", [P, U0, 2 * HID0], F32R, r0)
        dn0 = sb("dn0", [P, U0, HB0, D], F32, r0)

        with ExitStack() as st:
            stage = sb("stage", [P, U0 * 2 * HID0], F32, st)
            bn_0 = sb("bn_0", [P, TILES, 6], F32, st)
            mv_0 = sb("mv_0", [P, TILES, 2], F32, st)
            var_0 = sb("var_0", [P, TILES], F32, st)
            rstd_0 = sb("rstd_0", [P, TILES], F32, st)
            xn_0 = sb("xn_0", [P, TILES, D], F32, st)
            wfc = sb("wfc", [P, D], F32, st)
            wo_t = sb("wo_t", [P, P], F32, st)
            iota_i = sb("iota_i", [P, E], I32, st)

            def body(block):
                s = sems["P"]

                @block.sync
                def _(eng):
                    eng.dma_start(X[:, :, :], x).then_inc(load["x"], 16)
                    for dst, src in ((rw[0], router0), (rw[1], router1), (wfc, wfc0), (qkv_w[0], w_qkv0),
                                     (qkv_w[1], w_qkv1), (out_w[1], wo1)):
                        eng.dma_start(dst[:, :], src).then_inc(load["small"], 16)
                    eng.dma_start(ebias[:, 0, :], expert_bias.to_broadcast([P, E])).then_inc(load["small"], 16)
                    eng.dma_start(alpha_s[:, :], alpha.to_broadcast([P, 1])).then_inc(load["small"], 16)
                    for n, dst in enumerate((bq_s, bk, bv, bfc)):
                        eng.dma_start(dst[:, :], bias_rows0[n:n + 1, :].to_broadcast([P, D])).then_inc(load["small"], 16)
                    eng.wait_ge(consts_ready, 1)
                    for h in range(H):
                        eng.dma_start(wo_t[h * HD:(h + 1) * HD, h * HD:(h + 1) * HD], wo0_t[h]).then_inc(load["small"], 16)
                    eng.dma_start(stage[:, :], up0).then_inc(load["up0"], 16)
                    eng.dma_start(dn0[:, :, :, :], down0).then_inc(load["rest"], 16)

                @block.gpsimd
                def _(eng):
                    eng.memset(wo_t[:, :], 0.0)
                    eng.drain().then_inc(consts_ready, 1)
                    eng.memset(ident[:, :], 0.0)
                    eng.memset(ones_f[:, :], 1.0)
                    eng.memset(ones_b[:, :], 1.0)
                    eng.memset(half_neg[:, :], -0.5)
                    eng.memset(ebias[:, 1, :], 0.0)
                    eng.iota(iota_i[:, :], pattern=[[-1, E]], base=E, channel_multiplier=0)
                    eng.drain()
                    eng.affine_select(out=ident[:, :], in_=ident[:, :], compare_op=ALU.not_equal, fill=1.0, base=0,
                                      pattern=[[-1, P]], channel_multiplier=1)
                    eng.affine_select(out=before[:, :], in_=ones_b[:, :], compare_op=ALU.is_gt, fill=0.0, base=0,
                                      pattern=[[1, P]], channel_multiplier=-1)
                    eng.drain()
                    eng.tensor_copy(ident_b[:, :], ident[:, :])
                    eng.tensor_copy(incr[:, :], iota_i[:, :])
                    eng.drain().then_inc(consts_ready, 1)
                    for c in range(B):
                        eng.wait_ge(s["var_ready"], c + 1)
                        tiles = slice(TPC * c, TPC * (c + 1))
                        eng.tensor_tensor(rstd_0[:, tiles], var_0[:, tiles], half_neg[:, :],
                                          ALU.pow).then_inc(s["rstd_ready"], 1)
                    barrier(eng, 0)

                @block.tensor
                def _(eng):
                    eng.wait_ge(consts_ready, 2)
                    for c in range(B + 1):
                        if c < B:
                            eng.wait_ge(s["xn_ready"], c + 1)
                            if c >= 6:
                                eng.wait_ge(s["xt_copied"], c - 5)
                            for t in range(TPC):
                                last = eng.transpose(ps[:, c % 6, t * P:(t + 1) * P], xn_0[:, TPC * c + t, :], ident[:, :])
                            last.then_inc(s["tr_done"], 1)
                        if c == 1:
                            eng.wait_ge(load["small"], 16 * (12 + H))
                        if c > 0:
                            eng.wait_ge(s["xt_copied"], c)
                            for i in range(TPC * (c - 1), TPC * c):
                                last = eng.matmul(ps[:, 7, i * E:(i + 1) * E], XT[:, i * P:(i + 1) * P], rw[0][:, :],
                                                  start=True, stop=True)
                    last.then_inc(s["lg_done"], 1)
                    eng.matmul(ps[:, 6, 0:D], wo_t[:, :], wfc[:, :], start=True, stop=True).then_inc(step, 1)
                    barrier(eng, 0)

                @block.scalar
                def _(eng):
                    for c in range(B):
                        eng.wait_ge(s["tr_done"], c + 1)
                        eng.activation(XT[:, c * S:(c + 1) * S], ps[:, c % 6, :], ACT.Copy).then_inc(s["xt_copied"], 1)
                    eng.wait_ge(load["up0"], 16)
                    eng.activation(up0_hi[:, :, :].rearrange("p u n -> p (u n)"), stage[:, :],
                                   ACT.Copy).then_inc(s["split_done"], 1)
                    eng.wait_ge(step, 1)
                    eng.activation(out_w[0][:, :], ps[:, 6, 0:D], ACT.Copy)
                    barrier(eng, 0)

                @block.vector
                def _(eng):
                    eng.wait_ge(load["x"], 16)
                    for c in range(B):
                        tiles = range(TPC * c, TPC * (c + 1))
                        for i in tiles:
                            eng.bn_stats(bn_0[:, i, :], X[:, i, :])
                        eng.drain()
                        for i in tiles:
                            eng.bn_aggr(mv_0[:, i, :], bn_0[:, i, :])
                        eng.drain()
                        eng.tensor_scalar(var_0[:, tiles[0]:tiles[0] + TPC], mv_0[:, tiles[0]:tiles[0] + TPC, 1], EPS,
                                          None, ALU.add).then_inc(s["var_ready"], 1)
                    for c in range(B):
                        eng.wait_ge(s["rstd_ready"], c + 1)
                        for i in range(TPC * c, TPC * (c + 1)):
                            last = eng.tensor_scalar(xn_0[:, i, :], X[:, i, :], mv_0[:, i, 0:1], rstd_0[:, i:i + 1],
                                                     ALU.subtract, ALU.mult)
                        last.then_inc(s["xn_ready"], 1)
                    eng.wait_ge(load["small"], 16 * (12 + H))
                    eng.tensor_scalar(bq_s[:, :], bq_s[:, :], INV_SQRT, None, ALU.mult)
                    eng.wait_ge(s["lg_done"], 1)
                    eng.tensor_tensor(logits[:, :, :], ps[:, 7, 0:TILES * E].rearrange("p (t e) -> p t e", e=E),
                                      ebias[:, 0, :].unsqueeze(1).to_broadcast([P, TILES, E]), ALU.add)
                    eng.wait_ge(s["split_done"], 1)
                    eng.tensor_tensor(up0_lo[:, :, :].rearrange("p u n -> p (u n)"), stage[:, :],
                                      up0_hi[:, :, :].rearrange("p u n -> p (u n)").bitcast(F32), ALU.subtract)
                    eng.wait_ge(load["rest"], 16)
                    barrier(eng, 0)

            run("P", body)

        state = {"step": 1, "bar": 1}

        def ffn_phase(name, lay, nxt):
            s = sems[name]
            n0, b0 = state["step"], state["bar"]
            state["step"] += ROUTE_STEPS[lay]
            state["bar"] += 1
            U, HB, G, RING = ffn_shape(lay)
            load_number = 2 if name == "F1b" else 1
            w_hi, w_lo, dn = (up0_hi, up0_lo, dn0) if lay == 0 else (up1_hi, up1_lo, dn1)
            with ExitStack() as st:
                XS = sb(f"{name}_xs", [P, 2 * 2 * S], F32R, st)
                act_out = sb(f"{name}_act", [P, RING, S], F32, st)
                acc = sb(f"{name}_acc", [P, TPC, D], F32, st)
                hT = sb(f"{name}_hT", [P, 2, HB, S], F32, st)
                with ExitStack() as st2:
                    buf = route_buffers(st2, name)
                    route_done = sem(f"{name}_route_done")

                    def body_r(block):
                        if lay == 1:
                            w_raw = sb(f"{name}_up1", [P, U1 * HID1], F32, st2)
                            w_top, w_rest = (a[:, :, :].rearrange("p u n -> p (u n)") for a in (up1_hi, up1_lo))

                            @block.sync
                            def _(eng):
                                eng.wait_ge(bar, ENGINES * b0)
                                eng.dma_start(w_raw[:, :], up1).then_inc(load["up1"], 16)
                                eng.dma_start(dn1[:, :, :, :], down1).then_inc(load["dn1"], 16)

                            @block.gpsimd
                            def _(eng):
                                eng.wait_ge(up1_top, load_number)
                                eng.tensor_tensor(w_rest, w_raw[:, :], w_top.bitcast(F32),
                                                  ALU.subtract).then_inc(up1_split, 1)

                        @block.vector
                        def _(eng):
                            route_vector(eng, buf, n0, lay)
                            eng.drain().then_inc(route_done, 1)
                            eng.wait_ge(route_done, 3)

                        @block.scalar
                        def _(eng):
                            route_scalar(eng, buf, n0)
                            if lay == 1:
                                eng.wait_ge(load["up1"], 16 * load_number)
                                eng.activation(w_top, w_raw[:, :], ACT.Copy).then_inc(up1_top, 1)
                            eng.drain().then_inc(route_done, 1)
                            eng.wait_ge(route_done, 3)

                        @block.tensor
                        def _(eng):
                            route_tensor(eng, buf, n0, lay)
                            if lay == 1:
                                eng.wait_ge(load["dn1"], 16 * load_number)
                                eng.wait_ge(up1_split, load_number)
                            eng.drain().then_inc(route_done, 1)
                            eng.wait_ge(route_done, 3)

                    run(name, body_r)

                def body(block):
                    @block.tensor
                    def _(eng):
                        ffn_tensor(eng, s, lay, XS, hT, w_hi, w_lo, dn, nxt)
                        barrier(eng, b0)

                    @block.scalar
                    def _(eng):
                        ffn_scalar(eng, s, lay, act_out, nxt)
                        barrier(eng, b0)

                    @block.vector
                    def _(eng):
                        ffn_vector(eng, s, lay, act_out, hT, acc, nxt)
                        barrier(eng, b0)

                    @block.gpsimd
                    def _(eng):
                        ffn_gpsimd(eng, s, XS, nxt)
                        barrier(eng, b0)

                run(name, body)

        def window(t):
            lo, hi = max(0, t * P - HALO), min(S, t * P - HALO + WIN)
            return lo, hi, lo - (t * P - HALO), hi - (t * P - HALO)

        def unit_head(u, r, b):
            return 2 * (u // 2) + r, 2 * (u % 2) + b

        def bank_of(t, side):
            return ((0, 1), (2, 3))[t % 2][side]

        def attn0():
            name, lay, nxt = "A0", 0, 0
            UNITS = 4 * TPC
            MR, PR = 3, 4
            VB = TPC + 1
            s = sems[name]
            b0, n0 = state["bar"], state["step"]
            state["bar"] += 1
            state["step"] += 5
            with ExitStack() as st:
                def ab(n, shape, dt=F32):
                    return sb(f"{name}_{n}", shape, dt, st)
                QA = ab("QA", [P, TPC, H, 32], F32R)
                KA = ab("KA", [P, TPC, H, 32], F32R)
                VA = ab("VA", [P, VB, H, 32])
                QT = ab("QT", [P, 4, S], F32R)
                KT = ab("KT", [P, 4, S], F32R)
                M = ab("M", [P, MR, 2, 2, WIN])
                OT = ab("OT", [P, TPC, S])
                nmax = ab("nmax", [P, MR, 2, 2])
                rden = ab("rden", [P, H])
                on = ab("on", [P, TPC, D])
                oT = ab("oT", [P, S])
                PT = dn1[:, :, :, :].rearrange("p u b d -> p (u b d)").rearrange("p (n k q) -> p n k q", n=PR, k=2)
                xa = ab("xa", [P, S])
                qs = ab("qs", [P, 2, TPC, D])
                v_new = ab("v_new", [P, VB, D])
                (turn_out_tensor, divide_vector, turn_back_tensor, copy_back_scalar, project_out_tensor,
                 residual_vector) = tail_steps(s, lay, lambda t, g: OT[:, t, g * P:(g + 1) * P], on, oT, rden[:, :])
                dist = OT[:, 0:2, :].rearrange("p a q -> p (a q)").rearrange("p (a w) -> p a w", w=WIN)
                dist_i = OT[:, 2, 0:WIN].bitcast(I32)
                mask = ab("mask", [P, WIN])
                pad_ready = sem("A0_pad_ready")

                def older(c):
                    return (c + (B - 2)) % B

                def blocks(t):
                    _, _, w0, w1 = window(t)
                    return (w0, P), (P, w1)

                def copy_turned(eng, c, n, k, done):
                    k0, k1 = blocks(n // 4)[k]
                    eng.wait_ge(s["pt_done"], c * UNITS + n + 1)
                    if n >= PR:
                        eng.wait_ge(s["pv_done"], c * (UNITS // 2) + (n - PR) // 2 + 1)
                    dst, src = PT[0:k1 - k0, n % PR, k, :], ps[0:k1 - k0, 4 + k, :]
                    if k == 0 or n >= UNITS - 2:
                        eng.activation(dst, src, ACT.Copy).then_inc(done, 1)
                    else:
                        eng.tensor_copy(dst, src).then_inc(done, 1)

                def copy_out(eng, c, t):
                    eng.wait_ge(s["pv_done"], c * (UNITS // 2) + 2 * t + 2)
                    eng.activation(OT[:, t, :], ps[:, 6 + t % 2, :], ACT.Copy).then_inc(s["ot_copied"], 1)

                def body(block):
                    @block.gpsimd
                    def _(eng):
                        eng.iota(dist_i, pattern=[[1, WIN]], base=-HALO, channel_multiplier=-1)
                        for a in (QA, KA, VA):
                            eng.memset(a[:, :, :, :].rearrange("p t h r -> p (t h r)").bitcast(F32), 0.0)
                        eng.memset(PT.rearrange("p n k q -> p (n k q)"), 0.0)
                        eng.drain()
                        eng.memset(VA[:, :, :, HD:HD + 1], 1.0)
                        eng.drain()
                        eng.memset(VA[HALO:P, 0:VB:VB - 1, :, HD:HD + 1], 0.0)
                        eng.drain().then_inc(pad_ready, 1)

                        def chunk(c, first):
                            eng.wait_ge(s["asm_done"], c + 1)
                            if not first:
                                eng.wait_ge(s["pv_done"], c * (UNITS // 2))
                            for rows, m0, m1, by in ((P, 1, TPC, 1), (HALO, 0, VB, VB - 1)):
                                nb = len(range(m0, m1, by))
                                last = eng.tensor_tensor(
                                    VA[0:rows, m0:m1:by, :, 0:HD],
                                    v_new[0:rows, m0:m1:by, :].rearrange("p t (h d) -> p t h d", d=HD),
                                    bv[0:rows, :].rearrange("p (h d) -> p h d", d=HD).unsqueeze(1)
                                    .to_broadcast([rows, nb, H, HD]), ALU.add)
                            last.then_inc(s["va_ready"], 1)
                            norm_gpsimd(eng, s, c)

                        chunk(0, True)
                        with eng.Fori(1, B) as c:
                            chunk(c, False)
                        norm_gpsimd(eng, s, B)
                        norm_gpsimd(eng, s, B + 1)
                        barrier(eng, b0)

                    @block.scalar
                    def _(eng):
                        norm_credits_scalar(eng, s)
                        eng.preload_act_table(ACT.Exp)
                        eng.activation(col[:, 17:18], alpha_s[:, :], ACT.Exp, scale=-1.0).then_inc(step, 1)
                        eng.wait_ge(step, n0 + 3)
                        eng.activation(col[:, 22:23], ps[:, 0, 0:1], ACT.Exp, scale=-1.0).then_inc(step, 1)
                        def input_scalar(eng, chunk):
                            eng.activation(xa[:, :], XT[:, bass.ds(chunk * S, S)], ACT.Copy).then_inc(s["xs_ready"], 1)

                        input_scalar(eng, 0)

                        def chunk(c, first):
                            for t in range(TPC):
                                eng.wait_ge(s["qk_tr"], 2 * (c * TPC + t) + 1)
                                eng.activation(QT[:, :, t * P:(t + 1) * P],
                                               ps[:, bank_of(t, 0), :].rearrange("p (g q) -> p g q", g=4),
                                               ACT.Copy).then_inc(s["q_copied"], 1)

                            for n in range(UNITS + 2):
                                if n >= 2:
                                    copy_turned(eng, c, n - 2, 0, s["pa_copied"])
                                if n >= UNITS:
                                    copy_turned(eng, c, n - 2, 1, s["pb_copied"])
                                if n < UNITS:
                                    _, _, w0, w1 = window(n // 4)
                                    eng.wait_ge(s["m_ready"], c * UNITS + n + 1)
                                    for b in range(2):
                                        for r in range(2):
                                            m = M[:, n % MR, b, r, w0:w1]
                                            last = eng.activation(m, m, ACT.Exp, scale=-1.0,
                                                                  bias=nmax[:, n % MR, b, r:r + 1])
                                    last.then_inc(s["exp_done"], 1)
                                if n == 2:
                                    norm_scalar(eng, s, c, older(c), nxt)
                                if n == 4 and not first:
                                    copy_back_scalar(eng, c)
                                if n == 10:
                                    input_scalar(eng, (c + 1) % B)
                                if n >= 7 and (n - 7) % 4 == 0:
                                    copy_out(eng, c, (n - 7) // 4)
                            copy_out(eng, c, TPC - 1)

                        chunk(0, True)
                        with eng.Fori(1, B) as c:
                            chunk(c, False)
                        copy_back_scalar(eng, B)
                        norm_scalar(eng, s, B, B - 2, nxt)
                        norm_scalar(eng, s, B + 1, B - 1, nxt)
                        barrier(eng, b0)

                    @block.vector
                    def _(eng):
                        norm_credits_vector(eng, s, nxt)
                        eng.sem_inc(s["on_ready"], TPC)

                        def bias_vector(eng, chunk):
                            x_c = tiles_of(chunk)
                            eng.tensor_tensor(x_c, x_c, bfc[:, :].unsqueeze(1).to_broadcast([P, TPC, D]), ALU.add)

                        ends = XT[:, :].rearrange("p (b s) -> p b s", b=B)
                        eng.wait_ge(step, n0 + 1)
                        eng.tensor_tensor(col[:, 0:B], ends[:, :, S - 1], ends[:, :, S - 2], ALU.subtract)
                        eng.tensor_scalar(col[:, 18:19], col[:, 17:18], 1.0, None, ALU.add)
                        eng.drain()
                        eng.scalar_tensor_tensor(out=col[:, 8:16], in0=col[:, 0:B], scalar=-1.0, in1=col[:, 0:B],
                                                 op0=ALU.mult, op1=ALU.max)
                        eng.reciprocal(col[:, 19:20], col[:, 18:19])
                        eng.drain()
                        eng.tensor_reduce(col[:, 16:17], col[:, 8:16], AX.X, ALU.add)
                        eng.tensor_scalar(col[:, 20:21], col[:, 19:20], -1.0, 1.0, ALU.mult, ALU.add)
                        eng.drain()
                        eng.tensor_tensor(col[:, 18:19], col[:, 20:21], col[:, 8:9], ALU.mult)
                        eng.tensor_scalar(col[:, 21:22], col[:, 16:17], col[:, 19:20], 1.0 / (B * D), ALU.mult, ALU.mult)
                        eng.drain()
                        eng.scalar_tensor_tensor(out=col[:, 20:21], in0=col[:, 18:19], scalar=ident[:, 0:1],
                                                 in1=col[:, 21:22], op0=ALU.mult, op1=ALU.add)
                        eng.drain().then_inc(step, 1)
                        eng.wait_ge(pad_ready, 1)
                        eng.tensor_copy(dist[:, 0, :], dist_i)
                        eng.drain()
                        eng.scalar_tensor_tensor(out=dist[:, 1, :], in0=dist[:, 0, :], scalar=-1.0, in1=dist[:, 0, :],
                                                 op0=ALU.mult, op1=ALU.max)
                        eng.drain()
                        eng.tensor_scalar(dist[:, 2, :], dist[:, 1, :], 2.0, None, ALU.mult)
                        eng.wait_ge(step, n0 + 4)
                        eng.tensor_scalar(col[:, 18:19], col[:, 22:23], 1.0, None, ALU.add)
                        eng.drain()
                        eng.reciprocal(col[:, 19:20], col[:, 18:19])
                        eng.drain()
                        eng.tensor_scalar(col[:, 21:22], col[:, 19:20], 96.0, 24.0, ALU.mult, ALU.add)
                        eng.drain()
                        eng.tensor_scalar(mask[:, :], dist[:, 2, :], col[:, 21:22], NEG, ALU.is_gt, ALU.mult)
                        eng.drain().then_inc(step, 1)
                        def rows_vector(k):
                            pj = ps[:, 0:4, :]
                            eng.wait_ge(s["pj_done"], k + 1)
                            eng.scalar_tensor_tensor(out=qs[:, 0], in0=pj[:, :, 0:D], scalar=INV_SQRT,
                                                     in1=bq_s[:, :].unsqueeze(1).to_broadcast([P, TPC, D]),
                                                     op0=ALU.mult, op1=ALU.add)
                            eng.tensor_tensor(qs[:, 1], pj[:, :, D:2 * D],
                                              bk[:, :].unsqueeze(1).to_broadcast([P, TPC, D]), ALU.add)
                            eng.drain()
                            q3 = qs[:, 0].rearrange("p t (h d) -> p (t h) d", d=HD)
                            k3 = qs[:, 1].rearrange("p t (h d) -> p (t h) d", d=HD)
                            qa = QA[:, :, :, :].rearrange("p t h r -> p (t h) r")
                            ka = KA[:, :, :, :].rearrange("p t h r -> p (t h) r")
                            eng.tensor_copy(qa[:, :, 0:HD], q3)
                            eng.tensor_copy(qa[:, :, HD:2 * HD], q3)
                            eng.tensor_copy(ka[:, :, 0:HD], k3)
                            eng.tensor_copy(ka[:, :, 2 * HD:3 * HD], k3)
                            eng.drain()
                            eng.tensor_tensor(qa[:, :, 2 * HD:3 * HD], q3, qa[:, :, 0:HD].bitcast(F32), ALU.subtract)
                            eng.tensor_tensor(ka[:, :, HD:2 * HD], k3, ka[:, :, 0:HD].bitcast(F32), ALU.subtract)
                            if not (isinstance(k, int) and k == 0):
                                eng.wait_ge(s["va_ready"], k)
                            eng.tensor_copy(v_new[:, 1:TPC, :], pj[:, 1:TPC, 2 * D:3 * D])
                            eng.tensor_copy(v_new[0:HALO, 0:VB:VB - 1, :],
                                            ps[0:HALO, 0, 2 * D:4 * D].rearrange("p (t d) -> p t d", d=D))
                            eng.drain().then_inc(s["asm_done"], 1)

                        rows_vector(0)

                        def chunk(c, first):
                            for t in range(TPC):
                                eng.wait_ge(s["qk_tr"], 2 * (c * TPC + t) + 2)
                                eng.tensor_copy(KT[:, :, t * P:(t + 1) * P],
                                                ps[:, bank_of(t, 1), :].rearrange("p (g q) -> p g q", g=4))\
                                    .then_inc(s["k_copied"], 1)
                                if t == 1:
                                    norm_stats_vector(eng, s, c, older(c))
                            for n in range(UNITS + 2):
                                if n < UNITS:
                                    _, _, w0, w1 = window(n // 4)
                                    eng.wait_ge(s["sc_done"], c * UNITS + n + 1)
                                    if n >= MR:
                                        eng.wait_ge(s["pt_done"], c * UNITS + n - MR + 1)
                                    eng.sem_inc(s["unit_begun"], 1)
                                    for b in range(2):
                                        for r in range(2):
                                            last = eng.tensor_tensor_reduce(
                                                M[:, n % MR, b, r, w0:w1],
                                                ps[:, 2 * (n % 2) + b, r * WIN + w0:r * WIN + w1], mask[:, w0:w1],
                                                -1.0, 3e38, ALU.add, ALU.min, nmax[:, n % MR, b, r:r + 1])
                                    last.then_inc(s["m_ready"], 1)
                                if n == 0:
                                    norm_apply_vector(eng, s, c, older(c))
                                if n == 3:
                                    norm_logits_vector(eng, s, c, older(c), nxt, 6)
                                if n == UNITS:
                                    rows_vector(c + 1)
                                if 2 <= n < UNITS:
                                    copy_turned(eng, c, n - 2, 1, s["pb_copied"])
                                if not first:
                                    if n < TPC:
                                        divide_vector(eng, c, n)
                                    if n == TPC:
                                        bias_vector(eng, last_chunk(c))
                                    if n == TPC + 2:
                                        residual_vector(eng, c, last_chunk(c))

                        chunk(0, True)
                        with eng.Fori(1, B) as c:
                            chunk(c, False)
                        for t in range(TPC):
                            divide_vector(eng, B, t)
                        bias_vector(eng, B - 1)
                        eng.drain()
                        residual_vector(eng, B, B - 1)
                        norm_vector(eng, s, B, B - 2, nxt)
                        norm_vector(eng, s, B + 1, B - 1, nxt)
                        barrier(eng, b0)

                    @block.tensor
                    def _(eng):
                        norm_credits_tensor(eng, s)
                        eng.sem_inc(s["on_tr"], TPC)
                        eng.wait_ge(step, n0 + 2)
                        eng.matmul(ps[:, 0, 0:1], ones_f[:, :], col[:, 20:21], start=True, stop=True).then_inc(step, 1)
                        eng.wait_ge(step, n0 + 5)
                        eng.wait_ge(pad_ready, 1)

                        def scores(n):
                            t, u = n // 4, n % 4
                            lo, hi, w0, w1 = window(t)
                            for r in range(2):
                                for b in range(2):
                                    g, j = unit_head(u, r, b)
                                    last = eng.matmul(ps[:, 2 * (n % 2) + b, r * WIN + w0:r * WIN + w1],
                                                      QT[32 * j:32 * j + 24, g, t * P:(t + 1) * P],
                                                      KT[32 * j:32 * j + 24, g, lo:hi], start=True, stop=True)
                            return last

                        def turn(n):
                            whole_first = sorted(enumerate(blocks(n // 4)), key=lambda b: b[1][0] - b[1][1])
                            for k, (k0, k1) in whole_first:
                                for b in range(2):
                                    for r in range(2):
                                        i = 2 * b + r
                                        last = eng.transpose(ps[0:k1 - k0, 4 + k, i * P:(i + 1) * P],
                                                             M[:, n % MR, b, r, k0:k1], ident[:, :])
                            return last

                        def outputs(d):
                            t = d // 2
                            for r in range(2):
                                for k in range(2):
                                    for n in (2 * d, 2 * d + 1):
                                        for b in range(2):
                                            g, j = unit_head(n % 4, r, b)
                                            i = 2 * b + r
                                            last = eng.matmul(ps[32 * j:32 * j + 32, 6 + t % 2, g * P:(g + 1) * P],
                                                              VA[:, t + k, 4 * g + j, :],
                                                              PT[:, n % PR, k, i * P:(i + 1) * P], start=(k == 0),
                                                              stop=(k == 1), skip_group_check=True)
                            return last

                        def weigh(eng, c, d):
                            eng.wait_ge(s["pa_copied"], c * UNITS + 2 * d + 2)
                            eng.wait_ge(s["pb_copied"], c * UNITS + 2 * d + 2)
                            if d == 0:
                                eng.wait_ge(s["va_ready"], c + 1)
                            if d >= 4 and d % 2 == 0:
                                eng.wait_ge(s["ot_copied"], c * TPC + d // 2 - 1)
                            outputs(d).then_inc(s["pv_done"], 1)

                        def project(k):
                            eng.wait_ge(s["xs_ready"], k + 1)
                            for t in range(TPC):
                                eng.matmul(ps[:, t, 0:2 * D], xa[:, t * P:(t + 1) * P], qkv_w[lay][:, 0:2 * D],
                                           start=True, stop=True)
                            for m in range(VB):
                                k0, k1 = max(m * P - HALO, 0), min(m * P + HALO, S)
                                dst = ps[0:k1 - k0, m % TPC, (2 + m // TPC) * D:(3 + m // TPC) * D]
                                last = eng.matmul(dst, xa[:, k0:k1], qkv_w[lay][:, 2 * D:3 * D], start=True, stop=True)
                            last.then_inc(s["pj_done"], 1)

                        project(0)

                        def chunk(c, first):
                            eng.wait_ge(s["asm_done"], c + 1)
                            for t in range(TPC):
                                for side, src in enumerate((QA, KA)):
                                    for g in range(4):
                                        last = eng.transpose(
                                            ps[:, bank_of(t, side), g * P:(g + 1) * P],
                                            src[:, t, 4 * g:4 * g + 4, :].rearrange("p h r -> p (h r)").bitcast(F32),
                                            ident[:, :])
                                    last.then_inc(s["qk_tr"], 1)
                                if t == 1:
                                    eng.wait_ge(s["q_copied"], c * TPC + 2)
                                    eng.wait_ge(s["k_copied"], c * TPC + 2)
                            if not first:
                                eng.wait_ge(s["ot_copied"], c * TPC)
                            eng.wait_ge(s["q_copied"], TPC * (c + 1))
                            eng.wait_ge(s["k_copied"], TPC * (c + 1))
                            for n in range(UNITS + 2):
                                if n < UNITS:
                                    if n >= 2:
                                        eng.wait_ge(s["m_ready"], c * UNITS + n - 1)
                                    scores(n).then_inc(s["sc_done"], 1)
                                if n == 1:
                                    norm_turn_tensor(eng, s, c)
                                if n == 4:
                                    eng.wait_ge(s["lg_copied"], c + 2)
                                if n == UNITS:
                                    eng.wait_ge(s["m_ready"], (c + 1) * UNITS)
                                    project(c + 1)
                                if n >= 2:
                                    eng.wait_ge(s["exp_done"], c * UNITS + n - 1)
                                    if n >= 3:
                                        eng.wait_ge(s["pa_copied"], c * UNITS + n - 2)
                                        eng.wait_ge(s["pb_copied"], c * UNITS + n - 2)
                                    turn(n - 2).then_inc(s["pt_done"], 1)
                                if n == 3:
                                    norm_logits_tensor(eng, s, c, nxt, 6)
                                if not first:
                                    if n < TPC:
                                        turn_out_tensor(eng, c, n)
                                    if n == TPC:
                                        turn_back_tensor(eng, c)
                                    if n == TPC + 1:
                                        project_out_tensor(eng, c)
                                    if n == TPC + 4:
                                        eng.wait_ge(s["x_added"], c)
                                if n >= 4 and n % 2 == 0:
                                    weigh(eng, c, (n - 4) // 2)
                            weigh(eng, c, UNITS // 2 - 1)

                        chunk(0, True)
                        with eng.Fori(1, B) as c:
                            chunk(c, False)
                        for t in range(TPC):
                            turn_out_tensor(eng, B, t)
                        turn_back_tensor(eng, B)
                        project_out_tensor(eng, B)
                        eng.wait_ge(s["x_added"], B)
                        norm_tensor(eng, s, B, nxt)
                        norm_tensor(eng, s, B + 1, nxt)
                        barrier(eng, b0)

                run(name, body)

        def attn1():
            name, lay, nxt = "A1", 1, 1
            s = sems[name]
            b0 = state["bar"]
            state["bar"] += 1
            GR = H // 2
            UR, YR = 4, 6
            SETS = H // 4
            D_BANK = (6, 0, 1, 2)
            TWO = 4
            NM = 4 * H
            with ExitStack() as st:
                def ab(n, shape, dt=F32):
                    return sb(f"{name}_{n}", shape, dt, st)
                xa = ab("xa", [P, S])
                v_new = ab("v_new", [P, TPC, D])
                rden = ab("rden", [P, H])
                VA = ab("VA", [P, TPC, H, 32])
                QT = ab("QT", [P, GR, S], F32R)
                KT = ab("KT", [P, GR, S], F32R)
                OT = ab("OT", [P, SETS, S])
                Um = ab("U", [P, UR, TPC, S])
                Y = ab("Y", [P, YR - 2, TPC, S])
                y_more = dn1[:, :, :, :].rearrange("p u b d -> p (u b d)").rearrange("p (n t q) -> p n t q", n=2, t=TPC)

                def y_slot(h):
                    n = h % YR
                    return Y[:, n] if n < YR - 2 else y_more[:, n - (YR - 2)]

                def tiles_scalar(h):
                    return h + min(h, TWO)

                def tiles_vector(h):
                    return TPC * h - tiles_scalar(h)

                def flat(a):
                    return a.rearrange("p t q -> p (t q)")

                QA = up1_hi[:, :, :].rearrange("p u n -> p (u n)").rearrange("p (h r) -> p h r", r=64)
                KA = up1_lo[:, :, :].rearrange("p u n -> p (u n)").rearrange("p (h r) -> p h r", r=64)
                qk = Um[:, 0, 0:2, :]
                sq = Um[:, 0, 2:4, :]
                nrm = Um[:, 1, 0:3].rearrange("p a q -> p (a q)")[:, 0:9 * 2 * TPC * H]\
                    .rearrange("p (n a h) -> p n a h", a=2, h=TPC * H)
                on = xn
                pad_ready = sem("A1_pad_ready")

                ACT_TURNS = (7,)

                def pair_of(i):
                    return ((4, 5), (0, 1), (2, 3))[i % 3]

                def turned(i):
                    b = pair_of(i)[0]
                    return ps[:, b:b + 2, :].rearrange("p b (g q) -> p (b g) q", q=P)

                def rows_vector(eng, k):
                    q3 = qk[:, 0, :].rearrange("p (h d) -> p h d", d=HD)
                    k3 = qk[:, 1, :].rearrange("p (h d) -> p h d", d=HD)
                    pj = ps[:, 0:TPC, :]
                    eng.wait_ge(s["pj_done"], k + 1)
                    if not (isinstance(k, int) and k == 0):
                        eng.wait_ge(s["t_ready"], k * H - 2 + UR)
                    eng.tensor_copy(qk[:, 0, :].rearrange("p (t d) -> p t d", d=D), pj[:, :, 0:D])
                    eng.tensor_scalar(qk[:, 1, :].rearrange("p (t d) -> p t d", d=D), pj[:, :, D:2 * D], -2.0, None,
                                      ALU.mult)
                    eng.tensor_copy(v_new[:, :, :], pj[:, :, 2 * D:3 * D])
                    eng.drain()
                    eng.tensor_copy(QA[:, :, 0:8], q3)
                    eng.tensor_copy(KA[:, :, 0:8], k3)
                    eng.tensor_copy(QA[:, :, 8:16], q3)
                    eng.tensor_copy(KA[:, :, 16:24], k3)
                    eng.tensor_tensor(sq, qk, qk, ALU.mult)
                    eng.drain()
                    eng.tensor_tensor(QA[:, :, 16:24], q3, QA[:, :, 0:8].bitcast(F32), ALU.subtract)
                    eng.tensor_tensor(KA[:, :, 8:16], k3, KA[:, :, 0:8].bitcast(F32), ALU.subtract)
                    eng.tensor_reduce(nrm[:, 0], sq.rearrange("p a (h d) -> p a h d", d=HD), AX.X, ALU.add)
                    eng.drain()
                    eng.tensor_scalar(nrm[:, 0, 1], nrm[:, 0, 1], 0.25, None, ALU.mult)
                    eng.drain()
                    eng.tensor_scalar(nrm[:, 1], nrm[:, 0], -1.0, 1.0, ALU.mult, ALU.add)
                    eng.drain()
                    eng.tensor_scalar(nrm[:, 2], nrm[:, 1], 0.0, None, ALU.is_gt)
                    eng.tensor_scalar(nrm[:, 3], nrm[:, 1], 0.0, None, ALU.is_lt)
                    eng.tensor_scalar(nrm[:, 4], nrm[:, 1], 0.0, None, ALU.is_equal)
                    eng.drain()
                    eng.tensor_tensor(nrm[:, 5], nrm[:, 1], nrm[:, 4], ALU.add)
                    eng.drain()
                    eng.reciprocal(nrm[:, 6], nrm[:, 5])
                    eng.drain()
                    eng.tensor_scalar(nrm[:, 6, 1], nrm[:, 6, 1], 2.0, None, ALU.mult)
                    eng.drain()
                    eng.tensor_tensor(nrm[:, 7], nrm[:, 6], nrm[:, 2], ALU.mult)
                    eng.scalar_tensor_tensor(out=nrm[:, 8].rearrange("p a h -> p (a h)"),
                                             in0=nrm[:, 6].rearrange("p a h -> p (a h)"), scalar=-1.0,
                                             in1=nrm[:, 3].rearrange("p a h -> p (a h)"),
                                             op0=ALU.mult, op1=ALU.mult)
                    eng.drain()

                    def numbers(i0, i1, a):
                        return nrm[:, i0:i1, a, :].rearrange("p n h -> p h n")

                    def place(dst, part):
                        return dst[:, :, 32:38].rearrange("p h (n r) -> p h n r", r=3)[:, :, :, part]

                    eng.tensor_copy(QA[:, :, 24:25], numbers(0, 1, 0))
                    eng.tensor_copy(KA[:, :, 26:27], numbers(0, 1, 1))
                    eng.tensor_copy(place(QA, 0), numbers(7, 9, 0))
                    eng.tensor_copy(place(KA, 0), numbers(7, 9, 1))
                    eng.tensor_copy(place(QA, 1), numbers(7, 9, 0))
                    eng.tensor_copy(place(KA, 2), numbers(7, 9, 1))
                    eng.tensor_copy(QA[:, :, 38:41], numbers(2, 5, 0))
                    eng.tensor_scalar(KA[:, :, 38:40], numbers(2, 4, 1), -FAR, FAR, ALU.mult, ALU.add)
                    eng.drain()
                    eng.tensor_tensor(QA[:, :, 25:26], numbers(0, 1, 0), QA[:, :, 24:25].bitcast(F32), ALU.subtract)
                    eng.tensor_tensor(KA[:, :, 27:28], numbers(0, 1, 1), KA[:, :, 26:27].bitcast(F32), ALU.subtract)
                    eng.tensor_tensor(place(QA, 2), numbers(7, 9, 0), place(QA, 0).bitcast(F32), ALU.subtract)
                    eng.tensor_tensor(place(KA, 1), numbers(7, 9, 1), place(KA, 0).bitcast(F32), ALU.subtract)
                    eng.drain().then_inc(s["asm_done"], 1)
                    for i in range(2 * TPC):
                        if i not in ACT_TURNS:
                            t, dst = i // 2, (QT, KT)[i % 2]
                            eng.wait_ge(s["qk_tr"], 2 * TPC * k + i + 1)
                            eng.tensor_copy(dst[:, :, t * P:(t + 1) * P], turned(i)).then_inc(s["turned_vector"], 1)

                def rows_scalar(eng, k):
                    for i in ACT_TURNS:
                        t, dst = i // 2, (QT, KT)[i % 2]
                        eng.wait_ge(s["qk_tr"], 2 * TPC * k + i + 1)
                        eng.activation(dst[:, :, t * P:(t + 1) * P], turned(i), ACT.Copy).then_inc(s["turned_scalar"], 1)

                def wait_turned(eng, k, i):
                    before_i = len([j for j in ACT_TURNS if j <= i])
                    if i in ACT_TURNS:
                        eng.wait_ge(s["turned_scalar"], len(ACT_TURNS) * k + before_i)
                    else:
                        eng.wait_ge(s["turned_vector"], (2 * TPC - len(ACT_TURNS)) * k + i + 1 - before_i)

                def rows_tensor(eng, k, between):
                    project_tensor(eng, s, k, lay, xa)
                    between()
                    eng.wait_ge(s["asm_done"], k + 1)
                    for i in range(2 * TPC):
                        t, src = i // 2, (QA, KA)[i % 2]
                        if i >= 3:
                            wait_turned(eng, k, i - 3)
                        for g in range(GR):
                            last = eng.transpose(
                                ps[:, pair_of(i)[g // 4], (g % 4) * P:(g % 4 + 1) * P],
                                src[:, t * H + 2 * g:t * H + 2 * g + 2, :].rearrange("p h r -> p (h r)")
                                .bitcast(F32), ident[:, :])
                        last.then_inc(s["qk_tr"], 1)
                    wait_turned(eng, k, 2 * TPC - 2)
                    wait_turned(eng, k, 2 * TPC - 1)

                def input_scalar(eng, k, chunk):
                    eng.activation(xa[:, :], XT[:, bass.ds(chunk * S, S)], ACT.Copy).then_inc(s["xs_ready"], 1)

                def out_copy_vector(eng, c, g):
                    eng.wait_ge(s["pvh_done"], c * (H // 2) + 2 * g + 3)
                    eng.tensor_copy(OT[:, g, :], ps[:, OUT, :]).then_inc(s["ot_copied"], 1)

                (turn_out_tensor, divide_vector, turn_back_tensor, copy_back_scalar, project_out_tensor,
                 residual_vector) = tail_steps(s, lay, lambda t, g: OT[:, g, t * P:(t + 1) * P], on, xa, rden[:, :])

                def body(block):
                    @block.gpsimd
                    def _(eng):
                        eng.memset(QA.rearrange("p h r -> p (h r)").bitcast(F32), 0.0)
                        eng.memset(KA.rearrange("p h r -> p (h r)").bitcast(F32), 0.0)
                        eng.memset(VA[:, :, :, :].rearrange("p t h r -> p (t h r)"), 0.0)
                        eng.drain()
                        eng.memset(QA[:, :, 26:28].bitcast(F32), 1.0)
                        eng.memset(KA[:, :, 24:26].bitcast(F32), 1.0)
                        eng.memset(KA[:, :, 40:41].bitcast(F32), FAR)
                        eng.memset(VA[:, :, :, HD:HD + 1], 1.0)
                        eng.drain().then_inc(pad_ready, 1)
                        eng.sem_inc(s["t_ready"], UR)
                        eng.sem_inc(s["rstd_ready"], 1)

                        def main(c, first):
                            for h in range(H):
                                if h == 2 and not first:
                                    norm_gpsimd(eng, s, c)
                                eng.wait_ge(s["s_ready"], c * H + h + 1)
                                eng.tensor_tensor(flat(y_slot(h)), flat(y_slot(h)), flat(Um[:, h % UR]),
                                                  ALU.add).then_inc(s["t_ready"], 1)

                        main(0, True)
                        with eng.Fori(1, B) as c:
                            main(c, False)
                        norm_gpsimd(eng, s, B)
                        barrier(eng, b0)

                    @block.scalar
                    def _(eng):
                        norm_credits_scalar(eng, s)
                        eng.sem_inc(s["xt_copied"], 2)

                        def main(c, first):
                            def relu(h):
                                if h < H:
                                    eng.wait_ge(s["t_ready"], c * H + h + 1)
                                    eng.wait_ge(s["g_done"], c * NM + max(4 * h, 1))
                                    for kt in range(2 if h < TWO else 1):
                                        if kt == 1:
                                            eng.wait_ge(s["g_done"], c * NM + 4 * h + 1)
                                        eng.activation(Um[:, h % UR, kt, :], ps[:, D_BANK[kt], :],
                                                       ACT.Relu).then_inc(s["dp_scalar"], 1)

                            relu(0)
                            relu(1)
                            for heads in (range(0, 4), range(4, 8), range(8, 12), (12, 13), (14, 15)):
                                for h in heads:
                                    if h % 4 == 3:
                                        relu(h + 1)
                                    eng.wait_ge(s["y_ready"], c * H + h + 1)
                                    eng.activation(flat(y_slot(h)), flat(y_slot(h)), ACT.Sqrt).then_inc(s["s_ready"], 1)
                                    if h == 0:
                                        relu(2)
                                    if h == 1:
                                        if not first:
                                            copy_back_scalar(eng, c)
                                        relu(3)
                                    if h == 2 and not first:
                                        norm_scalar(eng, s, c, last_chunk(c), nxt, OUT)
                                    if h == 3:
                                        eng.wait_ge(s["pvh_done"], c * (H // 2) + 1)
                                        eng.wait_ge(s["asm_done"], c + 1)
                                        eng.activation(VA[:, :, :, 0:HD],
                                                       v_new[:, :, :].rearrange("p t (h d) -> p t h d", d=HD),
                                                       ACT.Copy).then_inc(s["v_ready"], 1)
                                eng.preload_act_table_set("natural_log_exp_and_others")
                                for h in heads:
                                    y = flat(y_slot(h))
                                    eng.wait_ge(s["t_ready"], c * H + h + 1 + UR)
                                    eng.activation(y, y, ACT.Ln, bias=1.0)
                                    eng.drain()
                                    eng.activation(y, y, ACT.Exp, scale=-1.0).then_inc(s["y_exp"], 1)
                                    if h == 7:
                                        input_scalar(eng, c + 1, (c + 1) % B)
                                    if h % 4 != 2:
                                        relu(h + 5 - (h % 4 == 3))
                            rows_scalar(eng, c + 1)

                        input_scalar(eng, 0, 0)
                        rows_scalar(eng, 0)
                        eng.wait_ge(pad_ready, 1)
                        main(0, True)
                        with eng.Fori(1, B) as c:
                            main(c, False)
                        copy_back_scalar(eng, B)
                        norm_scalar(eng, s, B, B - 1, nxt, OUT)
                        barrier(eng, b0)

                    @block.vector
                    def _(eng):
                        norm_credits_vector(eng, s, nxt)
                        eng.sem_inc(s["lg_copied"], 1)
                        eng.sem_inc(s["var_ready"], 1)
                        eng.sem_inc(s["xn_ready"], 1)
                        eng.sem_inc(s["on_ready"], TPC)

                        def main(c, first):
                            for h in range(H):
                                eng.wait_ge(s["t_ready"], c * H + h + 1)

                                def relu(kt):
                                    eng.wait_ge(s["g_done"], c * NM + 4 * h + kt)
                                    eng.tensor_scalar(Um[:, h % UR, kt, :], ps[:, D_BANK[kt], :], 0.0, None,
                                                      ALU.max).then_inc(s["dp_vector"], 1)

                                def scale(kt):
                                    m = 4 * h + kt
                                    eng.wait_ge(s["g_done"], c * NM + m + 1)
                                    mine = 2 if h < TWO else 1
                                    if kt < mine:
                                        eng.wait_ge(s["dp_scalar"], c * tiles_scalar(H) + tiles_scalar(h) + kt + 1)
                                    else:
                                        eng.wait_ge(s["dp_vector"],
                                                    c * tiles_vector(H) + tiles_vector(h) + kt + 1 - mine)
                                    eng.scalar_tensor_tensor(out=Um[:, h % UR, kt, :], in0=ps[:, 3 + m % 3, :],
                                                             scalar=CLAMP, in1=Um[:, h % UR, kt, :], op0=ALU.min,
                                                             op1=ALU.mult).then_inc(s["u_ready"], 1)

                                tail = not first
                                if h >= TWO:
                                    relu(1)
                                relu(2)
                                if tail and h == 1:
                                    divide_vector(eng, c, 0)
                                if tail and h == 2:
                                    divide_vector(eng, c, 3)
                                if tail and h == 3:
                                    norm_apply_vector(eng, s, c, last_chunk(c))
                                scale(0)
                                scale(1)
                                relu(3)
                                if tail and h == 1:
                                    divide_vector(eng, c, 1)
                                scale(2)
                                scale(3)
                                if tail and h == 1:
                                    divide_vector(eng, c, 2)
                                if tail and h == 2:
                                    residual_vector(eng, c, last_chunk(c))
                                    norm_stats_vector(eng, s, c, last_chunk(c))
                                if tail and h == 4:
                                    norm_logits_vector(eng, s, c, last_chunk(c), nxt)
                                u = flat(Um[:, h % UR])
                                eng.drain()
                                if h >= YR:
                                    eng.wait_ge(s["pvh_done"], c * (H // 2) + (h - YR) // 2 + 2)
                                elif tail and h < 4:
                                    eng.wait_ge(s["pvh_done"], c * (H // 2) + h // 2)
                                eng.scalar_tensor_tensor(out=flat(y_slot(h)), in0=u, scalar=2.0, in1=u, op0=ALU.add,
                                                         op1=ALU.mult).then_inc(s["y_ready"], 1)
                                if tail and h == 0:
                                    out_copy_last(c)
                                if h % 4 == 0 and h >= 8:
                                    out_copy_vector(eng, c, h // 4 - 2)
                            out_copy_vector(eng, c, SETS - 2)
                            rows_vector(eng, c + 1)

                        def out_copy_last(n):
                            eng.wait_ge(s["pvh_done"], n * (H // 2) + 1)
                            eng.tensor_copy(OT[:, SETS - 1, :], ps[:, OUT, :]).then_inc(s["ot_copied"], 1)

                        eng.wait_ge(pad_ready, 1)
                        rows_vector(eng, 0)
                        main(0, True)
                        with eng.Fori(1, B) as c:
                            main(c, False)
                        out_copy_last(B)
                        for t in range(TPC):
                            divide_vector(eng, B, t)
                        residual_vector(eng, B, B - 1)
                        norm_vector(eng, s, B, B - 1, nxt)
                        barrier(eng, b0)

                    @block.tensor
                    def _(eng):
                        norm_credits_tensor(eng, s)
                        eng.sem_inc(s["tr_done"], 1)
                        eng.sem_inc(s["lg_done"], 1)
                        eng.sem_inc(s["on_tr"], TPC)
                        eng.sem_inc(s["pvh_done"], 1)

                        def outputs(c, pair, kt):
                            if kt == 0:
                                eng.wait_ge(s["y_exp"], c * H + 2 * pair + 2)
                                if pair % 2 == 0 and pair > 0:
                                    eng.wait_ge(s["ot_copied"], c * SETS + pair // 2)
                            for h in (2 * pair, 2 * pair + 1):
                                j = 32 * (h % 4)
                                last = eng.matmul(ps[j:j + 32, OUT, :], VA[:, kt, h, :], y_slot(h)[:, kt, :],
                                                  start=(kt == 0), stop=(kt == TPC - 1))
                            if kt == TPC - 1:
                                last.then_inc(s["pvh_done"], 1)

                        def last_outputs(n):
                            eng.wait_ge(s["y_exp"], n * H)
                            for kt in range(TPC):
                                for h in (H - 2, H - 1):
                                    j = 32 * (h % 4)
                                    last = eng.matmul(ps[j:j + 32, OUT, :], VA[:, kt, h, :], y_slot(h)[:, kt, :],
                                                      start=(kt == 0), stop=(kt == TPC - 1))
                            last.then_inc(s["pvh_done"], 1)

                        def main(c, first):
                            def difference(h, kt):
                                if h == H:
                                    return
                                theirs = 2 if h - 1 < TWO else 1
                                if h > 0 and kt < theirs:
                                    eng.wait_ge(s["dp_scalar"], c * tiles_scalar(H) + tiles_scalar(h - 1) + kt + 1)
                                elif h > 0:
                                    eng.wait_ge(s["dp_vector"],
                                                c * tiles_vector(H) + tiles_vector(h - 1) + kt + 1 - theirs)
                                r = 64 * (h % 2)
                                eng.matmul(ps[:, D_BANK[kt], :], KT[r:r + 28, h // 2, kt * P:(kt + 1) * P],
                                           QT[r:r + 28, h // 2, :], start=True, stop=True)

                            difference(0, 0)
                            for h in range(H):
                                g, r = h // 2, 64 * (h % 2)
                                for kt in range(TPC):
                                    m = 4 * h + kt
                                    difference(h + (kt + 1) // 4, (kt + 1) % 4)
                                    if m >= 3:
                                        eng.wait_ge(s["u_ready"], c * NM + m - 2)
                                    eng.matmul(ps[:, 3 + m % 3, :], KT[r + 32:r + 41, g, kt * P:(kt + 1) * P],
                                               QT[r + 32:r + 41, g, :], start=True, stop=True)\
                                        .then_inc(s["g_done"], 1)
                                    if h >= 6 and h % 4 >= 2 and kt >= 2:
                                        if (h, kt) == (6, 2):
                                            eng.wait_ge(s["v_ready"], c + 1)
                                            if not first:
                                                eng.wait_ge(s["lg_copied"], c + 2)
                                        pair = 2 * (h // 4 - 1) + h % 2
                                        outputs(c, pair, 2 * (kt - 2))
                                        outputs(c, pair, 2 * (kt - 2) + 1)
                                    if not first:
                                        if (h, kt) == (0, 2):
                                            last_outputs(c)
                                        if (h, kt) == (1, 2):
                                            turn_out_tensor(eng, c, 0)
                                            turn_out_tensor(eng, c, 1)
                                        if (h, kt) == (1, 3):
                                            turn_out_tensor(eng, c, 2)
                                        if (h, kt) == (2, 2):
                                            turn_out_tensor(eng, c, 3)
                                            turn_back_tensor(eng, c)
                                        if (h, kt) == (3, 0):
                                            project_out_tensor(eng, c)
                                        if (h, kt) == (3, 2):
                                            norm_turn_tensor(eng, s, c, OUT)
                                        if (h, kt) == (4, 0):
                                            norm_logits_tensor(eng, s, c, nxt)
                            eng.wait_ge(s["u_ready"], (c + 1) * NM)
                            rows_tensor(eng, c + 1, lambda: [outputs(c, H // 2 - 2, kt) for kt in range(TPC)])

                        rows_tensor(eng, 0, lambda: None)
                        main(0, True)
                        with eng.Fori(1, B) as c:
                            main(c, False)
                        last_outputs(B)
                        for t in range(TPC):
                            turn_out_tensor(eng, B, t)
                        turn_back_tensor(eng, B)
                        project_out_tensor(eng, B)
                        norm_turn_tensor(eng, s, B, OUT)
                        norm_logits_tensor(eng, s, B, nxt)
                        barrier(eng, b0)

                run(name, body)

        phases = [("F0a", lambda: ffn_phase("F0a", 0, None)), ("A0", lambda: attn0()),
                  ("F0b", lambda: ffn_phase("F0b", 0, 1)), ("F1a", lambda: ffn_phase("F1a", 1, None)),
                  ("A1", lambda: attn1()), ("F1b", lambda: ffn_phase("F1b", 1, "end"))]
        for n, (name, f) in enumerate(phases):
            if n >= stop_after:
                break
            f()
            if name == "F0b":
                r0.close()
                up1_hi = sb("up1_hi", [P, U1, HID1], F32R)
                up1_lo = sb("up1_lo", [P, U1, HID1], F32R)
        if stop_after < 3:
            r0.close()

        with nc.Block() as block:
            @block.sync
            def _(eng):
                eng.wait_ge(bar, ENGINES * state["bar"])
                eng.dma_start(out, X[:, :, :]).then_inc(stored, 16)
                eng.wait_ge(stored, 16)


def kernel(stop_after=99, **inputs):
    import numpy as np
    import concourse.bacc as bacc
    from concourse.bass_utils import run_bass_kernel_spmd

    a = {k: np.asarray(v) for k, v in inputs.items()}
    E_, HID_ = 8, 256

    def up_pair(w1, w3):
        w = np.stack([w1, w3], 1).reshape(w1.shape[0], 2, 2, 128, 128)
        return w.transpose(4, 0, 2, 1, 3).reshape(128, -1)

    w1 = np.concatenate([a["L0_ffn_sw1"], a["L0_ffn_w1"]], 0)
    w3 = np.concatenate([a["L0_ffn_sw3"], a["L0_ffn_w3"]], 0)
    w2 = np.concatenate([a["L0_ffn_sw2"], a["L0_ffn_w2"]], 0)
    arrays = {
        "x": a["L0_attn_x"].reshape(32, 128, 128).transpose(1, 0, 2),
        "alpha": a["L0_attn_alpha"].reshape(1, 1),
        "w_qkv0": np.concatenate([a["L0_attn_Wq"], a["L0_attn_Wk"], a["L0_attn_Wv"]], 1),
        "bias_rows0": np.stack([a["L0_attn_bq"], a["L0_attn_bk"], a["L0_attn_bv"], a["L0_attn_bfc"]], 0),
        "wo0": a["L0_attn_W_o"],
        "wo0_t": a["L0_attn_W_o"].transpose(0, 2, 1),
        "wfc0": a["L0_attn_Wfc"],
        "router0": a["L0_ffn_router_w"].T,
        "expert_bias": a["L0_ffn_expert_bias"].reshape(1, 8),
        "up0": up_pair(w1, w3),
        "down0": w2.reshape(10, 128, 2, 128).transpose(3, 0, 2, 1),
        "w_qkv1": np.concatenate([a["L1_attn_Wq"].T, a["L1_attn_Wk"].T, a["L1_attn_Wv"].T], 1),
        "wo1": a["L1_attn_Wo"].T,
        "router1": a["L1_ffn_w_g"].T,
        "up1": a["L1_ffn_c_fc"].transpose(1, 0, 2).reshape(128, -1),
        "down1": a["L1_ffn_c_proj"].reshape(8, 4, 128, 128).transpose(2, 0, 1, 3),
    }
    nc = bacc.Bacc("TRN2", target_bir_lowering=False, num_devices=1)
    feed, args = {}, []
    for name, v in arrays.items():
        v = np.ascontiguousarray(v)
        feed[f"in_{name}"] = v
        args.append(nc.dram_tensor(f"in_{name}", v.shape, mybir.dt.from_np(v.dtype), kind="ExternalInput").ap())
    out = nc.dram_tensor("out_x", (128, 32, 128), mybir.dt.float32, kind="ExternalOutput").ap()
    macaron(nc, *args, out, stop_after=stop_after)
    r = run_bass_kernel_spmd(nc, [feed], core_ids=[0])
    return r.results[0]["out_x"].transpose(1, 0, 2).reshape(8, 512, 128)
```
